# Optimizing a Trainium2 kernel written in Bass

```python
import numpy as np
import jax
import jax.numpy as jnp

def _softmax(x, axis=-1):
    return jax.nn.softmax(x, axis=axis)

def _gelu(x):
    return jax.nn.gelu(x, approximate=True)

def _silu(x):
    return jax.nn.silu(x)

def _sigmoid(x):
    return jax.nn.sigmoid(x)

def _layernorm(x, axis=-1, eps=1e-05):
    m = jnp.mean(x, axis=axis, keepdims=True)
    v = jnp.var(x, axis=axis, keepdims=True)
    return (x - m) / jnp.sqrt(v + eps)

def _scatter_add(tgt, idx, src, axis=0):
    return tgt.at[idx].add(src)

def _segment_sum(src, seg, n):
    return jax.ops.segment_sum(src, seg, n)
kernel_name = 'mk_xattn_ffn_d2_seqx_r8_3e7f0e'

def setup_inputs(seed: int=0):
    np.random.seed(seed)
    _w = jnp.asarray

    def _rec_inputs():
        import jax
        import jax.numpy as jnp
        _rk = jax.random.key(seed)
        x = 0.0003765 + 1 * jax.random.normal(jax.random.fold_in(_rk, 1), (16, 128, 256), jnp.float32)
        _lenS = 128 - jax.random.randint(jax.random.fold_in(_rk, 7), (16,), 0, max(1, 128 // 4) + 1, jnp.int32)
        _lenS2 = 128 - jax.random.randint(jax.random.fold_in(_rk, 8), (16,), 0, max(1, 128 // 4) + 1, jnp.int32)
        _ctx_2048P = jax.random.normal(jax.random.fold_in(_rk, 11), (16, 16, 256), jnp.float32)
        _ctx_2048c = jax.random.dirichlet(jax.random.fold_in(_rk, 511), 0.3 * jnp.ones((16,), jnp.float32), (16, 128))
        _ctx_2048t = jnp.einsum('bsk,bkd->bsd', _ctx_2048c, _ctx_2048P)
        _ctx_2048t = _ctx_2048t * jax.lax.rsqrt(jnp.mean(jnp.square(_ctx_2048t)) + 1e-12) * 0.953939
        ctx_2048 = -0.000292821 + 1.00034 * (_ctx_2048t + 0.3 * jax.random.normal(jax.random.fold_in(_rk, 611), (16, 128, 256), jnp.float32))
        return (x, ctx_2048)
    x, ctx_2048 = _rec_inputs()

    def _L0_xattn_setup():
        import jax, jax.numpy as jnp
        import numpy as np
        key = jax.random.key(seed)
        k1, k2, k3, k4, k5 = jax.random.split(key, 5)
        B, D_MODEL, L = (2, 128, 256)
        HEAD_DIM = 8
        H = D_MODEL // HEAD_DIM
        return {'k': jax.random.normal(k1, (B, D_MODEL, L), dtype=jnp.float32), 'v': jax.random.normal(k2, (B, D_MODEL, L), dtype=jnp.float32), 'q': jax.random.normal(k3, (B, D_MODEL, L), dtype=jnp.float32), 'ssm_kernel': jax.random.normal(k4, (H, L), dtype=jnp.float32), 'D': jax.random.normal(k5, (H,), dtype=jnp.float32), 'head_dim': HEAD_DIM}
    _L0_xattn_all = _L0_xattn_setup()
    _L0_xattn_in = {k: v for k, v in _L0_xattn_all.items() if k in ('ssm_kernel', 'D')}
    del _L0_xattn_all

    def _L0_ffn_setup():
        import jax, jax.numpy as jnp
        import numpy as np
        N_EXPERTS = 16
        TOP_K = 4
        N_GROUP = 4
        TOPK_GROUP = 2
        NORM_TOPK = True
        ROUTED_SCALE = 2.5
        H = 256
        F_MOE = 128
        F_SHARED = 256
        B, S = (2, 256)

        def _route(hidden, gate_weight, bias):
            T = hidden.shape[0]
            epg = N_EXPERTS // N_GROUP
            logits = hidden @ gate_weight.T
            scores = jax.nn.sigmoid(logits)
            scores_for_choice = scores + bias[None, :]
            grp = scores_for_choice.reshape(T, N_GROUP, epg)
            group_scores = jax.lax.top_k(grp, 2)[0].sum(-1)
            group_idx = jax.lax.top_k(group_scores, TOPK_GROUP)[1]
            group_mask = jax.nn.one_hot(group_idx, N_GROUP, dtype=jnp.bool_).any(1)
            score_mask = jnp.repeat(group_mask, epg, axis=-1)
            masked = jnp.where(score_mask, scores_for_choice, -jnp.inf)
            topk_idx = jax.lax.top_k(masked, TOP_K)[1]
            topk_weight = jnp.take_along_axis(scores, topk_idx, axis=1)
            return (topk_weight, topk_idx)

        def _swiglu(x, gw, uw, dw):
            return jax.nn.silu(x @ gw.T) * (x @ uw.T) @ dw.T
        key = jax.random.key(seed)
        ks = jax.random.split(key, 9)
        std = 0.02
        return {'hidden_states': jax.random.normal(ks[0], (B, S, H), jnp.float32), 'gate_weight': jax.random.normal(ks[1], (N_EXPERTS, H), jnp.float32) * std, 'e_score_correction_bias': jnp.zeros((N_EXPERTS,), jnp.float32), 'gate_w': jax.random.normal(ks[2], (N_EXPERTS, F_MOE, H), jnp.float32) * std, 'up_w': jax.random.normal(ks[3], (N_EXPERTS, F_MOE, H), jnp.float32) * std, 'down_w': jax.random.normal(ks[4], (N_EXPERTS, H, F_MOE), jnp.float32) * std, 'sh_gate_w': jax.random.normal(ks[5], (F_SHARED, H), jnp.float32) * std, 'sh_up_w': jax.random.normal(ks[6], (F_SHARED, H), jnp.float32) * std, 'sh_down_w': jax.random.normal(ks[7], (H, F_SHARED), jnp.float32) * std}
    _L0_ffn_all = _L0_ffn_setup()
    _L0_ffn_in = {k: v for k, v in _L0_ffn_all.items() if k in ('gate_weight', 'e_score_correction_bias', 'gate_w', 'up_w', 'down_w', 'sh_gate_w', 'sh_up_w', 'sh_down_w')}
    del _L0_ffn_all

    def _L1_xattn_setup():
        import jax, jax.numpy as jnp
        import numpy as np
        BS, S, DK = (8, 64, 256)
        key = jax.random.key(seed)
        kq, kk, kv = jax.random.split(key, 3)
        q = jax.random.normal(kq, (BS, S, DK), dtype=jnp.float32)
        k = jax.random.normal(kk, (BS, S, DK), dtype=jnp.float32)
        v = jax.random.normal(kv, (BS, S, DK), dtype=jnp.float32)
        return {'q': q, 'k': k, 'v': v}
    _L1_xattn_all = _L1_xattn_setup()
    _L1_xattn_in = {k: v for k, v in _L1_xattn_all.items() if k in ()}
    del _L1_xattn_all

    def _L1_ffn_setup():
        import jax, jax.numpy as jnp
        import numpy as np
        B, S, H, F, E, R, K = (2, 128, 256, 896, 8, 32, 2)

        def _gather_slot(a_all, e):
            return jnp.take_along_axis(a_all, e[:, None, None], axis=1)[:, 0]
        key = jax.random.key(seed)
        ks = jax.random.split(key, 12)
        sc = 0.02
        n = lambda k, shape, s: jax.random.normal(k, shape, dtype=jnp.float32) * s
        return {'hidden_states': n(ks[0], (B, S, H), 1.0), 'Wg': n(ks[1], (E, H), sc), 'W1': n(ks[2], (F, H), sc), 'W2': n(ks[3], (H, F), sc), 'W3': n(ks[4], (F, H), sc), 'A1': n(ks[5], (E, R, H), sc), 'B1': n(ks[6], (E, F, R), sc), 'A2': n(ks[7], (E, R, F), sc), 'B2': n(ks[8], (E, H, R), sc), 'A3': n(ks[9], (E, R, H), sc), 'B3': n(ks[10], (E, F, R), sc)}
    _L1_ffn_all = _L1_ffn_setup()
    _L1_ffn_in = {k: v for k, v in _L1_ffn_all.items() if k in ('Wg', 'W1', 'W2', 'W3', 'A1', 'B1', 'A2', 'B2', 'A3', 'B3')}
    del _L1_ffn_all
    return {'x': x, 'ctx_2048': ctx_2048, 'L0_xattn_ssm_kernel': _L0_xattn_in['ssm_kernel'], 'L0_xattn_D': _L0_xattn_in['D'], 'L0_ffn_gate_weight': _L0_ffn_in['gate_weight'], 'L0_ffn_e_score_correction_bias': _L0_ffn_in['e_score_correction_bias'], 'L0_ffn_gate_w': _L0_ffn_in['gate_w'], 'L0_ffn_up_w': _L0_ffn_in['up_w'], 'L0_ffn_down_w': _L0_ffn_in['down_w'], 'L0_ffn_sh_gate_w': _L0_ffn_in['sh_gate_w'], 'L0_ffn_sh_up_w': _L0_ffn_in['sh_up_w'], 'L0_ffn_sh_down_w': _L0_ffn_in['sh_down_w'], 'L1_ffn_Wg': _L1_ffn_in['Wg'], 'L1_ffn_W1': _L1_ffn_in['W1'], 'L1_ffn_W2': _L1_ffn_in['W2'], 'L1_ffn_W3': _L1_ffn_in['W3'], 'L1_ffn_A1': _L1_ffn_in['A1'], 'L1_ffn_B1': _L1_ffn_in['B1'], 'L1_ffn_A2': _L1_ffn_in['A2'], 'L1_ffn_B2': _L1_ffn_in['B2'], 'L1_ffn_A3': _L1_ffn_in['A3'], 'L1_ffn_B3': _L1_ffn_in['B3']}

def reference(x, ctx_2048, L0_xattn_ssm_kernel, L0_xattn_D, L0_ffn_gate_weight, L0_ffn_e_score_correction_bias, L0_ffn_gate_w, L0_ffn_up_w, L0_ffn_down_w, L0_ffn_sh_gate_w, L0_ffn_sh_up_w, L0_ffn_sh_down_w, L1_ffn_Wg, L1_ffn_W1, L1_ffn_W2, L1_ffn_W3, L1_ffn_A1, L1_ffn_B1, L1_ffn_A2, L1_ffn_B2, L1_ffn_A3, L1_ffn_B3):
    import jax
    import jax.numpy as jnp

    def _L0_xattn_ref(k, v, q, ssm_kernel, D, head_dim):
        import jax, jax.numpy as jnp
        import numpy as np
        B, HD, L = k.shape
        H = HD // head_dim
        fft_size = 2 * L
        k_ = k.reshape(B, H, head_dim, L)
        v_ = v.reshape(B, H, head_dim, L)
        q_ = q.reshape(B, H, head_dim, L)
        kv = jnp.einsum('bhil,bhjl->bijhl', k_, v_)
        kv_f = jnp.fft.rfft(kv, n=fft_size)
        kernel_f = jnp.fft.rfft(ssm_kernel, n=fft_size)
        y = jnp.fft.irfft(kv_f * kernel_f, n=fft_size)[..., :L]
        out = y + kv * D[None, None, None, :, None]
        out = jnp.einsum('bijhl,bhil->bjhl', out, q_)
        out = jnp.transpose(out, (0, 2, 1, 3)).reshape(B, H * head_dim, L)
        return out.astype(k.dtype)

    def _L0_ffn_ref(hidden_states, gate_weight, e_score_correction_bias, gate_w, up_w, down_w, sh_gate_w, sh_up_w, sh_down_w):
        import jax, jax.numpy as jnp
        import numpy as np
        N_EXPERTS = 16
        TOP_K = 4
        N_GROUP = 4
        TOPK_GROUP = 2
        NORM_TOPK = True
        ROUTED_SCALE = 2.5
        H = 256
        F_MOE = 128
        F_SHARED = 256
        B, S = (2, 256)

        def _route(hidden, gate_weight, bias):
            T = hidden.shape[0]
            epg = N_EXPERTS // N_GROUP
            logits = hidden @ gate_weight.T
            scores = jax.nn.sigmoid(logits)
            scores_for_choice = scores + bias[None, :]
            grp = scores_for_choice.reshape(T, N_GROUP, epg)
            group_scores = jax.lax.top_k(grp, 2)[0].sum(-1)
            group_idx = jax.lax.top_k(group_scores, TOPK_GROUP)[1]
            group_mask = jax.nn.one_hot(group_idx, N_GROUP, dtype=jnp.bool_).any(1)
            score_mask = jnp.repeat(group_mask, epg, axis=-1)
            masked = jnp.where(score_mask, scores_for_choice, -jnp.inf)
            topk_idx = jax.lax.top_k(masked, TOP_K)[1]
            topk_weight = jnp.take_along_axis(scores, topk_idx, axis=1)
            return (topk_weight, topk_idx)

        def _swiglu(x, gw, uw, dw):
            return jax.nn.silu(x @ gw.T) * (x @ uw.T) @ dw.T
        Bh, Sh, Hh = hidden_states.shape
        hidden = hidden_states.reshape(-1, Hh)
        topk_weight, topk_idx = _route(hidden, gate_weight, e_score_correction_bias)
        if NORM_TOPK:
            topk_weight = topk_weight / (topk_weight.sum(-1, keepdims=True) + 1e-20)
        topk_weight = topk_weight * ROUTED_SCALE
        one_hot = jax.nn.one_hot(topk_idx, N_EXPERTS, dtype=topk_weight.dtype)
        weight_matrix = (one_hot * topk_weight[..., None]).sum(1)
        g = jnp.einsum('th,nfh->ntf', hidden, gate_w)
        u = jnp.einsum('th,nfh->ntf', hidden, up_w)
        act = jax.nn.silu(g) * u
        routed = jnp.einsum('ntf,nhf,tn->th', act, down_w, weight_matrix)
        out = routed + _swiglu(hidden, sh_gate_w, sh_up_w, sh_down_w)
        return out.reshape(Bh, Sh, Hh)

    def _L1_xattn_ref(q, k, v):
        import jax, jax.numpy as jnp
        import numpy as np
        BS, S, DK = (8, 64, 256)
        dk = q.shape[-1]
        scale = 1.0 / jnp.sqrt(jnp.asarray(dk, dtype=q.dtype))
        scaled = jnp.einsum('bsd,bse->bde', q, k) * scale
        attn = jax.nn.softmax(scaled, axis=1)
        out = jnp.einsum('bde,bse->bsd', attn, v)
        return out

    def _L1_ffn_ref(hidden_states, Wg, W1, W2, W3, A1, B1, A2, B2, A3, B3):
        import jax, jax.numpy as jnp
        import numpy as np
        B, S, H, F, E, R, K = (2, 128, 256, 896, 8, 32, 2)

        def _gather_slot(a_all, e):
            return jnp.take_along_axis(a_all, e[:, None, None], axis=1)[:, 0]
        b, s, h = hidden_states.shape
        x = hidden_states.reshape(-1, h)
        nE = Wg.shape[0]
        logits = x @ Wg.T
        probs = jax.nn.softmax(logits.astype(jnp.float32), axis=-1)
        rw, sel = jax.lax.top_k(probs, K)
        rw = (rw / rw.sum(axis=-1, keepdims=True)).astype(x.dtype)
        base1 = x @ W1.T
        base3 = x @ W3.T
        a1_all = jnp.einsum('th,erh->ter', x, A1)
        a3_all = jnp.einsum('th,erh->ter', x, A3)
        out = jnp.zeros_like(x)
        for k in range(K):
            e = sel[:, k]
            mask = jax.nn.one_hot(e, nE, dtype=x.dtype)
            a1 = _gather_slot(a1_all, e)
            a3 = _gather_slot(a3_all, e)
            lora1 = jnp.einsum('ter,efr->tf', mask[:, :, None] * a1[:, None, :], B1)
            lora3 = jnp.einsum('ter,efr->tf', mask[:, :, None] * a3[:, None, :], B3)
            x1 = base1 + lora1
            x3 = base3 + lora3
            x2 = jax.nn.silu(x1) * x3
            down = x2 @ W2.T
            a2_all = jnp.einsum('tf,erf->ter', x2, A2)
            a2 = _gather_slot(a2_all, e)
            lora2 = jnp.einsum('ter,ehr->th', mask[:, :, None] * a2[:, None, :], B2)
            out = out + (down + lora2) * rw[:, k:k + 1]
        return out.reshape(b, s, h)
    x = x + _L0_xattn_ref(ctx_2048, ctx_2048, _layernorm(x, axis=-1), L0_xattn_ssm_kernel, L0_xattn_D, 8)
    x = x + _L0_ffn_ref(_layernorm(x, axis=-1), L0_ffn_gate_weight, L0_ffn_e_score_correction_bias, L0_ffn_gate_w, L0_ffn_up_w, L0_ffn_down_w, L0_ffn_sh_gate_w, L0_ffn_sh_up_w, L0_ffn_sh_down_w)
    x = x + _L1_xattn_ref(_layernorm(x, axis=-1), ctx_2048, ctx_2048)
    x = x + _L1_ffn_ref(_layernorm(x, axis=-1), L1_ffn_Wg, L1_ffn_W1, L1_ffn_W2, L1_ffn_W3, L1_ffn_A1, L1_ffn_B1, L1_ffn_A2, L1_ffn_B2, L1_ffn_A3, L1_ffn_B3)
    return x

_drawn_inputs = setup_inputs


def setup_inputs(seed=0):
    import zlib

    import numpy as np

    out = dict(_drawn_inputs(seed))
    spreads = {'L0_ffn_e_score_correction_bias': (0.0, 0.8)}
    factors = {'L0_ffn_gate_weight': 8.0,
     'L0_ffn_gate_w': 8.0,
     'L0_ffn_up_w': 8.0,
     'L0_ffn_down_w': 8.0,
     'L0_ffn_sh_gate_w': 8.0,
     'L0_ffn_sh_up_w': 8.0,
     'L0_ffn_sh_down_w': 8.0,
     'L1_ffn_Wg': 8.0,
     'L1_ffn_W1': 8.0,
     'L1_ffn_W2': 8.0,
     'L1_ffn_W3': 8.0,
     'L1_ffn_A1': 8.0,
     'L1_ffn_B1': 8.0,
     'L1_ffn_A2': 8.0,
     'L1_ffn_B2': 8.0,
     'L1_ffn_A3': 8.0,
     'L1_ffn_B3': 8.0}
    for name, (base, spread) in spreads.items():
        noise = np.random.default_rng([zlib.crc32(name.encode()), seed]).standard_normal(out[name].shape)
        drawn = base * np.exp(spread * noise) if base else spread * noise
        out[name] = jnp.asarray(drawn.astype(out[name].dtype))
    for name, factor in factors.items():
        out[name] = (out[name] * factor).astype(out[name].dtype)
    return out
```

```python
import concourse.bass as bass
from concourse import mybir
from contextlib import ExitStack

UPTO = 4

FP32 = mybir.dt.float32
F32R = mybir.dt.float32r
BF16 = mybir.dt.bfloat16
ALU = mybir.AluOpType
ACT = mybir.ActivationFunctionType
AX = mybir.AxisListType

P = 128
BATCH = 16
SEQ = 128
DIM = 256
TOKENS = BATCH * SEQ
TILES = TOKENS // P
HALVES = DIM // P
EPS = 1e-5

HEADS = 16
HEAD_DIM = 8
CHUNK_B = 8
CHUNKS = BATCH // CHUNK_B
PAIRS = CHUNK_B * HEAD_DIM * HEAD_DIM
KPAD = 3 * P

EXPERTS = 16
GROUPS = 4
TOP_GROUPS = 2
TOP_EXPERTS = 4
ROUTED_SCALE = 2.5
SHARED_BLOCKS = 2
FBLOCKS = EXPERTS + SHARED_BLOCKS
MOE_COLS = 3 * DIM
GROUP_T = 512
TOKEN_GROUPS = TOKENS // GROUP_T
W_SLOTS = 4
LAG = 2
BIG = 1e30
STAGES = 4
SOFTMAX_SCALE = DIM ** -0.5
LORA_EXPERTS = 8
RANK = 32
PICKS = 2
LORA_BLOCKS = 7
LORA_CHUNKS = LORA_BLOCKS + 1
LORA_COLS = 6 * DIM
LORA_STAGES = 2
LORA_STEPS = 4 + PICKS * 7 + 3
STEPS = 5 + TOP_GROUPS * 7 + 3 + TOP_EXPERTS * 6 + 7


def build(nc, a, out):
    x_rows = a["x"].rearrange("(t p) d -> p t d", p=P)
    out_rows = out.rearrange("(t p) d -> p t d", p=P)
    kpad_dram = nc.dram_tensor("kpad_scratch", [HEADS, KPAD], FP32).ap()
    w_dram = nc.dram_tensor("w_scratch", [EXPERTS, TOKENS], FP32).ap()
    mask_dram = nc.dram_tensor("mask_scratch", [PICKS * LORA_EXPERTS, TOKENS], BF16).ap()
    rw_dram = nc.dram_tensor("rw_scratch", [PICKS, TOKENS], FP32).ap()
    x_dram_rows = nc.dram_tensor("x_scratch", [TOKENS, DIM], FP32).ap().rearrange("(t p) d -> p t d", p=P)

    with ExitStack() as whole:
        def keep(name, shape, dt=FP32):
            return whole.enter_context(nc.sbuf_tensor(name, shape, dt))

        ident = keep("ident", [P, P])
        norm = (keep("stats", [P, TILES, 6]), keep("meanvar", [P, TILES, 2]), keep("rstd", [P, TILES]),
                keep("minus_half", [P, TILES]))
        banks = [whole.enter_context(nc.psum_tensor(f"bank{i}", [P, 512], FP32)) for i in range(8)]

        def split_weights(stack, name, shape):
            return (stack.enter_context(nc.sbuf_tensor(name + "_hi", shape, F32R)),
                    stack.enter_context(nc.sbuf_tensor(name + "_lo", shape, F32R)))

        with ExitStack() as residual:
            x_sb = residual.enter_context(nc.sbuf_tensor("x_sb", [P, TILES, DIM], FP32))
            with ExitStack() as weights:
                w = split_weights(weights, "moe_w", [P, FBLOCKS, MOE_COLS])
                with ExitStack() as memory:
                    conv_phase(nc, memory, a, x_rows, kpad_dram, ident, x_sb, norm, *w, banks)
                if UPTO > 1:
                    with ExitStack() as memory:
                        moe_phase(nc, memory, a, w_dram, ident, x_sb, norm, *w, banks)
            if UPTO > 2:
                w_shape = [P, LORA_CHUNKS, LORA_COLS]
                x_shape = [P, HALVES, TOKENS]
                lora = whole.enter_context(ExitStack())
                with ExitStack() as memory:
                    w = [lora.enter_context(nc.sbuf_tensor(n, w_shape, F32R, side="right")) for n in (
                        "lora_w_hi", "lora_w_lo")]
                    softmax_phase(nc, memory, a, x_sb, norm, *w, banks)
                if UPTO > 3:
                    x_parts = [lora.enter_context(nc.sbuf_tensor(n, x_shape, F32R, side="right")) for n in (
                        "lora_x_hi", "lora_x_lo")]
                    with ExitStack() as memory:
                        def sm(name, shape):
                            return memory.enter_context(nc.sbuf_tensor(name, shape, FP32))

                        norm_block(nc, x_sb, *x_parts, sm("lora_gate", [P, HALVES, LORA_EXPERTS]), LORA_EXPERTS,
                                   a["lora_gate"], ident, norm, sm("lora_y", [P, 4, DIM]),
                                   sm("lora_x_t", [P, 2, HALVES, 2 * P]), banks)
                        lora_router(nc, memory, ident, mask_dram, rw_dram, x_dram_rows, x_sb, banks)
            if UPTO < 4:
                with ExitStack() as s:
                    stored = s.enter_context(nc.semaphore("stored"))
                    block = s.enter_context(nc.Block())

                    @block.sync
                    def _(sp):
                        sp.dma_start(out_rows, x_sb[:, :, :]).then_inc(stored, 16)
                        sp.wait_ge(stored, 16)

        if UPTO > 3:
            with ExitStack() as memory:
                lora_experts(nc, memory, out_rows, mask_dram, rw_dram, x_dram_rows, *x_parts, *w, banks)


def conv_phase(nc, memory, a, x_rows, kpad_dram, ident, x_sb, norm, w_hi, w_lo, banks):
    stats, meanvar, rstd, minus_half = norm

    def sb(name, shape, dt=FP32):
        return memory.enter_context(nc.sbuf_tensor(name, shape, dt))

    ctx_t = sb("ctx_t", [P, HALVES, TOKENS])
    toeplitz = sb("toeplitz", [P, HEADS, 2 * P])
    q_t = sb("q_t", [P, HALVES, TOKENS])
    y = sb("y", [P, 4, DIM])
    kv = sb("kv", [P, 2, HALVES, PAIRS])
    prod = sb("prod", [P, 2, PAIRS])
    kpad = sb("kpad", [HEADS, KPAD])
    d_col = sb("d_col", [HEADS, 1])
    stage = sb("stage", [P, STAGES, MOE_COLS])

    with ExitStack() as s:
        def sem(name):
            return s.enter_context(nc.semaphore(name))

        kpad_zero, k_loaded, d_added, kpad_stored, toeplitz_loaded = map(
            sem, ("kpad_zero", "k_loaded", "d_added", "kpad_stored", "toeplitz_loaded"))
        x_loaded = [sem(f"x_loaded{i}") for i in range(4)]
        ctx_loaded, consts, ident_zero = map(sem, ("ctx_loaded", "consts", "ident_zero"))
        stats_done, mv_done, rstd_half, rstd_done = map(sem, ("stats_done", "mv_done", "rstd_half", "rstd_done"))
        y_ready, q_transposed, q_copied = map(sem, ("y_ready", "q_transposed", "q_copied"))
        block = s.enter_context(nc.Block())

        @block.sync
        def _(sp):
            for i in range(4):
                sp.dma_start(x_sb[:, 4 * i:4 * i + 4, :], x_rows[:, 4 * i:4 * i + 4, :]).then_inc(x_loaded[i], 16)
            for h in range(HALVES):
                sp.dma_start(ctx_t[:, h, :], a["ctx_t"][h]).then_inc(ctx_loaded, 16)
            sp.wait_ge(ctx_loaded, 32)

        @block.gpsimd
        def _(pool):
            nc.gpsimd.memset(kpad[:, :], 0.0).then_inc(kpad_zero, 1)
            nc.gpsimd.memset(ident[:, :], 0.0).then_inc(ident_zero, 1)
            nc.gpsimd.memset(minus_half[:, :], -0.5)
            pool.wait_ge(ident_zero, 1)
            nc.gpsimd.affine_select(out=ident[:, :], in_=ident[:, :], compare_op=ALU.not_equal, fill=1.0,
                                    base=0, pattern=[[-1, P]], channel_multiplier=1).then_inc(consts, 1)
            pool.wait_ge(mv_done, 1)
            nc.gpsimd.tensor_scalar_add(rstd[:, :], meanvar[:, :, 1], EPS).then_inc(rstd_half, 1)
            pool.wait_ge(rstd_half, 1)
            nc.gpsimd.tensor_tensor(rstd[:, :], rstd[:, :], minus_half[:, :], ALU.pow).then_inc(rstd_done, 1)

        @block.scalar
        def _(act):
            act.wait_ge(kpad_zero, 1)
            act.dma_start(kpad[:, P - 1:P - 1 + DIM], a["ssm_kernel"]).then_inc(k_loaded, 16)
            act.dma_start(d_col[:, :], a["D"]).then_inc(k_loaded, 16)
            act.wait_ge(d_added, 1)
            act.dma_start(kpad_dram, kpad[:, :]).then_inc(kpad_stored, 16)
            act.wait_ge(kpad_stored, 16)
            act.dma_start(toeplitz[:, :, :],
                          bass.AP(kpad_dram.tensor, 0, [[1, P], [KPAD, HEADS], [1, 2 * P]])).then_inc(toeplitz_loaded, 16)
            for n in range(TILES // 2):
                act.wait_ge(q_transposed, n + 1)
                nc.scalar.copy(q_t[:, :, n * 2 * P:(n + 1) * 2 * P],
                               banks[n % 4][:, :].rearrange("p (c t) -> p c t", c=HALVES)).then_inc(q_copied, 1)
            act.wait_ge(toeplitz_loaded, 16)

        @block.vector
        def _(dve):
            dve.wait_ge(k_loaded, 32)
            nc.vector.tensor_tensor(kpad[:, P - 1:P], kpad[:, P - 1:P], d_col[:, :], ALU.add).then_inc(d_added, 1)
            for t in range(TILES):
                if t % 4 == 0:
                    dve.wait_ge(x_loaded[t // 4], 16)
                nc.vector.bn_stats(stats[:, t, :], x_sb[:, t, :]).then_inc(stats_done, 1)
            for t in range(TILES):
                dve.wait_ge(stats_done, t + 1)
                last = nc.vector.bn_aggr(meanvar[:, t, :], stats[:, t, :])
            last.then_inc(mv_done, 1)
            dve.wait_ge(rstd_done, 1)
            for t in range(TILES):
                if t >= 4 and t % 2 == 0:
                    dve.wait_ge(q_transposed, t // 2 - 1)
                last = nc.vector.tensor_scalar(y[:, t % 4, :], x_sb[:, t, :], meanvar[:, t, 0:1], rstd[:, t:t + 1],
                                               ALU.subtract, ALU.mult)
                if t % 2:
                    last.then_inc(y_ready, 1)

        @block.tensor
        def _(pe):
            pe.wait_ge(consts, 1)
            for n in range(TILES // 2):
                pe.wait_ge(y_ready, n + 1)
                if n >= 4:
                    pe.wait_ge(q_copied, n - 3)
                for c in range(HALVES):
                    for k in range(2):
                        last = nc.tensor.transpose(banks[n % 4][:, (2 * c + k) * P:(2 * c + k + 1) * P],
                                                   y[:, (2 * n + k) % 4, c * P:(c + 1) * P], ident[:, :])
                last.then_inc(q_transposed, 1)

    with ExitStack() as s:
        def sem(name):
            return s.enter_context(nc.semaphore(name))

        kv_ready, conv_done, prod_ready, reduced = map(sem, ("kv_ready", "conv_done", "prod_ready", "reduced"))
        staged = [sem(f"staged{i}") for i in range(STAGES)]
        hi_split, lo_split_pool, lo_split_dve = map(sem, ("hi_split", "lo_split_pool", "lo_split_dve"))
        on_dve = [n % 5 == 4 for n in range(FBLOCKS)]
        lo_split = [(lo_split_dve, sum(on_dve[:n + 1])) if on_dve[n] else
                    (lo_split_pool, n + 1 - sum(on_dve[:n + 1])) for n in range(FBLOCKS)]

        def low_weights(engine, ops, n):
            engine.wait_ge(hi_split, n + 1)
            ops.tensor_tensor(w_lo[:, n, :], stage[:, n % STAGES, :], w_hi[:, n, :].bitcast(FP32),
                              ALU.subtract).then_inc(lo_split[n][0], 1)
        wide = [P, CHUNK_B, HEAD_DIM, HEAD_DIM]
        block = s.enter_context(nc.Block())

        @block.sync
        def _(sp):
            for n in range(FBLOCKS):
                if n >= STAGES:
                    sp.wait_ge(*lo_split[n - STAGES])
                sp.dma_start(stage[:, n % STAGES, :], a["moe_weights"][n]).then_inc(staged[n % STAGES], 16)

        @block.scalar
        def _(act):
            for n in range(FBLOCKS):
                act.wait_ge(staged[n % STAGES], 16 * (n // STAGES + 1))
                nc.scalar.copy(w_hi[:, n, :], stage[:, n % STAGES, :]).then_inc(hi_split, 1)

        @block.gpsimd
        def _(pool):
            pool.sem_inc(conv_done, CHUNKS)
            for h in range(HEADS):
                for n in range(h * FBLOCKS // HEADS, (h + 1) * FBLOCKS // HEADS):
                    if not on_dve[n]:
                        low_weights(pool, nc.gpsimd, n)
                for c in range(CHUNKS):
                    pool.wait_ge(conv_done, CHUNKS * h + c + 1)
                    for m in range(HALVES):
                        feat = ctx_t[:, m, :].rearrange("p (b t) -> p b t", t=SEQ)[
                            :, c * CHUNK_B:(c + 1) * CHUNK_B, bass.ds(h * HEAD_DIM, HEAD_DIM)]
                        last = nc.gpsimd.tensor_tensor(
                            kv[:, c, m, :].rearrange("p (b j i) -> p b j i", j=HEAD_DIM, i=HEAD_DIM),
                            feat.unsqueeze(2).broadcast_to(wide), feat.unsqueeze(3).broadcast_to(wide), ALU.mult)
                    last.then_inc(kv_ready, 1)

        @block.tensor
        def _(pe):
            for h in range(HEADS):
                for c in range(CHUNKS):
                    n = CHUNKS * h + c
                    pe.wait_ge(kv_ready, n + 1)
                    if h >= 1:
                        pe.wait_ge(prod_ready, HALVES * (n - CHUNKS + 1))
                    same, across = toeplitz[:, h, 0:P], toeplitz[:, h, P:2 * P]
                    nc.tensor.matmul(banks[2 * c][:, :], same, kv[:, c, 0, :], start=True, stop=True)
                    nc.tensor.matmul(banks[2 * c + 1][:, :], across, kv[:, c, 0, :], start=True, stop=False)
                    nc.tensor.matmul(banks[2 * c + 1][:, :], same, kv[:, c, 1, :], start=False,
                                     stop=True).then_inc(conv_done, 1)

        @block.vector
        def _(dve):
            for n in range(HEADS * CHUNKS):
                h, c = n // CHUNKS, n % CHUNKS
                if c == 0:
                    for w in range(h * FBLOCKS // HEADS, (h + 1) * FBLOCKS // HEADS):
                        if on_dve[w]:
                            low_weights(dve, nc.vector, w)
                dve.wait_ge(conv_done, CHUNKS + n + 1)
                query = [q_t[:, m, :].rearrange("p (b t) -> p b t", t=SEQ)[
                    :, c * CHUNK_B:(c + 1) * CHUNK_B, h * HEAD_DIM:(h + 1) * HEAD_DIM] for m in range(HALVES)]
                for m in range(HALVES):
                    if n >= 1:
                        dve.wait_ge(reduced, HALVES * (n - 1) + m + 1)
                    nc.vector.tensor_tensor(
                        prod[:, m, :].rearrange("p (b j i) -> p b j i", j=HEAD_DIM, i=HEAD_DIM),
                        banks[2 * c + m][:, :].rearrange("p (b j i) -> p b j i", j=HEAD_DIM, i=HEAD_DIM),
                        query[m].unsqueeze(2).broadcast_to(wide), ALU.mult).then_inc(prod_ready, 1)
                for m in range(HALVES):
                    dve.wait_ge(prod_ready, HALVES * n + m + 1)
                    nc.vector.reduce_sum(query[m], prod[:, m, :].rearrange(
                        "p (b j i) -> p b j i", j=HEAD_DIM, i=HEAD_DIM), axis=AX.X).then_inc(reduced, 1)

    with ExitStack() as s:
        transposed = s.enter_context(nc.semaphore("att_transposed"))
        added = s.enter_context(nc.semaphore("att_added"))
        block = s.enter_context(nc.Block())

        @block.tensor
        def _(pe):
            for n in range(TILES // 2):
                if n >= 8:
                    pe.wait_ge(added, n - 7)
                for k in range(2):
                    for c in range(HALVES):
                        last = nc.tensor.transpose(banks[n % 8][:, (2 * k + c) * P:(2 * k + c + 1) * P],
                                                   q_t[:, c, (2 * n + k) * P:(2 * n + k + 1) * P], ident[:, :])
                last.then_inc(transposed, 1)

        @block.vector
        def _(dve):
            for n in range(TILES // 2):
                dve.wait_ge(transposed, n + 1)
                rows = x_sb[:, 2 * n:2 * n + 2, :]
                nc.vector.tensor_tensor(rows, rows, banks[n % 8][:, :].rearrange("p (t d) -> p t d", t=2),
                                        ALU.add).then_inc(added, 1)


def split_products(hi_lo_a, hi_lo_b):
    (a_hi, a_lo), (b_hi, b_lo) = hi_lo_a, hi_lo_b
    return ((a_hi, b_hi), (a_hi, b_lo), (a_lo, b_hi))


def norm_block(nc, x_sb, x_hi, x_lo, gate_sb, experts, gate_source, ident, norm, y, x_t, banks):
    stats, meanvar, rstd, minus_half = norm
    with ExitStack() as s:
        def sem(name):
            return s.enter_context(nc.semaphore(name))

        stats_done, mv_done, rstd_half, rstd_done, gate_loaded = map(
            sem, ("stats_done", "mv_done", "rstd_half", "rstd_done", "gate_loaded"))
        y_ready, transposed, xt_copied, hi_done, lo_done, logits_done = map(
            sem, ("y_ready", "transposed", "xt_copied", "hi_done", "lo_done", "logits_done"))
        block = s.enter_context(nc.Block())

        @block.sync
        def _(sp):
            sp.dma_start(gate_sb[:, :, :], gate_source).then_inc(gate_loaded, 16)
            sp.wait_ge(gate_loaded, 16)

        @block.vector
        def _(dve):
            for t in range(TILES):
                nc.vector.bn_stats(stats[:, t, :], x_sb[:, t, :]).then_inc(stats_done, 1)
            for t in range(TILES):
                dve.wait_ge(stats_done, t + 1)
                last = nc.vector.bn_aggr(meanvar[:, t, :], stats[:, t, :])
            last.then_inc(mv_done, 1)
            dve.wait_ge(rstd_done, 1)

            def normalize(n):
                if n >= 2:
                    dve.wait_ge(transposed, n - 1)
                for t in (2 * n, 2 * n + 1):
                    last = nc.vector.tensor_scalar(y[:, t % 4, :], x_sb[:, t, :], meanvar[:, t, 0:1],
                                                   rstd[:, t:t + 1], ALU.subtract, ALU.mult)
                last.then_inc(y_ready, 1)

            normalize(0)
            for n in range(TILES // 2):
                if n + 1 < TILES // 2:
                    normalize(n + 1)
                dve.wait_ge(xt_copied, n + 1)
                nc.vector.tensor_copy(x_hi[:, :, 2 * P * n:2 * P * (n + 1)], x_t[:, n % 2, :, :]).then_inc(hi_done, 1)

        @block.gpsimd
        def _(pool):
            pool.wait_ge(mv_done, 1)
            nc.gpsimd.tensor_scalar_add(rstd[:, :], meanvar[:, :, 1], EPS).then_inc(rstd_half, 1)
            pool.wait_ge(rstd_half, 1)
            nc.gpsimd.tensor_tensor(rstd[:, :], rstd[:, :], minus_half[:, :], ALU.pow).then_inc(rstd_done, 1)
            for n in range(TILES // 2):
                pool.wait_ge(hi_done, n + 1)
                cols = slice(2 * P * n, 2 * P * (n + 1))
                nc.gpsimd.tensor_tensor(x_lo[:, :, cols], x_t[:, n % 2, :, :], x_hi[:, :, cols].bitcast(FP32),
                                        ALU.subtract).then_inc(lo_done, 1)

        @block.scalar
        def _(act):
            for n in range(TILES // 2):
                act.wait_ge(transposed, n + 1)
                if n >= 2:
                    act.wait_ge(lo_done, n - 1)
                    act.wait_ge(logits_done, n - 1)
                nc.scalar.copy(x_t[:, n % 2, :, :],
                               banks[n % 2][:, :].rearrange("p (c t) -> p c t", c=HALVES)).then_inc(xt_copied, 1)

        @block.tensor
        def _(pe):
            def logits(n):
                pe.wait_ge(xt_copied, n + 1)
                for k in range(2):
                    t = 2 * n + k
                    for c in range(HALVES):
                        last = nc.tensor.matmul(banks[7][:, t * experts:(t + 1) * experts],
                                                x_t[:, n % 2, c, k * P:(k + 1) * P], gate_sb[:, c, :],
                                                start=(c == 0), stop=(c == HALVES - 1))
                last.then_inc(logits_done, 1)

            pe.wait_ge(gate_loaded, 16)
            for n in range(TILES // 2):
                pe.wait_ge(y_ready, n + 1)
                if n >= 2:
                    pe.wait_ge(xt_copied, n - 1)
                for c in range(HALVES):
                    for k in range(2):
                        last = nc.tensor.transpose(banks[n % 2][:, (2 * c + k) * P:(2 * c + k + 1) * P],
                                                   y[:, (2 * n + k) % 4, c * P:(c + 1) * P], ident[:, :])
                last.then_inc(transposed, 1)
                if n >= 1:
                    logits(n - 1)
            logits(TILES // 2 - 1)


def pick_first_max(dve_step, nc, values, shape, order, scratch):
    top, hit, top_hit = scratch
    top_wide, top_hit_wide = top.unsqueeze(2).broadcast_to(shape), top_hit.unsqueeze(2).broadcast_to(shape)
    dve_step(nc.vector.reduce_max(top, values, axis=AX.X))
    dve_step(nc.vector.tensor_tensor(hit, values, top_wide, ALU.is_equal))
    dve_step(nc.vector.tensor_tensor(hit, hit, order, ALU.mult))
    dve_step(nc.vector.reduce_max(top_hit, hit, axis=AX.X))
    dve_step(nc.vector.tensor_tensor(hit, hit, top_hit_wide, ALU.is_equal))
    dve_step(nc.vector.scalar_tensor_tensor(values, hit, -BIG, values, ALU.mult, ALU.add))
    return hit


def moe_phase(nc, memory, a, w_dram, ident, x_sb, norm, w_hi, w_lo, banks):
    def sb(name, shape, dt=FP32):
        return memory.enter_context(nc.sbuf_tensor(name, shape, dt))

    x_hi, x_lo = sb("moe_x_hi", [P, HALVES, TOKENS], F32R), sb("moe_x_lo", [P, HALVES, TOKENS], F32R)

    with ExitStack() as m:
        def sm(name, shape, dt=FP32):
            return m.enter_context(nc.sbuf_tensor(name, shape, dt))

        gate_sb = sm("moe_gate", [P, HALVES, EXPERTS])
        y, x_t = sm("moe_y", [P, 4, DIM]), sm("moe_x_t", [P, 2, HALVES, 2 * P])
        norm_block(nc, x_sb, x_hi, x_lo, gate_sb, EXPERTS, a["moe_gate"], ident, norm, y, x_t, banks)

        T, E, G, PER = TILES, EXPERTS, GROUPS, EXPERTS // GROUPS
        scores, choice, hit_e = (sm(n, [P, T, E]) for n in ("scores", "choice", "hit_e"))
        bias_sb, order = sm("bias_sb", [P, E]), sm("order", [P, E])
        pair_hi, pair_lo = sm("pair_hi", [P, T * G, 2]), sm("pair_lo", [P, T * G, 2])
        g_top, g_second, g_score, g_hit, g_mask, g_pen = (sm(n, [P, T, G]) for n in (
            "g_top", "g_second", "g_score", "g_hit", "g_mask", "g_pen"))
        top, top_hit, w_sum = (sm(n, [P, T]) for n in ("top", "top_hit", "w_sum"))
        w_t = sm("w_t", [P, 2, P])
        with ExitStack() as s:
            def sem(name):
                return s.enter_context(nc.semaphore(name))

            bias_loaded, order_done, sigmoid_done, step, w_transposed, w_copied, w_stored = map(sem, (
                "bias_loaded", "order_done", "sigmoid_done", "step", "w_transposed", "w_copied", "w_stored"))
            block = s.enter_context(nc.Block())

            @block.sync
            def _(sp):
                sp.dma_start(bias_sb[:, :], a["moe_bias"].partition_broadcast(P)).then_inc(bias_loaded, 16)
                for half in range(2):
                    sp.wait_ge(w_copied, half + 1)
                    sp.dma_start(w_dram.rearrange("e (t k) -> t e k", k=P)[half * 8:half * 8 + 8], w_t[:, half, :])\
                      .then_inc(w_stored, 16)
                sp.wait_ge(w_stored, 32)

            @block.gpsimd
            def _(pool):
                nc.gpsimd.iota(order[:, :], pattern=[[-1, E]], base=E, channel_multiplier=0,
                               allow_small_or_imprecise_dtypes=True).then_inc(order_done, 1)

            @block.scalar
            def _(act):
                nc.scalar.activation(scores[:, :, :], banks[7][:, 0:T * E].rearrange("p (t e) -> p t e", e=E),
                                     ACT.Sigmoid).then_inc(sigmoid_done, 1)
                act.wait_ge(w_transposed, 1)
                for half in range(2):
                    nc.scalar.copy(w_t[:, half, :], banks[0][:, half * P:(half + 1) * P]).then_inc(w_copied, 1)

            @block.tensor
            def _(pe):
                pe.wait_ge(step, STEPS)
                for half in range(2):
                    last = nc.tensor.transpose(banks[0][:, half * P:(half + 1) * P],
                                               choice[:, half * 8:half * 8 + 8, :], ident[:, :])
                last.then_inc(w_transposed, 1)

            @block.vector
            def _(dve):
                steps = [0]

                def dve_step(ins):
                    steps[0] += 1
                    ins.then_inc(step, 1)
                    dve.wait_ge(step, steps[0])

                dve.wait_ge(sigmoid_done, 1)
                dve.wait_ge(bias_loaded, 16)
                dve.wait_ge(order_done, 1)
                dve_step(nc.vector.tensor_tensor(choice[:, :, :], scores[:, :, :],
                                                 bias_sb[:, :].unsqueeze(1).broadcast_to([P, T, E]), ALU.add))
                pairs = choice[:, :, :].rearrange("p t (g q r) -> p (t g) q r", g=G, r=2)
                nc.vector.tensor_tensor(pair_hi[:, :, :], pairs[:, :, :, 0], pairs[:, :, :, 1], ALU.max)
                dve_step(nc.vector.tensor_tensor(pair_lo[:, :, :], pairs[:, :, :, 0], pairs[:, :, :, 1], ALU.min))
                flat = [v[:, :, :].rearrange("p t g -> p (t g)") for v in (g_top, g_second, g_score, g_pen)]
                nc.vector.tensor_tensor(flat[0], pair_hi[:, :, 0], pair_hi[:, :, 1], ALU.max)
                nc.vector.tensor_tensor(flat[1], pair_hi[:, :, 0], pair_hi[:, :, 1], ALU.min)
                dve_step(nc.vector.tensor_tensor(flat[3], pair_lo[:, :, 0], pair_lo[:, :, 1], ALU.max))
                dve_step(nc.vector.tensor_tensor(flat[1], flat[1], flat[3], ALU.max))
                dve_step(nc.vector.tensor_tensor(flat[2], flat[0], flat[1], ALU.add))
                wide_g = [P, T, G]
                order_g = order[:, E - G:E].unsqueeze(1).broadcast_to(wide_g)
                for n in range(TOP_GROUPS):
                    hit = pick_first_max(dve_step, nc, g_score[:, :, :], wide_g, order_g,
                                         (top[:, :], g_hit[:, :, :], top_hit[:, :]))
                    if n == 0:
                        dve_step(nc.vector.tensor_copy(g_mask[:, :, :], hit))
                    else:
                        dve_step(nc.vector.tensor_tensor(g_mask[:, :, :], g_mask[:, :, :], hit, ALU.add))
                dve_step(nc.vector.tensor_scalar(g_pen[:, :, :], g_mask[:, :, :], BIG, -BIG, ALU.mult, ALU.add))
                by_group = choice[:, :, :].rearrange("p t (g e) -> p (t g) e", g=G)
                wide_ge = [P, T * G, PER]
                mask_wide = g_mask[:, :, :].rearrange("p t g -> p (t g)").unsqueeze(2).broadcast_to(wide_ge)
                dve_step(nc.vector.tensor_tensor(by_group, by_group, mask_wide, ALU.mult))
                dve_step(nc.vector.tensor_tensor(by_group, by_group, flat[3].unsqueeze(2).broadcast_to(wide_ge),
                                                 ALU.add))
                wide_e = [P, T, E]
                order_e = order[:, :].unsqueeze(1).broadcast_to(wide_e)
                for n in range(TOP_EXPERTS):
                    pick_first_max(dve_step, nc, choice[:, :, :], wide_e, order_e,
                                   (top[:, :], hit_e[:, :, :], top_hit[:, :]))
                dve_step(nc.vector.scalar_tensor_tensor(choice[:, :, :], choice[:, :, :], -BIG / 2, scores[:, :, :],
                                                        ALU.is_lt, ALU.mult))
                dve_step(nc.vector.tensor_tensor(by_group, by_group, mask_wide, ALU.mult))
                dve_step(nc.vector.reduce_sum(w_sum[:, :], choice[:, :, :], axis=AX.X))
                dve_step(nc.vector.tensor_scalar_add(w_sum[:, :], w_sum[:, :], 1e-20))
                dve_step(nc.vector.reciprocal(w_sum[:, :], w_sum[:, :]))
                dve_step(nc.vector.tensor_scalar_mul(w_sum[:, :], w_sum[:, :], ROUTED_SCALE))
                dve_step(nc.vector.tensor_tensor(choice[:, :, :], choice[:, :, :],
                                                 w_sum[:, :].unsqueeze(2).broadcast_to(wide_e), ALU.mult))
                assert steps[0] == STEPS, steps

    w_ring = sb("w_ring", [P, W_SLOTS, GROUP_T])
    silu, prod, act = (sb(n, [P, 2, GROUP_T]) for n in ("moe_silu", "moe_prod", "moe_act"))
    act_hi, act_lo = (sb(n, [P, 2, GROUP_T], F32R) for n in ("moe_act_hi", "moe_act_lo"))
    gate_banks, up_banks, out_banks = banks[0:2], banks[2:4], banks[4:6]
    with ExitStack() as s:
        def sem(name):
            return s.enter_context(nc.semaphore(name))

        w_loaded = [sem(f"w_loaded{i}") for i in range(W_SLOTS)]
        gu_done, silu_done, prod_done, act_ready, hi_done, lo_done, down_done, x_added = map(sem, (
            "gu_done", "silu_done", "prod_done", "act_ready", "hi_done", "lo_done", "down_done", "x_added"))
        block = s.enter_context(nc.Block())

        @block.sync
        def _(sp):
            sp.sem_inc(act_ready, W_SLOTS)
            with sp.Fori(0, TOKEN_GROUPS) as g:
                for e in range(EXPERTS):
                    sp.wait_ge(act_ready, g * EXPERTS + e + 1)
                    sp.dma_start(w_ring[:, e % W_SLOTS, :],
                                 w_dram[e, bass.ds(g * GROUP_T, GROUP_T)].partition_broadcast(P))\
                      .then_inc(w_loaded[e % W_SLOTS], 16)

        @block.tensor
        def _(pe):
            pe.sem_inc(prod_done, 2)

            def gate_up(g, n):
                pe.wait_ge(prod_done, g * FBLOCKS + n + 1)
                for bank, off in ((gate_banks[n % 2], 0), (up_banks[n % 2], HALVES * P)):
                    last = None
                    for c in range(HALVES):
                        cols = slice(off + c * P, off + (c + 1) * P)
                        w = w_hi[:, n, cols], w_lo[:, n, cols]
                        x = (x_hi[:, c, bass.ds(g * GROUP_T, GROUP_T)], x_lo[:, c, bass.ds(g * GROUP_T, GROUP_T)])
                        for k, (wp, xp) in enumerate(split_products(w, x)):
                            last = nc.tensor.matmul(bank[:, :], wp, xp, start=(c == 0 and k == 0),
                                                    stop=(c == HALVES - 1 and k == 2))
                last.then_inc(gu_done, 1)

            def down(g, n):
                pe.wait_ge(lo_done, g * FBLOCKS + n + 3)
                if n == 0:
                    pe.wait_ge(x_added, 2 * g + 2)
                for t in range(GROUP_T // P):
                    rows = slice(t * P, (t + 1) * P)
                    act_parts = act_hi[:, n % 2, rows], act_lo[:, n % 2, rows]
                    w = w_hi[:, n, 2 * DIM:3 * DIM], w_lo[:, n, 2 * DIM:3 * DIM]
                    for k, (ap, wp) in enumerate(split_products(act_parts, w)):
                        last = nc.tensor.matmul(out_banks[t // 2][:, (t % 2) * DIM:(t % 2 + 1) * DIM], ap, wp,
                                                start=(n == 0 and k == 0 and t % 2 == 0),
                                                stop=(n == FBLOCKS - 1 and k == 2), skip_group_check=True)
                last.then_inc(down_done, 1)

            def group(g, last_group):
                for n in range(LAG, FBLOCKS):
                    gate_up(g, n)
                    down(g, n - LAG)
                for n in range(LAG):
                    if not last_group:
                        gate_up(g + 1, n)
                    down(g, FBLOCKS - LAG + n)

            pe.sem_inc(x_added, 2)
            for n in range(LAG):
                gate_up(0, n)
            with pe.Fori(0, TOKEN_GROUPS - 1) as g:
                group(g, False)
            group(TOKEN_GROUPS - 1, True)

        @block.scalar
        def _(act_eng):
            act_eng.sem_inc(down_done, 2)

            def silu_of(g, n):
                act_eng.wait_ge(gu_done, g * FBLOCKS + n + 1)
                nc.scalar.activation(silu[:, n % 2, :], gate_banks[n % 2][:, :], ACT.Silu).then_inc(silu_done, 1)

            def high_part(g, n):
                if n < EXPERTS:
                    act_eng.wait_ge(act_ready, g * EXPERTS + n + 1 + W_SLOTS)
                else:
                    act_eng.wait_ge(prod_done, g * FBLOCKS + n + 3)
                act_eng.wait_ge(down_done, g * FBLOCKS + n + 1)
                nc.scalar.copy(act_hi[:, n % 2, :], act[:, n % 2, :]).then_inc(hi_done, 1)

            def group(g, last_group):
                for n in range(LAG, FBLOCKS):
                    silu_of(g, n)
                    high_part(g, n - 1)
                if not last_group:
                    silu_of(g + 1, 0)
                high_part(g, FBLOCKS - 1)
                if not last_group:
                    silu_of(g + 1, 1)
                    high_part(g + 1, 0)

            silu_of(0, 0)
            silu_of(0, 1)
            high_part(0, 0)
            with act_eng.Fori(0, TOKEN_GROUPS - 1) as g:
                group(g, False)
            group(TOKEN_GROUPS - 1, True)

        @block.gpsimd
        def _(pool):
            pool.sem_inc(lo_done, 2)
            with pool.Fori(0, TOKEN_GROUPS) as g:
                for e in range(EXPERTS):
                    pool.wait_ge(w_loaded[e % W_SLOTS], 16 * (g * (EXPERTS // W_SLOTS) + e // W_SLOTS + 1))
                    pool.wait_ge(prod_done, g * FBLOCKS + e + 3)
                    pool.wait_ge(lo_done, g * FBLOCKS + e + 1)
                    nc.gpsimd.tensor_tensor(act[:, e % 2, :], prod[:, e % 2, :], w_ring[:, e % W_SLOTS, :],
                                            ALU.mult).then_inc(act_ready, 1)

        @block.vector
        def _(dve):
            def product(g, n):
                dve.wait_ge(silu_done, g * FBLOCKS + n + 1)
                if n < EXPERTS:
                    dve.wait_ge(act_ready, g * EXPERTS + max(n - 1, 0) + W_SLOTS)
                    into = prod
                else:
                    dve.wait_ge(lo_done, g * FBLOCKS + n + 1)
                    into = act
                nc.vector.tensor_tensor(into[:, n % 2, :], silu[:, n % 2, :], up_banks[n % 2][:, :],
                                        ALU.mult).then_inc(prod_done, 1)

            def low_part(g, n):
                dve.wait_ge(hi_done, g * FBLOCKS + n + 1)
                nc.vector.tensor_tensor(act_lo[:, n % 2, :], act[:, n % 2, :], act_hi[:, n % 2, :].bitcast(FP32),
                                        ALU.subtract).then_inc(lo_done, 1)

            def add_to_x(g):
                dve.wait_ge(down_done, g * FBLOCKS + FBLOCKS + 2)
                for o in range(2):
                    rows = x_sb[:, bass.ds(g * 4 + 2 * o, 2), :]
                    nc.vector.tensor_tensor(rows, rows, out_banks[o][:, :].rearrange("p (t d) -> p t d", t=2),
                                            ALU.add).then_inc(x_added, 1)

            def group(g, last_group):
                for n in range(LAG, FBLOCKS):
                    product(g, n)
                    low_part(g, n - 1)
                if not last_group:
                    product(g + 1, 0)
                low_part(g, FBLOCKS - 1)
                if not last_group:
                    product(g + 1, 1)
                    low_part(g + 1, 0)
                add_to_x(g)

            product(0, 0)
            product(0, 1)
            low_part(0, 0)
            with dve.Fori(0, TOKEN_GROUPS - 1) as g:
                group(g, False)
            group(TOKEN_GROUPS - 1, True)


def softmax_phase(nc, memory, a, x_sb, norm, w_hi, w_lo, banks):
    stats, meanvar, rstd, minus_half = norm

    def sb(name, shape, dt=FP32):
        return memory.enter_context(nc.sbuf_tensor(name, shape, dt))

    keys, values_t = sb("keys", [P, BATCH, DIM]), sb("values_t", [P, HALVES, TOKENS])
    stage = sb("lora_stage", [P, LORA_STAGES, LORA_COLS])
    y, weights, scaled = sb("att_y", [P, 2, DIM]), sb("att_weights", [P, 2, HALVES, DIM]), sb("att_scaled", [P, 2, DIM])
    top, bias, total, inverse = (sb(n, [P, BATCH, HALVES]) for n in ("att_top", "att_bias", "att_total", "att_inverse"))
    score_banks, out_banks = banks[0:2], banks[2:4]
    PARTS = 4
    with ExitStack() as s:
        def sem(name):
            return s.enter_context(nc.semaphore(name))

        ctx_loaded = [sem(f"ctx_loaded{i}") for i in range(PARTS)]
        staged = [sem(f"lora_staged{i}") for i in range(LORA_STAGES)]
        hi_split, lo_split = sem("lora_hi_split"), sem("lora_lo_split")
        stats_done, mv_done, rstd_half, rstd_done = map(sem, ("stats_done", "mv_done", "rstd_half", "rstd_done"))
        y_ready, scores_done, top_done, bias_done, exp_done, inverse_done, scaled_done, out_done, x_added = map(sem, (
            "y_ready", "scores_done", "top_done", "bias_done", "exp_done", "inverse_done", "scaled_done", "out_done",
            "x_added"))
        block = s.enter_context(nc.Block())

        @block.sync
        def _(sp):
            per = BATCH // PARTS
            for i in range(PARTS):
                b = slice(i * per, (i + 1) * per)
                sp.dma_start(keys[:, b, :], a["ctx_keys"].rearrange("(b s) d -> s b d", s=SEQ)[:, b, :])\
                  .then_inc(ctx_loaded[i], 16)
                for m in range(HALVES):
                    cols = slice(i * per * SEQ, (i + 1) * per * SEQ)
                    sp.dma_start(values_t[:, m, cols], a["ctx_t"][m, :, cols]).then_inc(ctx_loaded[i], 16)
            for n in range(LORA_CHUNKS):
                if n >= LORA_STAGES:
                    sp.wait_ge(lo_split, n - LORA_STAGES + 1)
                sp.dma_start(stage[:, n % LORA_STAGES, :], a["lora_weights"][n]).then_inc(staged[n % LORA_STAGES], 16)

        @block.gpsimd
        def _(pool):
            pool.wait_ge(mv_done, 1)
            nc.gpsimd.tensor_scalar_add(rstd[:, :], meanvar[:, :, 1], EPS).then_inc(rstd_half, 1)
            pool.wait_ge(rstd_half, 1)
            nc.gpsimd.tensor_tensor(rstd[:, :], rstd[:, :], minus_half[:, :], ALU.pow).then_inc(rstd_done, 1)
            for n in range(LORA_CHUNKS):
                pool.wait_ge(hi_split, n + 1)
                nc.gpsimd.tensor_tensor(w_lo[:, n, :], stage[:, n % LORA_STAGES, :], w_hi[:, n, :].bitcast(FP32),
                                        ALU.subtract).then_inc(lo_split, 1)

        @block.vector
        def _(dve):
            for t in range(TILES):
                nc.vector.bn_stats(stats[:, t, :], x_sb[:, t, :]).then_inc(stats_done, 1)
            for t in range(TILES):
                dve.wait_ge(stats_done, t + 1)
                last = nc.vector.bn_aggr(meanvar[:, t, :], stats[:, t, :])
            last.then_inc(mv_done, 1)
            dve.wait_ge(rstd_done, 1)

            def normalize(b):
                if b >= 2:
                    dve.wait_ge(scores_done, b - 1)
                nc.vector.tensor_scalar(y[:, b % 2, :], x_sb[:, b, :], meanvar[:, b, 0:1], rstd[:, b:b + 1],
                                        ALU.subtract, ALU.mult).then_inc(y_ready, 1)

            normalize(0)
            for i in range(BATCH + 2):
                if i + 1 < BATCH:
                    normalize(i + 1)
                if i < BATCH:
                    dve.wait_ge(scores_done, i + 1)
                    nc.vector.reduce_max(top[:, i, :], score_banks[i % 2][:, :].rearrange("p (m d) -> p m d", m=HALVES),
                                         axis=AX.X).then_inc(top_done, 1)
                if 1 <= i <= BATCH:
                    dve.wait_ge(exp_done, HALVES * i)
                    nc.vector.reciprocal(inverse[:, i - 1, :], total[:, i - 1, :]).then_inc(inverse_done, 1)
                if i < BATCH:
                    dve.wait_ge(top_done, i + 1)
                    nc.vector.tensor_scalar_mul(bias[:, i, :], top[:, i, :], -SOFTMAX_SCALE).then_inc(bias_done, 1)
                if 1 <= i <= BATCH:
                    b = i - 1
                    dve.wait_ge(inverse_done, i)
                    if b >= 2:
                        dve.wait_ge(out_done, b - 1)
                    for m in range(HALVES):
                        nc.vector.tensor_scalar_mul(scaled[:, b % 2, m * P:(m + 1) * P],
                                                    values_t[:, m, b * SEQ:(b + 1) * SEQ],
                                                    inverse[:, b, m:m + 1]).then_inc(scaled_done, 1)
                if i >= 2:
                    b = i - 2
                    dve.wait_ge(out_done, b + 1)
                    nc.vector.tensor_tensor(x_sb[:, b, :], x_sb[:, b, :], out_banks[b % 2][:, 0:DIM],
                                            ALU.add).then_inc(x_added, 1)

        @block.scalar
        def _(act):
            for b in range(BATCH):
                act.wait_ge(bias_done, b + 1)
                if b >= 2:
                    act.wait_ge(out_done, b - 1)
                for m in range(HALVES):
                    nc.scalar.activation(weights[:, b % 2, m, :], score_banks[b % 2][:, m * DIM:(m + 1) * DIM],
                                         ACT.Exp, bias=bias[:, b, m:m + 1], scale=SOFTMAX_SCALE,
                                         accum_out=total[:, b, m:m + 1]).then_inc(exp_done, 1)
                if b % 2:
                    n = b // 2
                    act.wait_ge(staged[n % LORA_STAGES], 16 * (n // LORA_STAGES + 1))
                    nc.scalar.copy(w_hi[:, n, :], stage[:, n % LORA_STAGES, :]).then_inc(hi_split, 1)

        @block.tensor
        def _(pe):
            def output(b):
                pe.wait_ge(scaled_done, HALVES * (b + 1))
                pe.wait_ge(exp_done, HALVES * (b + 1))
                if b >= 2:
                    pe.wait_ge(x_added, b - 1)
                for m in range(HALVES):
                    last = nc.tensor.matmul(out_banks[b % 2][:, 0:DIM], scaled[:, b % 2, m * P:(m + 1) * P],
                                            weights[:, b % 2, m, :], start=(m == 0), stop=(m == HALVES - 1))
                last.then_inc(out_done, 1)

            for b in range(BATCH):
                if b % (BATCH // PARTS) == 0:
                    pe.wait_ge(ctx_loaded[b // (BATCH // PARTS)], 16 * (1 + HALVES))
                pe.wait_ge(y_ready, b + 1)
                if b >= 2:
                    pe.wait_ge(exp_done, HALVES * (b - 1))
                for m in range(HALVES):
                    last = nc.tensor.matmul(score_banks[b % 2][:, m * DIM:(m + 1) * DIM],
                                            keys[:, b, m * P:(m + 1) * P], y[:, b % 2, :], start=True, stop=True)
                last.then_inc(scores_done, 1)
                if b >= 1:
                    output(b - 1)
            output(BATCH - 1)


def lora_router(nc, memory, ident, mask_dram, rw_dram, x_dram, x_sb, banks):
    def sm(name, shape, dt=FP32):
        return memory.enter_context(nc.sbuf_tensor(name, shape, dt))

    T, E = TILES, LORA_EXPERTS
    probs, order = sm("probs", [P, T, E]), sm("lora_order", [P, E])
    masks, rw = sm("picked_masks", [P, T, PICKS, E]), sm("rw", [P, P])
    top, top_hit, total = sm("picked_top", [P, PICKS, T]), sm("lora_top_hit", [P, T]), sm("lora_total", [P, T])
    hit = sm("lora_hit", [P, T, E])
    masks_t, rw_t = sm("masks_t", [P, 2, P], BF16), sm("rw_t", [P, P])
    with ExitStack() as s:
        def sem(name):
            return s.enter_context(nc.semaphore(name))

        consts, exp_ready, exp_done, step, transposed, copied, stored = map(sem, (
            "consts", "exp_ready", "exp_done", "step", "transposed", "copied", "stored"))
        block = s.enter_context(nc.Block())

        @block.gpsimd
        def _(pool):
            nc.gpsimd.memset(rw[:, :], 0.0)
            nc.gpsimd.iota(order[:, :], pattern=[[-1, E]], base=E, channel_multiplier=0,
                           allow_small_or_imprecise_dtypes=True).then_inc(consts, 1)

        @block.scalar
        def _(act):
            act.wait_ge(exp_ready, 1)
            nc.scalar.activation(probs[:, :, :], probs[:, :, :], ACT.Exp).then_inc(exp_done, 1)
            act.wait_ge(transposed, 1)
            for half in range(2):
                nc.scalar.copy(masks_t[:, half, :], banks[0][:, half * P:(half + 1) * P]).then_inc(copied, 1)
            nc.scalar.copy(rw_t[:, :], banks[0][:, 2 * P:3 * P]).then_inc(copied, 1)

        @block.tensor
        def _(pe):
            pe.wait_ge(step, LORA_STEPS)
            for half in range(2):
                nc.tensor.transpose(banks[0][:, half * P:(half + 1) * P], masks[:, half * 8:half * 8 + 8, :, :],
                                    ident[:, :])
            nc.tensor.transpose(banks[0][:, 2 * P:3 * P], rw[:, :], ident[:, :]).then_inc(transposed, 1)

        @block.sync
        def _(sp):
            sp.dma_start(x_dram, x_sb[:, :, :]).then_inc(stored, 16)
            for half in range(2):
                sp.wait_ge(copied, half + 1)
                sp.dma_start(mask_dram.rearrange("e (t k) -> t e k", k=P)[half * 8:half * 8 + 8], masks_t[:, half, :])\
                  .then_inc(stored, 16)
            sp.wait_ge(copied, 3)
            sp.dma_start(rw_dram.rearrange("e (t k) -> t e k", k=P), rw_t[0:T * PICKS, :]).then_inc(stored, 16)
            sp.wait_ge(stored, 64)

        @block.vector
        def _(dve):
            steps = [0]

            def dve_step(ins):
                steps[0] += 1
                ins.then_inc(step, 1)
                dve.wait_ge(step, steps[0])

            wide = [P, T, E]
            logits = banks[7][:, 0:T * E].rearrange("p (t e) -> p t e", e=E)
            dve.wait_ge(consts, 1)
            dve_step(nc.vector.reduce_max(total[:, :], logits, axis=AX.X))
            nc.vector.tensor_tensor(probs[:, :, :], logits, total[:, :].unsqueeze(2).broadcast_to(wide),
                                    ALU.subtract).then_inc(exp_ready, 1)
            dve.wait_ge(exp_done, 1)
            dve_step(nc.vector.reduce_sum(total[:, :], probs[:, :, :], axis=AX.X))
            dve_step(nc.vector.reciprocal(total[:, :], total[:, :]))
            dve_step(nc.vector.tensor_tensor(probs[:, :, :], probs[:, :, :],
                                             total[:, :].unsqueeze(2).broadcast_to(wide), ALU.mult))
            for k in range(PICKS):
                pick_first_max(dve_step, nc, probs[:, :, :], wide, order[:, :].unsqueeze(1).broadcast_to(wide),
                               (top[:, k, :], hit[:, :, :], top_hit[:, :]))
                if k == 0:
                    dve_step(nc.vector.tensor_copy(masks[:, :, 0, :], hit[:, :, :]))
                else:
                    dve_step(nc.vector.tensor_tensor(masks[:, :, 1, :], hit[:, :, :], masks[:, :, 0, :],
                                                     ALU.subtract))
            dve_step(nc.vector.tensor_tensor(total[:, :], top[:, 0, :], top[:, 1, :], ALU.add))
            dve_step(nc.vector.reciprocal(total[:, :], total[:, :]))
            rw_view = rw[:, 0:T * PICKS].rearrange("p (t k) -> p k t", k=PICKS)
            dve_step(nc.vector.tensor_tensor(rw_view, top[:, :, :], total[:, :].unsqueeze(1).broadcast_to(
                [P, PICKS, T]), ALU.mult))
            assert steps[0] == LORA_STEPS, steps


def lora_experts(nc, memory, out_rows, mask_dram, rw_dram, x_rows, x_hi, x_lo, w_hi, w_lo, banks):
    def sb(name, shape, dt=FP32):
        return memory.enter_context(nc.sbuf_tensor(name, shape, dt))

    am_hi, am_lo = (sb(n, [P, 2, 2, HALVES, GROUP_T], F32R) for n in ("am_hi", "am_lo"))
    masks = sb("masks_sb", [P, 2, HALVES, TOKENS], BF16)
    rw = sb("rw_sb", [P, PICKS, GROUP_T])
    hid_hi, hid_lo = (sb(n, [P, 2, GROUP_T], F32R) for n in ("hid_hi", "hid_lo"))
    f = sb("hid", [P, 4, GROUP_T])
    x_g = sb("x_g", [P, GROUP_T // P, DIM])
    FB, TG = LORA_BLOCKS, GROUP_T // P
    SECOND, BOTH = range(2)
    UNITS = [(kind, j) for kind in range(2) for j in range(4)]
    x_banks, out_banks = banks[0:2], banks[2:4]
    term_banks = {BOTH: banks[4:6], SECOND: banks[6:8]}
    a_banks = banks[6:8] + banks[4:6]
    with ExitStack() as s:
        def sem(name):
            return s.enter_context(nc.semaphore(name))

        masks_loaded, rw_loaded, x_loaded, stored = map(sem, ("masks_loaded", "rw_loaded", "x_loaded", "stored"))
        a_done, am_mul, am_hi_done, am_lo_dve, am_lo_pool = map(sem, (
            "a_done", "am_mul", "am_hi_done", "am_lo_dve", "am_lo_pool"))
        first_done, second_done, silu_done, prod_done, weighted, both_done = map(sem, (
            "first_done", "second_done", "silu_done", "prod_done", "weighted", "both_done"))
        hi_done, lo_done, down_done = sem("hi_done"), sem("lo_done"), sem("down_done")
        terms_done = [sem("second_terms_done"), sem("both_terms_done")]
        t_mul, t_sum, t_hi, t_lo, b2_done, x_added = map(sem, ("t_mul", "t_sum", "t_hi", "t_lo", "b2_done", "x_added"))
        block = s.enter_context(nc.Block())

        def mask(g, kind, half):
            return masks[:, kind, half, bass.ds(g * GROUP_T, GROUP_T)]

        def low_inputs_split(engine, g, units):
            engine.wait_ge(am_lo_dve, 4 * g + (units + 1) // 2)
            engine.wait_ge(am_lo_pool, 4 * g + units // 2)

        @block.sync
        def _(sp):
            for kind in range(2):
                for half in range(HALVES):
                    source = bass.AP(mask_dram.tensor, (kind * LORA_EXPERTS + half * 4) * TOKENS,
                                     [[TOKENS, 4], [0, RANK], [1, TOKENS]])
                    sp.dma_start(masks[:, kind, half, :], source).then_inc(masks_loaded, 16)

            def load_rw(g):
                for k in range(PICKS):
                    sp.dma_start(rw[:, k, :], rw_dram[k, bass.ds(g * GROUP_T, GROUP_T)].partition_broadcast(P))\
                      .then_inc(rw_loaded, 16)

            def load_x(g):
                sp.dma_start(x_g[:, :, :], x_rows[:, bass.ds(g * TG, TG), :]).then_inc(x_loaded, 16)

            def store(g):
                sp.wait_ge(x_added, 2 * g + 4)
                sp.dma_start(out_rows[:, bass.ds(g * TG, TG), :], x_g[:, :, :]).then_inc(stored, 16)

            load_rw(0)
            load_x(0)
            with sp.Fori(0, TOKEN_GROUPS - 1) as g:
                sp.wait_ge(weighted, 2 * FB * (g + 1))
                load_rw(g + 1)
                store(g)
                sp.wait_ge(stored, 16 * (g + 1))
                load_x(g + 1)
            store(TOKEN_GROUPS - 1)
            sp.wait_ge(stored, 16 * TOKEN_GROUPS)

        def weight_cols(chunk, which, c):
            cols = slice(which * DIM + c * P, which * DIM + (c + 1) * P)
            return w_hi[:, chunk, cols], w_lo[:, chunk, cols]

        @block.tensor
        def _(pe):
            def x_cols(g, c):
                return x_hi[:, c, bass.ds(g * GROUP_T, GROUP_T)], x_lo[:, c, bass.ds(g * GROUP_T, GROUP_T)]

            def low_rank_in(g, wait):
                for j in range(4):
                    w, half = j // 2, j % 2
                    if wait:
                        pe.wait_ge(t_mul, 4 * (g - 1) + j + 1)
                    last = None
                    for c in range(HALVES):
                        cols = slice(w * 2 * DIM + c * DIM + half * P, w * 2 * DIM + c * DIM + (half + 1) * P)
                        parts = w_hi[:, FB, cols], w_lo[:, FB, cols]
                        for k, (wp, xp) in enumerate(split_products(parts, x_cols(g, c))):
                            last = nc.tensor.matmul(a_banks[j][:, :], wp, xp,
                                                    start=(c == 0 and k == 0), stop=(c == 1 and k == 2))
                    last.then_inc(a_done, 1)

            def base(g, n, wait):
                if wait:
                    pe.wait_ge(prod_done, 2 * (FB * g + n))
                for w in range(2):
                    for c in range(HALVES):
                        for k, (wp, xp) in enumerate(split_products(weight_cols(n, w, c), x_cols(g, c))):
                            nc.tensor.matmul(x_banks[w][:, :], wp, xp, start=(c == 0 and k == 0), stop=False,
                                             skip_group_check=True)

            def low_rank(g, n, kind):
                if n == 0:
                    low_inputs_split(pe, g, 4 * (kind + 1))
                if kind == 1:
                    pe.wait_ge(prod_done, 2 * (FB * g + n) + 1)
                for w in range(2):
                    for half in range(HALVES):
                        am = am_hi[:, kind, w, half, :], am_lo[:, kind, w, half, :]
                        for k, (wp, ap) in enumerate(split_products(weight_cols(n, 2 + w, half), am)):
                            last = nc.tensor.matmul(x_banks[w][:, :], wp, ap, start=False,
                                                    stop=(half == 1 and k == 2), skip_group_check=True)
                last.then_inc(second_done if kind else first_done, 1)

            def terms(g, n, which):
                pe.wait_ge(lo_done, 2 * (FB * g + n) + which + 3)
                for half in range(HALVES):
                    hid = hid_hi[:, which, :], hid_lo[:, which, :]
                    for j, (wp, hp) in enumerate(split_products(weight_cols(n, 5, half), hid)):
                        last = nc.tensor.matmul(term_banks[which][half][:, :], wp, hp, start=(n == 0 and j == 0),
                                                stop=(n == FB - 1 and j == 2))
                last.then_inc(terms_done[which], 1)

            def down(g, n, tiles):
                pe.wait_ge(lo_done, 2 * (FB * g + n) + BOTH + 3)
                if n == 0 and tiles[0] == 0:
                    pe.wait_ge(x_added, 2 * g + 2)
                for t in tiles:
                    rows = slice(t * P, (t + 1) * P)
                    w = w_hi[:, n, 4 * DIM:5 * DIM], w_lo[:, n, 4 * DIM:5 * DIM]
                    for k, (hp, wp) in enumerate(split_products((hid_hi[:, BOTH, rows], hid_lo[:, BOTH, rows]), w)):
                        last = nc.tensor.matmul(out_banks[t // 2][:, (t % 2) * DIM:(t % 2 + 1) * DIM], hp, wp,
                                                start=(n == 0 and k == 0 and t % 2 == 0), stop=False,
                                                skip_group_check=True)
                if tiles[-1] == TG - 1:
                    last.then_inc(down_done, 1)

            def low_rank_out(g):
                pe.wait_ge(t_lo, 2 * (g + 1))
                for t in range(TG):
                    for half in range(HALVES):
                        rows = slice(t * P, (t + 1) * P)
                        cols = slice(4 * DIM + half * DIM, 4 * DIM + (half + 1) * DIM)
                        w = w_hi[:, FB, cols], w_lo[:, FB, cols]
                        parts = hid_hi[:, half, rows], hid_lo[:, half, rows]
                        for k, (hp, wp) in enumerate(split_products(parts, w)):
                            last = nc.tensor.matmul(out_banks[t // 2][:, (t % 2) * DIM:(t % 2 + 1) * DIM], hp, wp,
                                                    start=False, stop=(half == 1 and k == 2), skip_group_check=True)
                last.then_inc(b2_done, 1)

            def group(g, last_group):
                low_rank(g, 0, 0)
                low_rank(g, 0, 1)
                for n in range(1, FB):
                    base(g, n, True)
                    low_rank(g, n, 0)
                    terms(g, n - 1, BOTH)
                    down(g, n - 1, (0, 1))
                    low_rank(g, n, 1)
                    terms(g, n - 1, SECOND)
                    down(g, n - 1, (2, 3))
                terms(g, FB - 1, SECOND)
                if not last_group:
                    base(g + 1, 0, True)
                terms(g, FB - 1, BOTH)
                down(g, FB - 1, (0, 1, 2, 3))
                if not last_group:
                    low_rank_in(g + 1, True)
                low_rank_out(g)

            pe.sem_inc(x_added, 2)
            low_rank_in(0, False)
            base(0, 0, False)
            with pe.Fori(0, TOKEN_GROUPS - 1) as g:
                group(g, False)
            group(TOKEN_GROUPS - 1, True)

        @block.scalar
        def _(act):
            def low_inputs_high(g):
                for u, (kind, j) in enumerate(UNITS):
                    act.wait_ge(am_mul, 8 * g + u + 1)
                    nc.scalar.copy(am_hi[:, kind, j // 2, j % 2, :], f[:, u % 4, :]).then_inc(am_hi_done, 1)

            def group(g, last_group):
                for n in range(FB):
                    F = FB * g + n
                    for k in range(PICKS):
                        act.wait_ge(second_done if k else first_done, F + 1)
                        if k == 0:
                            act.wait_ge(lo_done, 2 * F + 2)
                            if n == 0:
                                low_inputs_split(act, g, 8)
                        nc.scalar.activation(f[:, k, :], x_banks[0][:, :], ACT.Silu).then_inc(silu_done, 1)
                    act.wait_ge(weighted, 2 * F + 2)
                    act.wait_ge(terms_done[SECOND], F + 1)
                    if n == 0:
                        act.wait_ge(b2_done, g + 1)
                    nc.scalar.copy(hid_hi[:, SECOND, :], f[:, 1, :]).then_inc(hi_done, 1)
                    act.wait_ge(both_done, F + 1)
                    act.wait_ge(down_done, F + 1)
                    nc.scalar.copy(hid_hi[:, BOTH, :], f[:, 0, :]).then_inc(hi_done, 1)
                for half in range(HALVES):
                    act.wait_ge(t_sum, 2 * g + half + 1)
                    if half == 0:
                        act.wait_ge(down_done, FB * (g + 1) + 1)
                    nc.scalar.copy(hid_hi[:, half, :], f[:, 2 + half, :]).then_inc(t_hi, 1)
                if not last_group:
                    low_inputs_high(g + 1)

            for which in range(2):
                act.sem_inc(terms_done[which], 1)
            act.sem_inc(down_done, 1)
            act.sem_inc(b2_done, 1)
            act.sem_inc(lo_done, 2)
            low_inputs_high(0)
            with act.Fori(0, TOKEN_GROUPS - 1) as g:
                group(g, False)
            group(TOKEN_GROUPS - 1, True)

        def low_input_low(engine, ops, g, u):
            kind, j = UNITS[u]
            engine.wait_ge(am_hi_done, 8 * g + u + 1)
            ops.tensor_tensor(am_lo[:, kind, j // 2, j % 2, :], f[:, u % 4, :],
                              am_hi[:, kind, j // 2, j % 2, :].bitcast(FP32), ALU.subtract)\
               .then_inc(am_lo_pool if u % 2 else am_lo_dve, 1)

        @block.gpsimd
        def _(pool):
            def group(g, last_group):
                for n in range(FB):
                    F = FB * g + n
                    if n == 0:
                        pool.wait_ge(rw_loaded, 16 * PICKS * (g + 1))
                    for k in range(PICKS):
                        pool.wait_ge(prod_done, 2 * F + k + 1)
                        nc.gpsimd.tensor_tensor(f[:, k, :], f[:, k, :], rw[:, k, :], ALU.mult).then_inc(weighted, 1)
                    pool.wait_ge(weighted, 2 * F + 2)
                    nc.gpsimd.tensor_tensor(f[:, 0, :], f[:, 0, :], f[:, 1, :], ALU.add).then_inc(both_done, 1)
                for half in range(HALVES):
                    pool.wait_ge(t_mul, 4 * g + 2 + half + 1)
                    nc.gpsimd.tensor_tensor(f[:, 2 + half, :], f[:, 2 + half, :], f[:, half, :],
                                            ALU.add).then_inc(t_sum, 1)
                if not last_group:
                    for u in range(1, 8, 2):
                        low_input_low(pool, nc.gpsimd, g + 1, u)

            for u in range(1, 8, 2):
                low_input_low(pool, nc.gpsimd, 0, u)
            with pool.Fori(0, TOKEN_GROUPS - 1) as g:
                group(g, False)
            group(TOKEN_GROUPS - 1, True)

        @block.vector
        def _(dve):
            def low_input_product(g, u, wait):
                kind, j = UNITS[u]
                dve.wait_ge(a_done, 4 * g + j + 1)
                if u >= 4:
                    low_inputs_split(dve, g, u - 3)
                elif wait:
                    if u < 2:
                        dve.wait_ge(t_sum, 2 * (g - 1) + u + 1)
                    else:
                        dve.wait_ge(t_lo, 2 * (g - 1) + u - 1)
                nc.vector.tensor_tensor(f[:, u % 4, :], a_banks[j][:, :], mask(g, kind, j % 2),
                                        ALU.mult).then_inc(am_mul, 1)

            def low_inputs(g, wait):
                for u in range(4):
                    low_input_product(g, u, wait)
                low_input_low(dve, nc.vector, g, 0)
                low_input_product(g, 4, wait)
                low_input_product(g, 5, wait)
                low_input_low(dve, nc.vector, g, 2)
                low_input_product(g, 6, wait)
                low_input_product(g, 7, wait)
                low_input_low(dve, nc.vector, g, 4)
                low_input_low(dve, nc.vector, g, 6)

            def add_to_x(g):
                dve.wait_ge(b2_done, g + 2)
                dve.wait_ge(x_loaded, 16 * (g + 1))
                for o in range(2):
                    rows = x_g[:, 2 * o:2 * o + 2, :]
                    nc.vector.tensor_tensor(rows, rows, out_banks[o][:, :].rearrange("p (t d) -> p t d", t=2),
                                            ALU.add).then_inc(x_added, 1)

            def masked_terms(g, which):
                dve.wait_ge(terms_done[which], FB * (g + 1) + 1)
                if which == SECOND:
                    low_inputs_split(dve, g, 8)
                else:
                    dve.wait_ge(lo_done, 2 * FB * (g + 1) + 2)
                for half in range(HALVES):
                    nc.vector.tensor_tensor(f[:, (2 if which == SECOND else 0) + half, :],
                                            term_banks[which][half][:, :], mask(g, 1 - which, half),
                                            ALU.mult).then_inc(t_mul, 1)

            def group(g, last_group):
                for n in range(FB):
                    F = FB * g + n
                    for k in range(PICKS):
                        dve.wait_ge(silu_done, 2 * F + k + 1)
                        nc.vector.tensor_tensor(f[:, k, :], f[:, k, :], x_banks[1][:, :],
                                                ALU.mult).then_inc(prod_done, 1)
                    for which in (SECOND, BOTH):
                        dve.wait_ge(hi_done, 2 * F + which + 1)
                        nc.vector.tensor_tensor(hid_lo[:, which, :], f[:, 1 - which, :],
                                                hid_hi[:, which, :].bitcast(FP32), ALU.subtract).then_inc(lo_done, 1)
                masked_terms(g, SECOND)
                masked_terms(g, BOTH)
                for half in range(HALVES):
                    dve.wait_ge(t_hi, 2 * g + half + 1)
                    nc.vector.tensor_tensor(hid_lo[:, half, :], f[:, 2 + half, :],
                                            hid_hi[:, half, :].bitcast(FP32), ALU.subtract).then_inc(t_lo, 1)
                if not last_group:
                    low_inputs(g + 1, True)
                add_to_x(g)

            dve.wait_ge(masks_loaded, 16 * 2 * HALVES)
            low_inputs(0, False)
            with dve.Fori(0, TOKEN_GROUPS - 1) as g:
                group(g, False)
            group(TOKEN_GROUPS - 1, True)


def lora_weights(inputs):
    import numpy as np

    def rows_in_halves(w):
        w = np.asarray(w)
        return w.reshape(HALVES, P, -1).transpose(1, 0, 2).reshape(P, -1)

    def get(n):
        return np.asarray(inputs["L1_ffn_" + n])

    b1, b3 = (get(n).transpose(0, 2, 1).reshape(DIM, -1) for n in ("B1", "B3"))
    a2 = get("A2").reshape(DIM, -1).T
    chunks = []
    for n in range(LORA_BLOCKS):
        fs = slice(n * P, (n + 1) * P)
        chunks.append(np.concatenate([rows_in_halves(m) for m in (
            get("W1")[fs].T, get("W3")[fs].T, b1[:, fs], b3[:, fs])] + [get("W2").T[fs], a2[fs]], axis=1))
    chunks.append(np.concatenate([rows_in_halves(m) for m in (
        get("A1").reshape(DIM, DIM).T, get("A3").reshape(DIM, DIM).T,
        get("B2").transpose(0, 2, 1).reshape(DIM, DIM))], axis=1))
    return np.stack(chunks)


def moe_weights(inputs):
    import numpy as np

    def blocks(experts, shared):
        return np.concatenate([np.asarray(experts), np.asarray(shared)])

    gate = blocks(np.asarray(inputs["L0_ffn_gate_w"]).reshape(-1, DIM), inputs["L0_ffn_sh_gate_w"])
    up = blocks(np.asarray(inputs["L0_ffn_up_w"]).reshape(-1, DIM), inputs["L0_ffn_sh_up_w"])
    down = blocks(np.asarray(inputs["L0_ffn_down_w"]).transpose(0, 2, 1).reshape(-1, DIM),
                  np.asarray(inputs["L0_ffn_sh_down_w"]).T)
    in_rows = [w.reshape(FBLOCKS, P, HALVES, P).transpose(0, 3, 2, 1).reshape(FBLOCKS, P, DIM) for w in (gate, up)]
    return np.concatenate([*in_rows, down.reshape(FBLOCKS, P, DIM)], axis=2)


def kernel(**inputs):
    import numpy as np
    import concourse.bacc as bacc
    from concourse.bass_utils import run_bass_kernel_spmd

    nc = bacc.Bacc("TRN2", target_bir_lowering=False, num_devices=1)
    ctx = np.asarray(inputs["ctx_2048"])
    ctx_rev = ctx.reshape(TOKENS, HALVES, P)[:, :, ::-1]
    arrays = {
        "x": np.asarray(inputs["x"]).reshape(TOKENS, DIM),
        "ctx_t": ctx_rev.transpose(1, 2, 0),
        "ssm_kernel": inputs["L0_xattn_ssm_kernel"],
        "moe_gate": np.asarray(inputs["L0_ffn_gate_weight"]).T.reshape(HALVES, P, EXPERTS).transpose(1, 0, 2),
        "moe_bias": inputs["L0_ffn_e_score_correction_bias"],
        "moe_weights": moe_weights(inputs),
        "ctx_keys": ctx_rev.reshape(TOKENS, DIM),
        "lora_gate": np.asarray(inputs["L1_ffn_Wg"]).T.reshape(HALVES, P, LORA_EXPERTS).transpose(1, 0, 2),
        "lora_weights": lora_weights(inputs),
        "D": np.asarray(inputs["L0_xattn_D"]).reshape(HEADS, 1),
    }
    in_map, args = {}, {}
    for name, value in arrays.items():
        value = np.ascontiguousarray(value)
        in_map["in_" + name] = value
        args[name] = nc.dram_tensor("in_" + name, value.shape, mybir.dt.from_np(value.dtype), kind="ExternalInput").ap()
    out = nc.dram_tensor("out_x", (TOKENS, DIM), FP32, kind="ExternalOutput").ap()
    build(nc, args, out)
    r = run_bass_kernel_spmd(nc, [in_map], core_ids=[0])
    return r.results[0]["out_x"].reshape(BATCH, SEQ, DIM)
```

```python
import concourse.bass as bass
from concourse import mybir
from contextlib import ExitStack

UPTO = 4

FP32 = mybir.dt.float32
F32R = mybir.dt.float32r
BF16 = mybir.dt.bfloat16
ALU = mybir.AluOpType
ACT = mybir.ActivationFunctionType
AX = mybir.AxisListType

P = 128
BATCH = 16
SEQ = 128
DIM = 256
TOKENS = BATCH * SEQ
TILES = TOKENS // P
HALVES = DIM // P
EPS = 1e-5

HEADS = 16
HEAD_DIM = 8
CHUNK_B = 8
CHUNKS = BATCH // CHUNK_B
PAIRS = CHUNK_B * HEAD_DIM * HEAD_DIM
KPAD = 3 * P

EXPERTS = 16
GROUPS = 4
TOP_GROUPS = 2
TOP_EXPERTS = 4
ROUTED_SCALE = 2.5
SHARED_BLOCKS = 2
FBLOCKS = EXPERTS + SHARED_BLOCKS
MOE_COLS = 3 * DIM
GROUP_T = 512
TOKEN_GROUPS = TOKENS // GROUP_T
W_SLOTS = 4
EARLY_NORM = TILES - TILES // TOKEN_GROUPS
LAG = 2
BIG = 1e30
W_ORDER = [EXPERTS + n for n in range(SHARED_BLOCKS)] + list(range(EXPERTS))
SPLIT_EARLY = HEADS // 2
STAGES, LATE_STAGES = 4, 2
SHARED_STEPS = TOKEN_GROUPS * SHARED_BLOCKS
SENTINELS = 8 - TOP_EXPERTS
SOFTMAX_SCALE = DIM ** -0.5
LORA_EXPERTS = 8
RANK = 32
PICKS = 2
LORA_BLOCKS = 7
LORA_CHUNKS = LORA_BLOCKS + 1
LORA_COLS = 6 * DIM
CTX_SLOTS = 3
LORA_STEPS = 4 + PICKS * 7 + 3
STEPS = 5 + TOP_GROUPS * 7 + 3 + 2 + 6


def build(nc, a, out):
    x_rows = a["x"].rearrange("(t p) d -> p t d", p=P)
    out_rows = out.rearrange("(t p) d -> p t d", p=P)
    kpad_dram = nc.dram_tensor("kpad_scratch", [HEADS, KPAD], FP32).ap()
    w_dram = nc.dram_tensor("w_scratch", [EXPERTS, TOKENS], FP32).ap()
    mask_dram = nc.dram_tensor("mask_scratch", [PICKS * LORA_EXPERTS, TOKENS], BF16).ap()
    rw_dram = nc.dram_tensor("rw_scratch", [PICKS, TOKENS], FP32).ap()
    x_dram_rows = nc.dram_tensor("x_scratch", [TOKENS, DIM], FP32).ap().rearrange("(t p) d -> p t d", p=P)

    with ExitStack() as whole:
        def keep(name, shape, dt=FP32):
            return whole.enter_context(nc.sbuf_tensor(name, shape, dt))

        ident = keep("ident", [P, P])
        norm = (keep("stats", [P, TILES, 6]), keep("meanvar", [P, TILES, 2]), keep("rstd", [P, TILES]),
                keep("minus_half", [P, TILES]))
        banks = [whole.enter_context(nc.psum_tensor(f"bank{i}", [P, 512], FP32)) for i in range(8)]

        def split_weights(stack, name, shape):
            return (stack.enter_context(nc.sbuf_tensor(name + "_hi", shape, F32R)),
                    stack.enter_context(nc.sbuf_tensor(name + "_lo", shape, F32R)))

        def far(name, shape, dt=F32R):
            return whole.enter_context(nc.sbuf_tensor(name, shape, dt, side="right"))

        with ExitStack() as residual:
            x_sb = residual.enter_context(nc.sbuf_tensor("x_sb", [P, TILES, DIM], FP32))
            with ExitStack() as weights:
                w = split_weights(weights, "moe_w", [P, FBLOCKS, MOE_COLS])
                with ExitStack() as queries:
                    q_t = queries.enter_context(nc.sbuf_tensor("q_t", [P, HALVES, TOKENS], FP32, side="right"))
                    with ExitStack() as memory:
                        conv_phase(nc, memory, a, x_rows, kpad_dram, ident, x_sb, norm, q_t, *w, banks)
                    x_parts = split_weights(weights, "moe_x", [P, HALVES, TOKENS])
                    with ExitStack() as memory:
                        conv_end_phase(nc, memory, a, ident, x_sb, norm, q_t, *x_parts, banks)
                ctx_ring = far("ctx_ring", [P, CTX_SLOTS, 2 * DIM], FP32)
                if UPTO > 1:
                    with ExitStack() as memory:
                        moe_phase(nc, memory, a, w_dram, ident, x_sb, norm, *x_parts, *w, ctx_ring, banks)
            if UPTO > 2:
                w = [far(n, [P, LORA_CHUNKS, LORA_COLS]) for n in ("lora_w_hi", "lora_w_lo")]
                x_parts = [far(n, [P, HALVES, TOKENS]) for n in ("lora_x_hi", "lora_x_lo")]
                masks = far("masks_sb", [P, 2, HALVES, TOKENS], BF16)
                with ExitStack() as memory:
                    softmax_phase(nc, memory, a, mask_dram, rw_dram, x_dram_rows, ident, x_sb, norm, *w, *x_parts,
                                  masks, ctx_ring, banks)
            if UPTO < 4:
                with ExitStack() as s:
                    stored = s.enter_context(nc.semaphore("stored"))
                    block = s.enter_context(nc.Block())

                    @block.sync
                    def _(sp):
                        sp.dma_start(out_rows, x_sb[:, :, :]).then_inc(stored, 16)
                        sp.wait_ge(stored, 16)

        if UPTO > 3:
            with ExitStack() as memory:
                lora_experts(nc, memory, out_rows, mask_dram, rw_dram, x_dram_rows, *x_parts, *w, masks, ctx_ring,
                             banks)


def conv_phase(nc, memory, a, x_rows, kpad_dram, ident, x_sb, norm, q_t, w_hi, w_lo, banks):
    stats, meanvar, rstd, minus_half = norm

    def sb(name, shape, dt=FP32):
        return memory.enter_context(nc.sbuf_tensor(name, shape, dt))

    ctx_t = sb("ctx_t", [P, HALVES, TOKENS])
    toeplitz = sb("toeplitz", [P, HEADS, 2 * P])
    y = sb("y", [P, 4, DIM])
    kv = sb("kv", [P, 2, HALVES, PAIRS])
    prod = sb("prod", [P, 2, PAIRS])
    kpad = sb("kpad", [HEADS, KPAD])
    d_col = sb("d_col", [HEADS, 1])
    stage = sb("stage", [P, STAGES, MOE_COLS])

    QUARTERS = 4
    with ExitStack() as s:
        def sem(name):
            return s.enter_context(nc.semaphore(name))

        kpad_zero, k_loaded, d_added, kpad_stored = map(sem, ("kpad_zero", "k_loaded", "d_added", "kpad_stored"))
        toeplitz_loaded = [sem(f"toeplitz_loaded{i}") for i in range(2)]
        x_loaded = [sem(f"x_loaded{i}") for i in range(QUARTERS)]
        ctx_loaded, consts, ident_zero = map(sem, ("ctx_loaded", "consts", "ident_zero"))
        stats_done, mv_done, rstd_half, rstd_done = map(sem, ("stats_done", "mv_done", "rstd_half", "rstd_done"))
        y_ready, q_transposed, q_copied = map(sem, ("y_ready", "q_transposed", "q_copied"))
        kv_ready, conv_done, prod_ready, reduced = map(sem, ("kv_ready", "conv_done", "prod_ready", "reduced"))
        hi_split, lo_split = sem("hi_split"), sem("lo_split")
        staged = [sem(f"staged{i}") for i in range(STAGES)]
        q_banks, conv_banks = banks[4:8], banks[0:4]
        wide = [P, CHUNK_B, HEAD_DIM, HEAD_DIM]
        block = s.enter_context(nc.Block())

        @block.sync
        def _(sp):
            for i in range(QUARTERS):
                sp.dma_start(x_sb[:, 4 * i:4 * i + 4, :], x_rows[:, 4 * i:4 * i + 4, :]).then_inc(x_loaded[i], 16)
            for h in range(HALVES):
                sp.dma_start(ctx_t[:, h, :], a["ctx_t"][h]).then_inc(ctx_loaded, 16)
            sp.wait_ge(kpad_stored, 16)
            for part in range(2):
                heads = slice(part * HEADS // 2, (part + 1) * HEADS // 2)
                sp.dma_start(toeplitz[:, heads, :], bass.AP(kpad_dram.tensor, part * HEADS // 2 * KPAD, [
                    [1, P], [KPAD, HEADS // 2], [1, 2 * P]])).then_inc(toeplitz_loaded[part], 16)
            for k, n in enumerate(W_ORDER[:SPLIT_EARLY]):
                if k >= STAGES:
                    sp.wait_ge(lo_split, k - STAGES + 1)
                sp.dma_start(stage[:, k % STAGES, :], a["moe_weights"][n]).then_inc(staged[k % STAGES], 16)

        @block.gpsimd
        def _(pool):
            nc.gpsimd.memset(kpad[:, :], 0.0).then_inc(kpad_zero, 1)
            nc.gpsimd.memset(ident[:, :], 0.0).then_inc(ident_zero, 1)
            nc.gpsimd.memset(minus_half[:, :], -0.5)
            pool.wait_ge(ident_zero, 1)
            nc.gpsimd.affine_select(out=ident[:, :], in_=ident[:, :], compare_op=ALU.not_equal, fill=1.0,
                                    base=0, pattern=[[-1, P]], channel_multiplier=1).then_inc(consts, 1)
            for i in range(QUARTERS):
                tiles = slice(4 * i, 4 * i + 4)
                pool.wait_ge(mv_done, i + 1)
                nc.gpsimd.tensor_scalar_add(rstd[:, tiles], meanvar[:, tiles, 1], EPS).then_inc(rstd_half, 1)
                pool.wait_ge(rstd_half, i + 1)
                nc.gpsimd.tensor_tensor(rstd[:, tiles], rstd[:, tiles], minus_half[:, tiles], ALU.pow)\
                  .then_inc(rstd_done, 1)
            pool.sem_inc(conv_done, CHUNKS)
            pool.wait_ge(ctx_loaded, 16 * HALVES)
            for h in range(HEADS):
                if h % 2:
                    k, n = h // 2, W_ORDER[h // 2]
                    pool.wait_ge(hi_split, k + 1)
                    nc.gpsimd.tensor_tensor(w_lo[:, n, :], stage[:, k % STAGES, :], w_hi[:, n, :].bitcast(FP32),
                                            ALU.subtract).then_inc(lo_split, 1)
                for c in range(CHUNKS):
                    pool.wait_ge(conv_done, CHUNKS * h + c + 1)
                    for m in range(HALVES):
                        feat = ctx_t[:, m, :].rearrange("p (b t) -> p b t", t=SEQ)[
                            :, c * CHUNK_B:(c + 1) * CHUNK_B, bass.ds(h * HEAD_DIM, HEAD_DIM)]
                        last = nc.gpsimd.tensor_tensor(
                            kv[:, c, m, :].rearrange("p (b j i) -> p b j i", j=HEAD_DIM, i=HEAD_DIM),
                            feat.unsqueeze(2).broadcast_to(wide), feat.unsqueeze(3).broadcast_to(wide), ALU.mult)
                    last.then_inc(kv_ready, 1)

        @block.scalar
        def _(act):
            act.wait_ge(kpad_zero, 1)
            act.dma_start(kpad[:, P - 1:P - 1 + DIM], a["ssm_kernel"]).then_inc(k_loaded, 16)
            act.dma_start(d_col[:, :], a["D"]).then_inc(k_loaded, 16)
            act.wait_ge(d_added, 1)
            act.dma_start(kpad_dram, kpad[:, :]).then_inc(kpad_stored, 16)
            for n in range(TILES // 2):
                act.wait_ge(q_transposed, n + 1)
                nc.scalar.copy(q_t[:, :, n * 2 * P:(n + 1) * 2 * P],
                               q_banks[n % 4][:, :].rearrange("p (c t) -> p c t", c=HALVES)).then_inc(q_copied, 1)
            for k, n in enumerate(W_ORDER[:SPLIT_EARLY]):
                act.wait_ge(staged[k % STAGES], 16 * (k // STAGES + 1))
                nc.scalar.copy(w_hi[:, n, :], stage[:, k % STAGES, :]).then_inc(hi_split, 1)

        @block.tensor
        def _(pe):
            pe.wait_ge(consts, 1)
            for n in range(TILES // 2):
                pe.wait_ge(y_ready, n + 1)
                if n >= 4:
                    pe.wait_ge(q_copied, n - 3)
                for c in range(HALVES):
                    for k in range(2):
                        last = nc.tensor.transpose(q_banks[n % 4][:, (2 * c + k) * P:(2 * c + k + 1) * P],
                                                   y[:, (2 * n + k) % 4, c * P:(c + 1) * P], ident[:, :])
                last.then_inc(q_transposed, 1)
            for h in range(HEADS):
                if h % (HEADS // 2) == 0:
                    pe.wait_ge(toeplitz_loaded[h // (HEADS // 2)], 16)
                for c in range(CHUNKS):
                    n = CHUNKS * h + c
                    pe.wait_ge(kv_ready, n + 1)
                    if h >= 1:
                        pe.wait_ge(prod_ready, HALVES * (n - CHUNKS + 1))
                    same, across = toeplitz[:, h, 0:P], toeplitz[:, h, P:2 * P]
                    nc.tensor.matmul(conv_banks[2 * c][:, :], same, kv[:, c, 0, :], start=True, stop=True)
                    nc.tensor.matmul(conv_banks[2 * c + 1][:, :], across, kv[:, c, 0, :], start=True, stop=False)
                    nc.tensor.matmul(conv_banks[2 * c + 1][:, :], same, kv[:, c, 1, :], start=False,
                                     stop=True).then_inc(conv_done, 1)

        @block.vector
        def _(dve):
            dve.wait_ge(k_loaded, 32)
            nc.vector.tensor_tensor(kpad[:, P - 1:P], kpad[:, P - 1:P], d_col[:, :], ALU.add).then_inc(d_added, 1)
            for i in range(QUARTERS + 1):
                if i < QUARTERS:
                    dve.wait_ge(x_loaded[i], 16)
                    for t in range(4 * i, 4 * i + 4):
                        nc.vector.bn_stats(stats[:, t, :], x_sb[:, t, :]).then_inc(stats_done, 1)
                    for t in range(4 * i, 4 * i + 4):
                        dve.wait_ge(stats_done, t + 1)
                        last = nc.vector.bn_aggr(meanvar[:, t, :], stats[:, t, :])
                    last.then_inc(mv_done, 1)
                if i >= 1:
                    dve.wait_ge(rstd_done, i)
                    for t in range(4 * i - 4, 4 * i):
                        if t >= 4 and t % 2 == 0:
                            dve.wait_ge(q_transposed, t // 2 - 1)
                        last = nc.vector.tensor_scalar(y[:, t % 4, :], x_sb[:, t, :], meanvar[:, t, 0:1],
                                                       rstd[:, t:t + 1], ALU.subtract, ALU.mult)
                        if t % 2:
                            last.then_inc(y_ready, 1)
            dve.wait_ge(q_copied, TILES // 2)
            for n in range(HEADS * CHUNKS):
                h, c = n // CHUNKS, n % CHUNKS
                dve.wait_ge(conv_done, CHUNKS + n + 1)
                query = [q_t[:, m, :].rearrange("p (b t) -> p b t", t=SEQ)[
                    :, c * CHUNK_B:(c + 1) * CHUNK_B, h * HEAD_DIM:(h + 1) * HEAD_DIM] for m in range(HALVES)]
                for m in range(HALVES):
                    if n >= 1:
                        dve.wait_ge(reduced, HALVES * (n - 1) + m + 1)
                    nc.vector.tensor_tensor(
                        prod[:, m, :].rearrange("p (b j i) -> p b j i", j=HEAD_DIM, i=HEAD_DIM),
                        conv_banks[2 * c + m][:, :].rearrange("p (b j i) -> p b j i", j=HEAD_DIM, i=HEAD_DIM),
                        query[m].unsqueeze(2).broadcast_to(wide), ALU.mult).then_inc(prod_ready, 1)
                for m in range(HALVES):
                    dve.wait_ge(prod_ready, HALVES * n + m + 1)
                    nc.vector.reduce_sum(query[m], prod[:, m, :].rearrange(
                        "p (b j i) -> p b j i", j=HEAD_DIM, i=HEAD_DIM), axis=AX.X).then_inc(reduced, 1)


def split_products(hi_lo_a, hi_lo_b):
    (a_hi, a_lo), (b_hi, b_lo) = hi_lo_a, hi_lo_b
    return ((a_hi, b_hi), (a_hi, b_lo), (a_lo, b_hi))


def conv_end_phase(nc, memory, a, ident, x_sb, norm, q_t, x_hi, x_lo, banks):
    stats, meanvar, rstd, minus_half = norm

    def sb(name, shape, dt=FP32):
        return memory.enter_context(nc.sbuf_tensor(name, shape, dt))

    gate_sb = sb("moe_gate", [P, HALVES, EXPERTS])
    y, x_t = sb("moe_y", [P, 4, DIM]), sb("moe_x_t", [P, 2, HALVES, 2 * P])
    back_banks, turn_banks, logit_bank = banks[0:4], banks[4:6], banks[7]
    PAIRS_T = TILES // 2
    with ExitStack() as s:
        def sem(name):
            return s.enter_context(nc.semaphore(name))

        att_turned, x_added, stats_done, mv_done, rstd_half, rstd_done, gate_loaded = map(sem, (
            "att_turned", "x_added", "stats_done", "mv_done", "rstd_half", "rstd_done", "gate_loaded"))
        y_ready, turned, xt_copied, hi_done, lo_done, logits_done = map(
            sem, ("y_ready", "turned", "xt_copied", "hi_done", "lo_done", "logits_done"))
        block = s.enter_context(nc.Block())

        @block.sync
        def _(sp):
            sp.dma_start(gate_sb[:, :, :], a["moe_gate"]).then_inc(gate_loaded, 16)

        @block.vector
        def _(dve):
            for i in range(PAIRS_T + 1):
                if i < PAIRS_T:
                    tiles = slice(2 * i, 2 * i + 2)
                    dve.wait_ge(att_turned, i + 1)
                    nc.vector.tensor_tensor(x_sb[:, tiles, :], x_sb[:, tiles, :],
                                            back_banks[i % 4][:, :].rearrange("p (t d) -> p t d", t=2),
                                            ALU.add).then_inc(x_added, 1)
                    dve.wait_ge(x_added, i + 1)
                    for t in (2 * i, 2 * i + 1):
                        last = nc.vector.bn_stats(stats[:, t, :], x_sb[:, t, :])
                    last.then_inc(stats_done, 1)
                if i >= 1:
                    n = i - 1
                    dve.wait_ge(rstd_done, n + 1)
                    if n >= 2:
                        dve.wait_ge(turned, n - 1)
                    for t in (2 * n, 2 * n + 1):
                        last = nc.vector.tensor_scalar(y[:, t % 4, :], x_sb[:, t, :], meanvar[:, t, 0:1],
                                                       rstd[:, t:t + 1], ALU.subtract, ALU.mult)
                    last.then_inc(y_ready, 1)
                if i < PAIRS_T:
                    dve.wait_ge(stats_done, i + 1)
                    for t in (2 * i, 2 * i + 1):
                        last = nc.vector.bn_aggr(meanvar[:, t, :], stats[:, t, :])
                    last.then_inc(mv_done, 1)

        @block.gpsimd
        def _(pool):
            for i in range(PAIRS_T + 2):
                if i < PAIRS_T:
                    tiles = slice(2 * i, 2 * i + 2)
                    pool.wait_ge(mv_done, i + 1)
                    nc.gpsimd.tensor_scalar_add(rstd[:, tiles], meanvar[:, tiles, 1], EPS).then_inc(rstd_half, 1)
                    pool.wait_ge(rstd_half, i + 1)
                    nc.gpsimd.tensor_tensor(rstd[:, tiles], rstd[:, tiles], minus_half[:, tiles],
                                            ALU.pow).then_inc(rstd_done, 1)
                if i >= 2:
                    n = i - 2
                    pool.wait_ge(hi_done, n + 1)
                    cols = slice(2 * P * n, 2 * P * (n + 1))
                    nc.gpsimd.tensor_tensor(x_lo[:, :, cols], x_t[:, n % 2, :, :], x_hi[:, :, cols].bitcast(FP32),
                                            ALU.subtract).then_inc(lo_done, 1)

        @block.scalar
        def _(act):
            for n in range(PAIRS_T):
                act.wait_ge(turned, n + 1)
                if n >= 2:
                    act.wait_ge(lo_done, n - 1)
                    act.wait_ge(logits_done, n - 1)
                nc.scalar.copy(x_t[:, n % 2, :, :], turn_banks[n % 2][:, :].rearrange(
                    "p (c t) -> p c t", c=HALVES)).then_inc(xt_copied, 1)
                act.wait_ge(xt_copied, n + 1)
                nc.scalar.copy(x_hi[:, :, 2 * P * n:2 * P * (n + 1)], x_t[:, n % 2, :, :]).then_inc(hi_done, 1)

        @block.tensor
        def _(pe):
            def attention_back(n):
                if n >= 4:
                    pe.wait_ge(x_added, n - 3)
                for k in range(2):
                    for c in range(HALVES):
                        last = nc.tensor.transpose(back_banks[n % 4][:, (2 * k + c) * P:(2 * k + c + 1) * P],
                                                   q_t[:, c, (2 * n + k) * P:(2 * n + k + 1) * P], ident[:, :])
                last.then_inc(att_turned, 1)

            attention_back(0)
            attention_back(1)
            for i in range(PAIRS_T + 2):
                if i + 2 < PAIRS_T:
                    attention_back(i + 2)
                if 1 <= i <= PAIRS_T:
                    n = i - 1
                    pe.wait_ge(y_ready, n + 1)
                    if n >= 2:
                        pe.wait_ge(xt_copied, n - 1)
                    for c in range(HALVES):
                        for k in range(2):
                            last = nc.tensor.transpose(turn_banks[n % 2][:, (2 * c + k) * P:(2 * c + k + 1) * P],
                                                       y[:, (2 * n + k) % 4, c * P:(c + 1) * P], ident[:, :])
                    last.then_inc(turned, 1)
                if i >= 2:
                    n = i - 2
                    if n == 0:
                        pe.wait_ge(gate_loaded, 16)
                    pe.wait_ge(xt_copied, n + 1)
                    for k in range(2):
                        t = 2 * n + k
                        for c in range(HALVES):
                            last = nc.tensor.matmul(logit_bank[:, t * EXPERTS:(t + 1) * EXPERTS],
                                                    x_t[:, n % 2, c, k * P:(k + 1) * P], gate_sb[:, c, :],
                                                    start=(c == 0), stop=(c == HALVES - 1))
                    last.then_inc(logits_done, 1)


def pick_first_max(dve_step, nc, values, shape, order, scratch):
    top, hit, top_hit = scratch
    top_wide, top_hit_wide = top.unsqueeze(2).broadcast_to(shape), top_hit.unsqueeze(2).broadcast_to(shape)
    dve_step(nc.vector.reduce_max(top, values, axis=AX.X))
    dve_step(nc.vector.tensor_tensor(hit, values, top_wide, ALU.is_equal))
    dve_step(nc.vector.tensor_tensor(hit, hit, order, ALU.mult))
    dve_step(nc.vector.reduce_max(top_hit, hit, axis=AX.X))
    dve_step(nc.vector.tensor_tensor(hit, hit, top_hit_wide, ALU.is_equal))
    dve_step(nc.vector.scalar_tensor_tensor(values, hit, -BIG, values, ALU.mult, ALU.add))
    return hit


def attention_rstd(nc, norm, tiles, step):
    meanvar, rstd, minus_half = norm[1:]
    nc.gpsimd.tensor_scalar_add(rstd[:, tiles], meanvar[:, tiles, 1], EPS).then_inc(step, 1)
    nc.gpsimd.wait_ge(step, 1)
    nc.gpsimd.tensor_tensor(rstd[:, tiles], rstd[:, tiles], minus_half[:, tiles], ALU.pow).then_inc(step, 1)
    nc.gpsimd.wait_ge(step, 2)
    nc.gpsimd.tensor_scalar_mul(rstd[:, tiles], rstd[:, tiles], SOFTMAX_SCALE).then_inc(step, 1)


def moe_phase(nc, memory, a, w_dram, ident, x_sb, norm, x_hi, x_lo, w_hi, w_lo, ctx_ring, banks):
    stats, meanvar, rstd, minus_half = norm

    def sb(name, shape, dt=FP32):
        return memory.enter_context(nc.sbuf_tensor(name, shape, dt))

    T, E, G, PER = TILES, EXPERTS, GROUPS, EXPERTS // GROUPS
    scores, weights = sb("scores", [P, T, E]), sb("router_weights", [P, T, E])
    choice, rest = sb("choice", [P, T, E + SENTINELS]), sb("rest", [P, T, E + SENTINELS])
    bias_sb, order, best = sb("bias_sb", [P, E]), sb("order", [P, G]), sb("best", [P, T, 8])
    pair_hi, pair_lo = sb("pair_hi", [P, T * G, 2]), sb("pair_lo", [P, T * G, 2])
    g_top, g_second, g_score, g_hit, g_mask, g_pen = (sb(n, [P, T, G]) for n in (
        "g_top", "g_second", "g_score", "g_hit", "g_mask", "g_pen"))
    top, top_hit, w_sum = (sb(n, [P, T]) for n in ("top", "top_hit", "w_sum"))
    w_t = sb("w_t", [P, 2, P])
    stage = sb("late_stage", [P, LATE_STAGES, MOE_COLS])
    late = W_ORDER[SPLIT_EARLY:]
    w_ring = sb("w_ring", [P, W_SLOTS, GROUP_T])
    silu, prod, act = (sb(n, [P, 2, GROUP_T]) for n in ("moe_silu", "moe_prod", "moe_act"))
    act_hi, act_lo = (sb(n, [P, 2, GROUP_T], F32R) for n in ("moe_act_hi", "moe_act_lo"))
    gate_banks, up_banks, out_banks, shared_banks = banks[0:2], banks[2:4], banks[4:6], (banks[4:6], banks[6:8])
    router_bank = banks[6]
    with ExitStack() as s:
        def sem(name):
            return s.enter_context(nc.semaphore(name))

        bias_loaded, order_done, sigmoid_done, step, w_transposed, w_copied, w_stored = map(sem, (
            "bias_loaded", "order_done", "sigmoid_done", "step", "w_transposed", "w_copied", "w_stored"))
        w_loaded = [sem(f"w_loaded{i}") for i in range(W_SLOTS)]
        gu_done, silu_done, prod_done, act_ready, hi_done, lo_done, down_done, x_added = map(sem, (
            "gu_done", "silu_done", "prod_done", "act_ready", "hi_done", "lo_done", "down_done", "x_added"))
        shared_lo, hi_split, lo_split = map(sem, ("shared_lo_done", "hi_split", "lo_split"))
        staged = [sem(f"staged{i}") for i in range(LATE_STAGES)]
        stats_done, mv_done, rstd_step, ctx_loaded = map(sem, ("stats_done", "mv_done", "rstd_step", "ctx_loaded"))
        block = s.enter_context(nc.Block())

        def late_splits(m):
            return range(m * len(late) // SHARED_STEPS, (m + 1) * len(late) // SHARED_STEPS)

        def step_of(g, n):
            return SHARED_STEPS + g * EXPERTS + n

        @block.sync
        def _(sp):
            sp.sem_inc(act_ready, W_SLOTS)
            sp.dma_start(bias_sb[:, :], a["moe_bias"].partition_broadcast(P)).then_inc(bias_loaded, 16)
            for k, n in enumerate(late):
                if k >= LATE_STAGES:
                    sp.wait_ge(lo_split, k - LATE_STAGES + 1)
                sp.dma_start(stage[:, k % LATE_STAGES, :], a["moe_weights"][n]).then_inc(staged[k % LATE_STAGES], 16)
            for half in range(2):
                sp.wait_ge(w_copied, half + 1)
                sp.dma_start(w_dram.rearrange("e (t k) -> t e k", k=P)[half * 8:half * 8 + 8], w_t[:, half, :])\
                  .then_inc(w_stored, 16)
            sp.wait_ge(w_stored, 32)
            with sp.Fori(0, TOKEN_GROUPS) as g:
                for e in range(EXPERTS):
                    sp.wait_ge(act_ready, g * EXPERTS + e + 1)
                    sp.dma_start(w_ring[:, e % W_SLOTS, :],
                                 w_dram[e, bass.ds(g * GROUP_T, GROUP_T)].partition_broadcast(P))\
                      .then_inc(w_loaded[e % W_SLOTS], 16)
            for b in range(CTX_SLOTS):
                load_ctx(sp, a, ctx_ring, b, ctx_loaded)
            sp.wait_ge(ctx_loaded, 32 * CTX_SLOTS)

        @block.tensor
        def _(pe):
            def gate_up(F, n, token):
                for bank, off in ((gate_banks[n % 2], 0), (up_banks[n % 2], HALVES * P)):
                    last = None
                    for c in range(HALVES):
                        cols = slice(off + c * P, off + (c + 1) * P)
                        w = w_hi[:, n, cols], w_lo[:, n, cols]
                        x = (x_hi[:, c, bass.ds(token, GROUP_T)], x_lo[:, c, bass.ds(token, GROUP_T)])
                        for k, (wp, xp) in enumerate(split_products(w, x)):
                            last = nc.tensor.matmul(bank[:, :], wp, xp, start=(c == 0 and k == 0),
                                                    stop=(c == HALVES - 1 and k == 2))
                last.then_inc(gu_done, 1)

            def expert_gate_up(g, n):
                pe.wait_ge(prod_done, step_of(g, n) - 1)
                if n >= SPLIT_EARLY - SHARED_BLOCKS:
                    pe.wait_ge(lo_split, n + 1 - (SPLIT_EARLY - SHARED_BLOCKS))
                gate_up(step_of(g, n), n, g * GROUP_T)

            def down(n, into, first, last_one):
                for t in range(GROUP_T // P):
                    rows = slice(t * P, (t + 1) * P)
                    act_parts = act_hi[:, n % 2, rows], act_lo[:, n % 2, rows]
                    w = w_hi[:, n, 2 * DIM:3 * DIM], w_lo[:, n, 2 * DIM:3 * DIM]
                    for k, (ap, wp) in enumerate(split_products(act_parts, w)):
                        last = nc.tensor.matmul(into[t // 2][:, (t % 2) * DIM:(t % 2 + 1) * DIM], ap, wp,
                                                start=(first and k == 0 and t % 2 == 0),
                                                stop=(last_one and k == 2), skip_group_check=True)
                last.then_inc(down_done, 1)

            def expert_down(g, n):
                pe.wait_ge(lo_done, g * EXPERTS + n + 3)
                if n == 0:
                    pe.wait_ge(x_added, 2 * g + 2 * TOKEN_GROUPS)
                down(n, out_banks, n == 0, n == EXPERTS - 1)

            def shared_gate_up(m):
                if m >= 2:
                    pe.wait_ge(prod_done, m - 1)
                gate_up(m, EXPERTS + m % SHARED_BLOCKS, m // SHARED_BLOCKS * GROUP_T)

            def group(g, last_group):
                for n in range(LAG, EXPERTS):
                    expert_gate_up(g, n)
                    expert_down(g, n - LAG)
                for n in range(LAG):
                    if not last_group:
                        expert_gate_up(g + 1, n)
                    expert_down(g, EXPERTS - LAG + n)

            for m in range(LAG):
                shared_gate_up(m)
            for m in range(SHARED_STEPS):
                if m + LAG < SHARED_STEPS:
                    shared_gate_up(m + LAG)
                else:
                    expert_gate_up(0, m + LAG - SHARED_STEPS)
                g, n = m // SHARED_BLOCKS, m % SHARED_BLOCKS
                pe.wait_ge(shared_lo, m + 1)
                if n == 0 and g == 1:
                    pe.wait_ge(sigmoid_done, 1)
                if n == 0 and g >= 2:
                    pe.wait_ge(x_added, 2 * (g - 1))
                if m == SHARED_STEPS - SHARED_BLOCKS:
                    pe.wait_ge(step, STEPS)
                    for half in range(2):
                        last = nc.tensor.transpose(router_bank[:, half * P:(half + 1) * P],
                                                   weights[:, half * 8:half * 8 + 8, :], ident[:, :])
                    last.then_inc(w_transposed, 1)
                    pe.wait_ge(w_copied, 2)
                down(EXPERTS + n, shared_banks[g % 2], n == 0, n == SHARED_BLOCKS - 1)
            with pe.Fori(0, TOKEN_GROUPS - 1) as g:
                group(g, False)
            group(TOKEN_GROUPS - 1, True)

        @block.scalar
        def _(act_eng):
            def silu_of(F, n):
                act_eng.wait_ge(gu_done, F + 1)
                nc.scalar.activation(silu[:, n % 2, :], gate_banks[n % 2][:, :], ACT.Silu).then_inc(silu_done, 1)

            def high_part(F, n):
                nc.scalar.copy(act_hi[:, n % 2, :], act[:, n % 2, :]).then_inc(hi_done, 1)

            def expert_high_part(g, n):
                act_eng.wait_ge(act_ready, g * EXPERTS + n + 1 + W_SLOTS)
                act_eng.wait_ge(down_done, step_of(g, n) - 1)
                high_part(step_of(g, n), n)

            def shared_high_part(m):
                act_eng.wait_ge(prod_done, m + 1)
                if m >= 2:
                    act_eng.wait_ge(down_done, m - 1)
                high_part(m, m)

            def group(g, last_group):
                for n in range(LAG, EXPERTS):
                    silu_of(step_of(g, n), n)
                    expert_high_part(g, n - 1)
                if not last_group:
                    silu_of(step_of(g + 1, 0), 0)
                expert_high_part(g, EXPERTS - 1)
                if not last_group:
                    silu_of(step_of(g + 1, 1), 1)
                    expert_high_part(g + 1, 0)

            nc.scalar.activation(scores[:, :, :], banks[7][:, 0:T * E].rearrange("p (t e) -> p t e", e=E),
                                 ACT.Sigmoid).then_inc(sigmoid_done, 1)
            silu_of(0, 0)
            for m in range(SHARED_STEPS):
                silu_of(m + 1, m + 1)
                shared_high_part(m)
                for k in late_splits(m):
                    act_eng.wait_ge(staged[k % LATE_STAGES], 16 * (k // LATE_STAGES + 1))
                    nc.scalar.copy(w_hi[:, late[k], :], stage[:, k % LATE_STAGES, :]).then_inc(hi_split, 1)
                if m == SHARED_STEPS - SHARED_BLOCKS:
                    act_eng.wait_ge(w_transposed, 1)
                    for half in range(2):
                        nc.scalar.copy(w_t[:, half, :], router_bank[:, half * P:(half + 1) * P]).then_inc(w_copied, 1)
            silu_of(step_of(0, 1), 1)
            expert_high_part(0, 0)
            with act_eng.Fori(0, TOKEN_GROUPS - 1) as g:
                group(g, False)
            group(TOKEN_GROUPS - 1, True)

        @block.gpsimd
        def _(pool):
            nc.gpsimd.iota(order[:, :], pattern=[[-1, G]], base=G, channel_multiplier=0,
                           allow_small_or_imprecise_dtypes=True)
            nc.gpsimd.memset(choice[:, :, E:], 2 * BIG).then_inc(order_done, 1)
            for m in range(SHARED_STEPS):
                pool.wait_ge(hi_done, m + 1)
                if m >= 2:
                    pool.wait_ge(down_done, m - 1)
                nc.gpsimd.tensor_tensor(act_lo[:, m % 2, :], act[:, m % 2, :], act_hi[:, m % 2, :].bitcast(FP32),
                                        ALU.subtract).then_inc(shared_lo, 1)
                for k in late_splits(m):
                    pool.wait_ge(hi_split, k + 1)
                    n = late[k]
                    nc.gpsimd.tensor_tensor(w_lo[:, n, :], stage[:, k % LATE_STAGES, :], w_hi[:, n, :].bitcast(FP32),
                                            ALU.subtract).then_inc(lo_split, 1)
            pool.wait_ge(shared_lo, SHARED_STEPS)
            pool.sem_inc(lo_done, 2)
            with pool.Fori(0, TOKEN_GROUPS) as g:
                for e in range(EXPERTS):
                    pool.wait_ge(w_loaded[e % W_SLOTS], 16 * (g * (EXPERTS // W_SLOTS) + e // W_SLOTS + 1))
                    pool.wait_ge(prod_done, step_of(g, e) + 1)
                    pool.wait_ge(lo_done, g * EXPERTS + e + 1)
                    nc.gpsimd.tensor_tensor(act[:, e % 2, :], prod[:, e % 2, :], w_ring[:, e % W_SLOTS, :],
                                            ALU.mult).then_inc(act_ready, 1)
            pool.wait_ge(mv_done, EARLY_NORM)
            attention_rstd(nc, norm, slice(0, EARLY_NORM), rstd_step)

        @block.vector
        def _(dve):
            steps = [0]

            def dve_step(ins):
                steps[0] += 1
                ins.then_inc(step, 1)
                dve.wait_ge(step, steps[0])

            flat_top, flat_second, flat_score, flat_pen = (
                v[:, :, :].rearrange("p t g -> p (t g)") for v in (g_top, g_second, g_score, g_pen))
            wide_g, wide_e = [P, T, G], [P, T, E]

            def group_scores():
                dve.wait_ge(sigmoid_done, 1)
                dve.wait_ge(bias_loaded, 16)
                dve.wait_ge(order_done, 1)
                dve_step(nc.vector.tensor_tensor(choice[:, :, 0:E], scores[:, :, :],
                                                 bias_sb[:, :].unsqueeze(1).broadcast_to([P, T, E]), ALU.add))
                for half in range(2):
                    pairs = [choice[:, :, 0:E].rearrange("p t (g q r) -> p t g q r", g=G, r=2)[:, :, :, half, r]
                             for r in range(2)]
                    into = [v[:, :, half].rearrange("p (t g) -> p t g", g=G) for v in (pair_hi, pair_lo)]
                    nc.vector.tensor_tensor(into[0], pairs[0], pairs[1], ALU.max)
                    last = nc.vector.tensor_tensor(into[1], pairs[0], pairs[1], ALU.min)
                dve_step(last)
                nc.vector.tensor_tensor(flat_top, pair_hi[:, :, 0], pair_hi[:, :, 1], ALU.max)
                nc.vector.tensor_tensor(flat_second, pair_hi[:, :, 0], pair_hi[:, :, 1], ALU.min)
                dve_step(nc.vector.tensor_tensor(flat_pen, pair_lo[:, :, 0], pair_lo[:, :, 1], ALU.max))
                dve_step(nc.vector.tensor_tensor(flat_second, flat_second, flat_pen, ALU.max))
                dve_step(nc.vector.tensor_tensor(flat_score, flat_top, flat_second, ALU.add))

            def pick_group(n):
                hit = pick_first_max(dve_step, nc, g_score[:, :, :], wide_g,
                                     order[:, :].unsqueeze(1).broadcast_to(wide_g),
                                     (top[:, :], g_hit[:, :, :], top_hit[:, :]))
                if n == 0:
                    dve_step(nc.vector.tensor_copy(g_mask[:, :, :], hit))
                else:
                    dve_step(nc.vector.tensor_tensor(g_mask[:, :, :], g_mask[:, :, :], hit, ALU.add))

            def drop_groups():
                dve_step(nc.vector.tensor_scalar(g_pen[:, :, :], g_mask[:, :, :], BIG, -BIG, ALU.mult, ALU.add))
                for per_group, op in ((g_mask, ALU.mult), (g_pen, ALU.add)):
                    for g in range(G):
                        of_group = choice[:, :, g * PER:(g + 1) * PER]
                        last = nc.vector.tensor_tensor(
                            of_group, of_group, per_group[:, :, g:g + 1].broadcast_to([P, T, PER]), op)
                    dve_step(last)

            def best_experts():
                for t in range(T):
                    last = nc.vector.max(best[:, t, :], choice[:, t, :])
                dve_step(last)

            def take_out():
                for t in range(T):
                    last = nc.vector.match_replace(rest[:, t, :], best[:, t, :], choice[:, t, :], -3 * BIG)
                dve_step(last)

            def expert_weights():
                dve_step(nc.vector.scalar_tensor_tensor(weights[:, :, :], rest[:, :, 0:E], -2 * BIG, scores[:, :, :],
                                                        ALU.is_lt, ALU.mult))
                dve_step(nc.vector.reduce_sum(w_sum[:, :], weights[:, :, :], axis=AX.X))
                dve_step(nc.vector.tensor_scalar_add(w_sum[:, :], w_sum[:, :], 1e-20))
                dve_step(nc.vector.reciprocal(w_sum[:, :], w_sum[:, :]))
                dve_step(nc.vector.tensor_scalar_mul(w_sum[:, :], w_sum[:, :], ROUTED_SCALE))
                dve_step(nc.vector.tensor_tensor(weights[:, :, :], weights[:, :, :],
                                                 w_sum[:, :].unsqueeze(2).broadcast_to(wide_e), ALU.mult))

            def product(F, n, into):
                dve.wait_ge(silu_done, F + 1)
                nc.vector.tensor_tensor(into[:, n % 2, :], silu[:, n % 2, :], up_banks[n % 2][:, :],
                                        ALU.mult).then_inc(prod_done, 1)

            def shared_product(m):
                if m >= 2:
                    dve.wait_ge(shared_lo, m - 1)
                product(m, m, act)

            def expert_product(g, n):
                dve.wait_ge(act_ready, g * EXPERTS + n - 1 + W_SLOTS)
                product(step_of(g, n), n, prod)

            def low_part(g, n):
                dve.wait_ge(hi_done, step_of(g, n) + 1)
                nc.vector.tensor_tensor(act_lo[:, n % 2, :], act[:, n % 2, :], act_hi[:, n % 2, :].bitcast(FP32),
                                        ALU.subtract).then_inc(lo_done, 1)

            def add_to_x(g, from_banks, down_steps):
                dve.wait_ge(down_done, down_steps)
                for o in range(2):
                    rows = x_sb[:, bass.ds(g * 4 + 2 * o, 2), :]
                    nc.vector.tensor_tensor(rows, rows, from_banks[o][:, :].rearrange("p (t d) -> p t d", t=2),
                                            ALU.add).then_inc(x_added, 1)

            def add_experts_to_x(g):
                add_to_x(g, out_banks, step_of(g, EXPERTS))
                for k in range(4):
                    if k % 2 == 0:
                        dve.wait_ge(x_added, 2 * TOKEN_GROUPS + 2 * g + 1 + k // 2)
                    nc.vector.bn_stats(stats[:, bass.ds(g * 4 + k, 1), :].rearrange("p o s -> p (o s)"),
                                       x_sb[:, bass.ds(g * 4 + k, 1), :].rearrange("p o d -> p (o d)"))\
                      .then_inc(stats_done, 1)

            def group(g, last_group):
                for n in range(LAG, EXPERTS):
                    expert_product(g, n)
                    low_part(g, n - 1)
                if not last_group:
                    expert_product(g + 1, 0)
                low_part(g, EXPERTS - 1)
                if not last_group:
                    expert_product(g + 1, 1)
                    low_part(g + 1, 0)
                else:
                    for t in range(EARLY_NORM):
                        dve.wait_ge(stats_done, t + 1)
                        nc.vector.bn_aggr(meanvar[:, t, :], stats[:, t, :]).then_inc(mv_done, 1)
                add_experts_to_x(g)

            group_scores()
            shared_product(0)
            pick_group(0)
            shared_product(1)
            pick_group(1)
            drop_groups()
            shared_product(2)
            best_experts()
            take_out()
            shared_product(3)
            add_to_x(0, shared_banks[0], SHARED_BLOCKS)
            expert_weights()
            assert steps[0] == STEPS, steps
            for m in range(4, SHARED_STEPS + 1):
                if m < SHARED_STEPS:
                    shared_product(m)
                else:
                    expert_product(0, 0)
                if m % 2 == 1:
                    g = (m - 3) // 2
                    add_to_x(g, shared_banks[g % 2], SHARED_BLOCKS * (g + 1))
            expert_product(0, 1)
            add_to_x(TOKEN_GROUPS - 1, shared_banks[1], SHARED_STEPS)
            low_part(0, 0)
            with dve.Fori(0, TOKEN_GROUPS - 1) as g:
                group(g, False)
            group(TOKEN_GROUPS - 1, True)


def load_ctx(sp, a, ctx_ring, b, loaded):
    sp.dma_start(ctx_ring[:, b % CTX_SLOTS, 0:DIM], a["ctx_keys"][b * SEQ:(b + 1) * SEQ, :]).then_inc(loaded, 16)
    sp.dma_start(ctx_ring[:, b % CTX_SLOTS, DIM:].rearrange("p (m t) -> p m t", m=HALVES), a["ctx_t"].rearrange("m p t -> p m t")[
        :, :, b * SEQ:(b + 1) * SEQ]).then_inc(loaded, 16)


def softmax_phase(nc, memory, a, mask_dram, rw_dram, x_dram, ident, x_sb, norm, w_hi, w_lo, x_hi, x_lo, masks_sb,
                  ctx_ring, banks):
    stats, meanvar, rstd, minus_half = norm

    def sb(name, shape, dt=FP32):
        return memory.enter_context(nc.sbuf_tensor(name, shape, dt))

    W_SLOTS_L, W_COLS = 4, LORA_COLS // 2
    LAST = BATCH + 7
    T, E, HT = TILES, LORA_EXPERTS, TILES // 2
    stage = sb("lora_stage", [P, W_SLOTS_L, W_COLS])
    y, weights, scaled = sb("att_y", [P, 2, DIM]), sb("att_weights", [P, 3, HALVES, DIM]), sb("att_scaled", [P, 2, DIM])
    minus_top, total, inverse = (sb(n, [P, BATCH, HALVES]) for n in ("att_minus_top", "att_total", "att_inverse"))
    gate_sb = sb("lora_gate", [P, HALVES, E])
    stats2, meanvar2, rstd2 = sb("stats2", [P, T, 6]), sb("meanvar2", [P, T, 2]), sb("rstd2", [P, T])
    z, x_t = sb("lora_y", [P, 2, DIM]), sb("lora_x_t", [P, 2, HALVES, P])
    probs, order, hit = sb("probs", [P, HT, E]), sb("lora_order", [P, E]), sb("lora_hit", [P, HT, E])
    masks, rw = sb("picked_masks", [P, HT, PICKS, E]), sb("rw", [P, HT, PICKS])
    top, top_hit, prob_sum = sb("picked_top", [P, PICKS, HT]), sb("lora_top_hit", [P, HT]), sb("lora_total", [P, HT])
    masks_t, rw_t = sb("masks_t", [P, P], BF16), sb("rw_t", [HT * PICKS, P])
    score_banks, out_banks, turn_banks, logit_banks = banks[0:2], banks[2:4], banks[4:6], banks[6:8]
    router_bank = logit_banks[0]
    with ExitStack() as s:
        def sem(name):
            return s.enter_context(nc.semaphore(name))

        ctx_loaded = [sem(f"ctx_loaded{i}") for i in range(CTX_SLOTS)]
        staged = [sem(f"lora_staged{i}") for i in range(W_SLOTS_L)]
        hi_split, lo_split_pool, lo_split_dve = map(sem, ("lora_hi_split", "lora_lo_split_pool", "lora_lo_split_dve"))
        y_ready, scores_done, top_done, exp_done, inverse_done, scaled_done, out_done, x_added = map(sem, (
            "y_ready", "scores_done", "top_done", "exp_done", "inverse_done", "scaled_done", "out_done", "x_added"))
        stats_done, mv_done, eps_added, rstd_done, z_ready, turned, xt_copied, x_hi_done, x_lo_done, logits_done = map(
            sem, ("stats_done", "mv_done", "eps_added", "rstd_done", "z_ready", "turned", "xt_copied", "x_hi_done",
                  "x_lo_done", "logits_done"))
        gate_loaded, order_done, exp_ready, probs_exp, step, picks_turned, picks_copied, picks_stored = map(sem, (
            "gate_loaded", "order_done", "exp_ready", "probs_exp", "step", "picks_turned", "picks_copied",
            "picks_stored"))
        x_stored, masks_loaded, late_mv, late_rstd = map(sem, ("x_stored", "masks_loaded", "late_mv", "late_rstd"))
        block = s.enter_context(nc.Block())

        def wait_lo_split(engine, k):
            if k % W_SLOTS_L == W_SLOTS_L - 1:
                engine.wait_ge(lo_split_dve, k // W_SLOTS_L + 1)
            else:
                engine.wait_ge(lo_split_pool, k // W_SLOTS_L * (W_SLOTS_L - 1) + k % W_SLOTS_L + 1)

        def low_weights(engine, ops, k, done):
            engine.wait_ge(hi_split, k + 1)
            cols = slice((k % 2) * W_COLS, (k % 2 + 1) * W_COLS)
            ops.tensor_tensor(w_lo[:, k // 2, cols], stage[:, k % W_SLOTS_L, :], w_hi[:, k // 2, cols].bitcast(FP32),
                              ALU.subtract).then_inc(done, 1)

        @block.sync
        def _(sp):
            def load_picks_masks(half):
                sp.wait_ge(picks_copied, 2 * half + 1)
                sp.dma_start(mask_dram.rearrange("e (t k) -> t e k", k=P)[half * HT:(half + 1) * HT], masks_t[:, :])\
                  .then_inc(picks_stored, 16)
                sp.wait_ge(picks_copied, 2 * half + 2)
                sp.dma_start(rw_dram.rearrange("e (t k) -> t e k", k=P)[half * HT:(half + 1) * HT], rw_t[:, :])\
                  .then_inc(picks_stored, 16)
                sp.wait_ge(picks_stored, 32 * (half + 1))

            def store_x(n):
                tiles = slice(4 * n, 4 * n + 4)
                sp.wait_ge(x_added, 4 * n + 4)
                sp.dma_start(x_dram[:, tiles, :], x_sb[:, tiles, :]).then_inc(x_stored, 16)

            sp.dma_start(gate_sb[:, :, :], a["lora_gate"]).then_inc(gate_loaded, 16)
            for b in range(BATCH):
                if b >= CTX_SLOTS:
                    sp.wait_ge(scaled_done, HALVES * (b - CTX_SLOTS + 1))
                    load_ctx(sp, a, ctx_ring, b, ctx_loaded[b % CTX_SLOTS])
                if b >= W_SLOTS_L:
                    wait_lo_split(sp, b - W_SLOTS_L)
                sp.dma_start(stage[:, b % W_SLOTS_L, :], a["lora_weights"][b // 2, :, (b % 2) * W_COLS:
                                                                           (b % 2 + 1) * W_COLS])\
                  .then_inc(staged[b % W_SLOTS_L], 16)
                if b in (9, 13):
                    store_x(b // 4 - 2)
            store_x(2)
            load_picks_masks(0)
            store_x(3)
            for kind in range(2):
                for m in range(HALVES):
                    source = bass.AP(mask_dram.tensor, (kind * E + m * 4) * TOKENS,
                                     [[TOKENS, 4], [0, RANK], [1, TOKENS // 2]])
                    sp.dma_start(masks_sb[:, kind, m, 0:TOKENS // 2], source).then_inc(masks_loaded, 16)
            load_picks_masks(1)
            sp.wait_ge(masks_loaded, 16 * 2 * HALVES)
            sp.wait_ge(x_stored, 64)

        @block.gpsimd
        def _(pool):
            nc.gpsimd.iota(order[:, :], pattern=[[-1, E]], base=E, channel_multiplier=0,
                           allow_small_or_imprecise_dtypes=True).then_inc(order_done, 1)
            pool.wait_ge(late_mv, TILES - EARLY_NORM)
            attention_rstd(nc, norm, slice(EARLY_NORM, TILES), late_rstd)
            for i in range(LAST):
                if 1 <= i <= BATCH:
                    b = i - 1
                    if b % W_SLOTS_L < W_SLOTS_L - 1:
                        low_weights(pool, nc.gpsimd, b, lo_split_pool)
                if i >= 7:
                    t = i - 7
                    pool.wait_ge(x_hi_done, t + 1)
                    cols = slice(P * t, P * (t + 1))
                    nc.gpsimd.tensor_tensor(x_lo[:, :, cols], x_t[:, t % 2, :, :], x_hi[:, :, cols].bitcast(FP32),
                                            ALU.subtract).then_inc(x_lo_done, 1)
                if 3 <= i < BATCH + 3:
                    b = i - 3
                    pool.wait_ge(mv_done, b + 1)
                    nc.gpsimd.tensor_scalar_add(rstd2[:, b:b + 1], meanvar2[:, b, 1:2], EPS).then_inc(eps_added, 1)
                    pool.wait_ge(eps_added, b + 1)
                    nc.gpsimd.tensor_tensor(rstd2[:, b:b + 1], rstd2[:, b:b + 1], minus_half[:, 0:1],
                                            ALU.pow).then_inc(rstd_done, 1)

        @block.scalar
        def _(act):
            def router_exp(half):
                act.wait_ge(exp_ready, half + 1)
                nc.scalar.activation(probs[:, :, :], probs[:, :, :], ACT.Exp).then_inc(probs_exp, 1)

            def copy_picks(half):
                act.wait_ge(picks_turned, half + 1)
                if half:
                    act.wait_ge(picks_stored, 32)
                nc.scalar.copy(masks_t[:, :], router_bank[:, 0:P]).then_inc(picks_copied, 1)
                nc.scalar.copy(rw_t[:, :], router_bank[0:HT * PICKS, P:2 * P]).then_inc(picks_copied, 1)

            for i in range(LAST):
                if 6 <= i < BATCH + 6:
                    t = i - 6
                    act.wait_ge(turned, t + 1)
                    if t >= 2:
                        act.wait_ge(x_lo_done, t - 1)
                        act.wait_ge(logits_done, t - 1)
                    nc.scalar.copy(x_t[:, t % 2, :, :], turn_banks[t % 2][:, 0:DIM].rearrange(
                        "p (c t) -> p c t", c=HALVES)).then_inc(xt_copied, 1)
                if i < BATCH:
                    b = i
                    act.wait_ge(top_done, b + 1)
                    if b >= 3:
                        act.wait_ge(out_done, b - 2)
                    for m in range(HALVES):
                        nc.scalar.activation(weights[:, b % 3, m, :], score_banks[b % 2][:, m * DIM:(m + 1) * DIM],
                                             ACT.Exp, bias=minus_top[:, b, m:m + 1],
                                             accum_out=total[:, b, m:m + 1]).then_inc(exp_done, 1)
                if 6 <= i < BATCH + 6:
                    t = i - 6
                    act.wait_ge(xt_copied, t + 1)
                    nc.scalar.copy(x_hi[:, :, P * t:P * (t + 1)], x_t[:, t % 2, :, :]).then_inc(x_hi_done, 1)
                if i < BATCH:
                    act.wait_ge(staged[i % W_SLOTS_L], 16 * (i // W_SLOTS_L + 1))
                    nc.scalar.copy(w_hi[:, i // 2, (i % 2) * W_COLS:(i % 2 + 1) * W_COLS],
                                   stage[:, i % W_SLOTS_L, :]).then_inc(hi_split, 1)
                if i == HT + 7:
                    router_exp(0)
                if i == HT + 12:
                    copy_picks(0)
            router_exp(1)
            copy_picks(1)

        @block.tensor
        def _(pe):
            def turn_picks(half):
                pe.wait_ge(step, LORA_STEPS * (half + 1))
                if half:
                    pe.wait_ge(picks_copied, 2)
                nc.tensor.transpose(router_bank[:, 0:P], masks[:, :, :, :], ident[:, :])
                nc.tensor.transpose(router_bank[0:HT * PICKS, P:2 * P], rw[:, :, :], ident[:, :])\
                  .then_inc(picks_turned, 1)

            for i in range(LAST):
                if i < BATCH:
                    b = i
                    if b >= CTX_SLOTS:
                        pe.wait_ge(ctx_loaded[b % CTX_SLOTS], 32 * (b // CTX_SLOTS))
                    pe.wait_ge(y_ready, b + 1)
                    if b >= 2:
                        pe.wait_ge(exp_done, HALVES * (b - 1))
                    for m in range(HALVES):
                        last = nc.tensor.matmul(score_banks[b % 2][:, m * DIM:(m + 1) * DIM],
                                                ctx_ring[:, b % CTX_SLOTS, m * P:(m + 1) * P], y[:, b % 2, :],
                                                start=True, stop=True)
                    last.then_inc(scores_done, 1)
                if 2 <= i < BATCH + 2:
                    b = i - 2
                    pe.wait_ge(scaled_done, HALVES * (b + 1))
                    pe.wait_ge(exp_done, HALVES * (b + 1))
                    if b >= 2:
                        pe.wait_ge(x_added, b - 1)
                    for m in range(HALVES):
                        last = nc.tensor.matmul(out_banks[b % 2][:, 0:DIM], scaled[:, b % 2, m * P:(m + 1) * P],
                                                weights[:, b % 3, m, :], start=(m == 0), stop=(m == HALVES - 1))
                    last.then_inc(out_done, 1)
                if 5 <= i < BATCH + 5:
                    t = i - 5
                    pe.wait_ge(z_ready, t + 1)
                    if t >= 2:
                        pe.wait_ge(xt_copied, t - 1)
                    for c in range(HALVES):
                        last = nc.tensor.transpose(turn_banks[t % 2][:, c * P:(c + 1) * P],
                                                   z[:, t % 2, c * P:(c + 1) * P], ident[:, :])
                    last.then_inc(turned, 1)
                if i >= 7:
                    t = i - 7
                    if t == 0:
                        pe.wait_ge(gate_loaded, 16)
                    pe.wait_ge(xt_copied, t + 1)
                    for c in range(HALVES):
                        last = nc.tensor.matmul(logit_banks[t // HT][:, t % HT * E:(t % HT + 1) * E],
                                                x_t[:, t % 2, c, :], gate_sb[:, c, :],
                                                start=(c == 0), stop=(c == HALVES - 1))
                    last.then_inc(logits_done, 1)
                if i == HT + 11:
                    turn_picks(0)
            turn_picks(1)

        @block.vector
        def _(dve):
            steps = [0]

            def dve_step(ins):
                steps[0] += 1
                ins.then_inc(step, 1)
                dve.wait_ge(step, steps[0])

            wide = [P, HT, E]

            def router_shift(half):
                logits = logit_banks[half][:, 0:HT * E].rearrange("p (t e) -> p t e", e=E)
                dve.wait_ge(logits_done, HT * (half + 1))
                dve_step(nc.vector.reduce_max(prob_sum[:, :], logits, axis=AX.X))
                nc.vector.tensor_tensor(probs[:, :, :], logits, prob_sum[:, :].unsqueeze(2).broadcast_to(wide),
                                        ALU.subtract).then_inc(exp_ready, 1)

            def router_probs(half):
                dve.wait_ge(probs_exp, half + 1)
                dve_step(nc.vector.reduce_sum(prob_sum[:, :], probs[:, :, :], axis=AX.X))
                dve_step(nc.vector.reciprocal(prob_sum[:, :], prob_sum[:, :]))
                dve_step(nc.vector.tensor_tensor(probs[:, :, :], probs[:, :, :],
                                                 prob_sum[:, :].unsqueeze(2).broadcast_to(wide), ALU.mult))

            def router_pick(half, k):
                if k == 0:
                    dve.wait_ge(order_done, 1)
                    if half:
                        dve.wait_ge(picks_turned, 1)
                pick_first_max(dve_step, nc, probs[:, :, :], wide, order[:, :].unsqueeze(1).broadcast_to(wide),
                               (top[:, k, :], hit[:, :, :], top_hit[:, :]))
                if k == 0:
                    dve_step(nc.vector.tensor_copy(masks[:, :, 0, :], hit[:, :, :]))
                else:
                    dve_step(nc.vector.tensor_tensor(masks[:, :, 1, :], hit[:, :, :], masks[:, :, 0, :],
                                                     ALU.subtract))

            def router_weights(half):
                dve_step(nc.vector.tensor_tensor(prob_sum[:, :], top[:, 0, :], top[:, 1, :], ALU.add))
                dve_step(nc.vector.reciprocal(prob_sum[:, :], prob_sum[:, :]))
                dve_step(nc.vector.tensor_tensor(rw[:, :, :].rearrange("p t k -> p k t"), top[:, :, :],
                                                 prob_sum[:, :].unsqueeze(1).broadcast_to([P, PICKS, HT]), ALU.mult))

            def normalize(b):
                if b == EARLY_NORM:
                    dve.wait_ge(late_rstd, 3)
                if b >= 2:
                    dve.wait_ge(scores_done, b - 1)
                nc.vector.tensor_scalar(y[:, b % 2, :], x_sb[:, b, :], meanvar[:, b, 0:1], rstd[:, b:b + 1],
                                        ALU.subtract, ALU.mult).then_inc(y_ready, 1)

            normalize(0)
            for t in range(EARLY_NORM, TILES):
                nc.vector.bn_aggr(meanvar[:, t, :], stats[:, t, :]).then_inc(late_mv, 1)
            for i in range(LAST):
                if i < BATCH:
                    dve.wait_ge(scores_done, i + 1)
                    nc.vector.tensor_reduce(minus_top[:, i, :], score_banks[i % 2][:, :].rearrange(
                        "p (m d) -> p m d", m=HALVES), AX.X, ALU.max, negate=True).then_inc(top_done, 1)
                if 1 <= i <= BATCH:
                    dve.wait_ge(exp_done, HALVES * i)
                    nc.vector.reciprocal(inverse[:, i - 1, :], total[:, i - 1, :]).then_inc(inverse_done, 1)
                if i + 1 < BATCH:
                    normalize(i + 1)
                if 1 <= i <= BATCH:
                    b = i - 1
                    dve.wait_ge(inverse_done, b + 1)
                    if b >= 2:
                        dve.wait_ge(out_done, b - 1)
                    for m in range(HALVES):
                        nc.vector.tensor_scalar_mul(scaled[:, b % 2, m * P:(m + 1) * P],
                                                    ctx_ring[:, b % CTX_SLOTS, DIM + m * P:DIM + (m + 1) * P],
                                                    inverse[:, b, m:m + 1]).then_inc(scaled_done, 1)
                if 3 <= i < BATCH + 3:
                    b = i - 3
                    dve.wait_ge(out_done, b + 1)
                    nc.vector.tensor_tensor(x_sb[:, b, :], x_sb[:, b, :], out_banks[b % 2][:, 0:DIM],
                                            ALU.add).then_inc(x_added, 1)
                if 4 <= i < BATCH + 4:
                    t = i - 4
                    dve.wait_ge(rstd_done, t + 1)
                    if t >= 2:
                        dve.wait_ge(turned, t - 1)
                    nc.vector.tensor_scalar(z[:, t % 2, :], x_sb[:, t, :], meanvar2[:, t, 0:1], rstd2[:, t:t + 1],
                                            ALU.subtract, ALU.mult).then_inc(z_ready, 1)
                if 3 <= i < BATCH + 3:
                    b = i - 3
                    dve.wait_ge(x_added, b + 1)
                    nc.vector.bn_stats(stats2[:, b, :], x_sb[:, b, :]).then_inc(stats_done, 1)
                    dve.wait_ge(stats_done, b + 1)
                    nc.vector.bn_aggr(meanvar2[:, b, :], stats2[:, b, :]).then_inc(mv_done, 1)
                if 1 <= i <= BATCH and i % W_SLOTS_L == 0:
                    low_weights(dve, nc.vector, i - 1, lo_split_dve)
                if i == HT + 7:
                    router_shift(0)
                if i == HT + 8:
                    router_probs(0)
                if i == HT + 9:
                    router_pick(0, 0)
                if i == HT + 10:
                    router_pick(0, 1)
                    router_weights(0)
            router_shift(1)
            router_probs(1)
            router_pick(1, 0)
            router_pick(1, 1)
            router_weights(1)
            assert steps[0] == 2 * LORA_STEPS, steps


def lora_experts(nc, memory, out_rows, mask_dram, rw_dram, x_rows, x_hi, x_lo, w_hi, w_lo, masks, scratch, banks):
    def sb(name, shape, dt=FP32):
        return memory.enter_context(nc.sbuf_tensor(name, shape, dt))

    am_hi, am_lo = (sb(n, [P, 2, 2, HALVES, GROUP_T], F32R) for n in ("am_hi", "am_lo"))
    rw = sb("rw_sb", [P, PICKS, GROUP_T])
    hid_hi, hid_lo = (sb(n, [P, 2, GROUP_T], F32R) for n in ("hid_hi", "hid_lo"))
    f = sb("hid", [P, 4, GROUP_T])
    x_g = sb("x_g", [P, GROUP_T // P, DIM])
    FB, TG = LORA_BLOCKS, GROUP_T // P
    SECOND, BOTH = range(2)
    UNITS = [(kind, j) for kind in range(2) for j in range(4)]
    POOL_UNITS = (1, 2, 5, 6)
    unit_slots = [scratch[:, k, :] for k in range(3)] + [f[:, 2, :], f[:, 3, :]]
    x_banks, out_banks = banks[0:2], banks[2:4]
    term_banks = {BOTH: banks[4:6], SECOND: banks[6:8]}
    a_banks = banks[6:8] + banks[4:6]
    with ExitStack() as s:
        def sem(name):
            return s.enter_context(nc.semaphore(name))

        masks_loaded, rw_loaded, x_loaded, stored = map(sem, ("masks_loaded", "rw_loaded", "x_loaded", "stored"))
        a_done, am_mul, am_hi_done, am_lo_dve, am_lo_pool = map(sem, (
            "a_done", "am_mul", "am_hi_done", "am_lo_dve", "am_lo_pool"))
        first_done, second_done, silu_done, prod_done, weighted, both_done = map(sem, (
            "first_done", "second_done", "silu_done", "prod_done", "weighted", "both_done"))
        hi_done, lo_done, down_done = sem("hi_done"), sem("lo_done"), sem("down_done")
        terms_done = [sem("second_terms_done"), sem("both_terms_done")]
        t_mul, t_sum, t_hi, t_lo, b2_done, x_added = map(sem, ("t_mul", "t_sum", "t_hi", "t_lo", "b2_done", "x_added"))
        block = s.enter_context(nc.Block())

        def mask(g, kind, half):
            return masks[:, kind, half, bass.ds(g * GROUP_T, GROUP_T)]

        def low_inputs_split(engine, g, units):
            on_pool = sum(u in POOL_UNITS for u in range(units))
            engine.wait_ge(am_lo_dve, 4 * g + units - on_pool)
            if on_pool:
                engine.wait_ge(am_lo_pool, 4 * g + on_pool)

        @block.sync
        def _(sp):
            def load_rw(g):
                for k in range(PICKS):
                    sp.dma_start(rw[:, k, :], rw_dram[k, bass.ds(g * GROUP_T, GROUP_T)].partition_broadcast(P))\
                      .then_inc(rw_loaded, 16)

            def load_x(g):
                sp.dma_start(x_g[:, :, :], x_rows[:, bass.ds(g * TG, TG), :]).then_inc(x_loaded, 16)

            def store(g):
                sp.wait_ge(x_added, 2 * g + 4)
                sp.dma_start(out_rows[:, bass.ds(g * TG, TG), :], x_g[:, :, :]).then_inc(stored, 16)

            load_rw(0)
            load_x(0)
            for kind in range(2):
                for half in range(HALVES):
                    source = bass.AP(mask_dram.tensor, (kind * LORA_EXPERTS + half * 4) * TOKENS + TOKENS // 2,
                                     [[TOKENS, 4], [0, RANK], [1, TOKENS // 2]])
                    sp.dma_start(masks[:, kind, half, TOKENS // 2:], source).then_inc(masks_loaded, 16)
            with sp.Fori(0, TOKEN_GROUPS - 1) as g:
                sp.wait_ge(weighted, 2 * FB * (g + 1))
                load_rw(g + 1)
                store(g)
                sp.wait_ge(stored, 16 * (g + 1))
                load_x(g + 1)
            store(TOKEN_GROUPS - 1)
            sp.wait_ge(stored, 16 * TOKEN_GROUPS)

        def weight_cols(chunk, which, c):
            cols = slice(which * DIM + c * P, which * DIM + (c + 1) * P)
            return w_hi[:, chunk, cols], w_lo[:, chunk, cols]

        @block.tensor
        def _(pe):
            def x_cols(g, c):
                return x_hi[:, c, bass.ds(g * GROUP_T, GROUP_T)], x_lo[:, c, bass.ds(g * GROUP_T, GROUP_T)]

            def low_rank_in(g, parts, wait):
                for j in parts:
                    w, half = j // 2, j % 2
                    if wait:
                        pe.wait_ge(t_mul, 4 * (g - 1) + j + 1)
                    last = None
                    for c in range(HALVES):
                        cols = slice(w * 2 * DIM + c * DIM + half * P, w * 2 * DIM + c * DIM + (half + 1) * P)
                        w_parts = w_hi[:, FB, cols], w_lo[:, FB, cols]
                        for k, (wp, xp) in enumerate(split_products(w_parts, x_cols(g, c))):
                            last = nc.tensor.matmul(a_banks[j][:, :], wp, xp,
                                                    start=(c == 0 and k == 0), stop=(c == 1 and k == 2))
                    last.then_inc(a_done, 1)

            def base(g, n, wait):
                if wait:
                    pe.wait_ge(prod_done, 2 * (FB * g + n))
                for w in range(2):
                    for c in range(HALVES):
                        for k, (wp, xp) in enumerate(split_products(weight_cols(n, w, c), x_cols(g, c))):
                            nc.tensor.matmul(x_banks[w][:, :], wp, xp, start=(c == 0 and k == 0), stop=False,
                                             skip_group_check=True)

            def low_rank(g, n, kind):
                if n == 0:
                    low_inputs_split(pe, g, 4 * (kind + 1))
                if kind == 1:
                    pe.wait_ge(prod_done, 2 * (FB * g + n) + 1)
                for w in range(2):
                    for half in range(HALVES):
                        am = am_hi[:, kind, w, half, :], am_lo[:, kind, w, half, :]
                        for k, (wp, ap) in enumerate(split_products(weight_cols(n, 2 + w, half), am)):
                            last = nc.tensor.matmul(x_banks[w][:, :], wp, ap, start=False,
                                                    stop=(half == 1 and k == 2), skip_group_check=True)
                last.then_inc(second_done if kind else first_done, 1)

            def terms(g, n, which):
                pe.wait_ge(lo_done, 2 * (FB * g + n) + which + 3)
                for half in range(HALVES):
                    hid = hid_hi[:, which, :], hid_lo[:, which, :]
                    for j, (wp, hp) in enumerate(split_products(weight_cols(n, 5, half), hid)):
                        last = nc.tensor.matmul(term_banks[which][half][:, :], wp, hp, start=(n == 0 and j == 0),
                                                stop=(n == FB - 1 and j == 2))
                last.then_inc(terms_done[which], 1)

            def down(g, n, tiles):
                pe.wait_ge(lo_done, 2 * (FB * g + n) + BOTH + 3)
                if n == 0 and tiles[0] == 0:
                    pe.wait_ge(x_added, 2 * g + 2)
                for t in tiles:
                    rows = slice(t * P, (t + 1) * P)
                    w = w_hi[:, n, 4 * DIM:5 * DIM], w_lo[:, n, 4 * DIM:5 * DIM]
                    for k, (hp, wp) in enumerate(split_products((hid_hi[:, BOTH, rows], hid_lo[:, BOTH, rows]), w)):
                        last = nc.tensor.matmul(out_banks[t // 2][:, (t % 2) * DIM:(t % 2 + 1) * DIM], hp, wp,
                                                start=(n == 0 and k == 0 and t % 2 == 0), stop=False,
                                                skip_group_check=True)
                if tiles[-1] == TG - 1:
                    last.then_inc(down_done, 1)

            def low_rank_out(g, tiles):
                if tiles[0] == 0:
                    pe.wait_ge(t_lo, 2 * (g + 1))
                for t in tiles:
                    for half in range(HALVES):
                        rows = slice(t * P, (t + 1) * P)
                        cols = slice(4 * DIM + half * DIM, 4 * DIM + (half + 1) * DIM)
                        w = w_hi[:, FB, cols], w_lo[:, FB, cols]
                        parts = hid_hi[:, half, rows], hid_lo[:, half, rows]
                        for k, (hp, wp) in enumerate(split_products(parts, w)):
                            last = nc.tensor.matmul(out_banks[t // 2][:, (t % 2) * DIM:(t % 2 + 1) * DIM], hp, wp,
                                                    start=False, stop=(half == 1 and k == 2), skip_group_check=True)
                last.then_inc(b2_done, 1)

            def group(g, last_group):
                low_rank(g, 0, 1)
                for n in range(1, FB):
                    base(g, n, True)
                    low_rank(g, n, 0)
                    terms(g, n - 1, BOTH)
                    down(g, n - 1, (0, 1))
                    low_rank(g, n, 1)
                    terms(g, n - 1, SECOND)
                    down(g, n - 1, (2, 3))
                if not last_group:
                    base(g + 1, 0, True)
                terms(g, FB - 1, SECOND)
                terms(g, FB - 1, BOTH)
                if not last_group:
                    low_rank_in(g + 1, (0, 1), True)
                down(g, FB - 1, (0, 1, 2, 3))
                if not last_group:
                    low_rank_in(g + 1, (2, 3), True)
                low_rank_out(g, (0, 1))
                if not last_group:
                    low_rank(g + 1, 0, 0)
                low_rank_out(g, (2, 3))

            pe.sem_inc(x_added, 2)
            low_rank_in(0, range(4), False)
            base(0, 0, False)
            low_rank(0, 0, 0)
            with pe.Fori(0, TOKEN_GROUPS - 1) as g:
                group(g, False)
            group(TOKEN_GROUPS - 1, True)

        @block.scalar
        def _(act):
            def low_inputs_high(g, units):
                for u in units:
                    kind, j = UNITS[u]
                    act.wait_ge(am_mul, 8 * g + u + 1)
                    nc.scalar.copy(am_hi[:, kind, j // 2, j % 2, :], unit_slots[u % 5]).then_inc(am_hi_done, 1)

            def silu_of_first(F):
                act.wait_ge(first_done, F + 1)
                act.wait_ge(lo_done, 2 * F + 2)
                nc.scalar.activation(f[:, 0, :], x_banks[0][:, :], ACT.Silu).then_inc(silu_done, 1)

            def group(g, last_group):
                for n in range(FB):
                    F = FB * g + n
                    if n > 0:
                        silu_of_first(F)
                    act.wait_ge(second_done, F + 1)
                    nc.scalar.activation(f[:, 1, :], x_banks[0][:, :], ACT.Silu).then_inc(silu_done, 1)
                    act.wait_ge(weighted, 2 * F + 2)
                    act.wait_ge(terms_done[SECOND], F + 1)
                    if n == 0:
                        act.wait_ge(b2_done, 2 * g + 1)
                    nc.scalar.copy(hid_hi[:, SECOND, :], f[:, 1, :]).then_inc(hi_done, 1)
                    act.wait_ge(both_done, F + 1)
                    act.wait_ge(down_done, F + 1)
                    nc.scalar.copy(hid_hi[:, BOTH, :], f[:, 0, :]).then_inc(hi_done, 1)
                for half in range(HALVES):
                    act.wait_ge(t_sum, 2 * g + half + 1)
                    if half == 0:
                        act.wait_ge(down_done, FB * (g + 1) + 1)
                    nc.scalar.copy(hid_hi[:, half, :], f[:, 2 + half, :]).then_inc(t_hi, 1)
                    if not last_group:
                        low_inputs_high(g + 1, [half])
                if not last_group:
                    low_inputs_high(g + 1, range(2, 8))
                    silu_of_first(FB * (g + 1))

            for which in range(2):
                act.sem_inc(terms_done[which], 1)
            act.sem_inc(down_done, 1)
            act.sem_inc(b2_done, 1)
            act.sem_inc(lo_done, 2)
            low_inputs_high(0, range(8))
            silu_of_first(0)
            with act.Fori(0, TOKEN_GROUPS - 1) as g:
                group(g, False)
            group(TOKEN_GROUPS - 1, True)

        def low_input_low(engine, ops, g, u):
            kind, j = UNITS[u]
            engine.wait_ge(am_hi_done, 8 * g + u + 1)
            ops.tensor_tensor(am_lo[:, kind, j // 2, j % 2, :], unit_slots[u % 5],
                              am_hi[:, kind, j // 2, j % 2, :].bitcast(FP32), ALU.subtract)\
               .then_inc(am_lo_pool if u in POOL_UNITS else am_lo_dve, 1)

        @block.gpsimd
        def _(pool):
            def group(g, last_group):
                for n in range(FB):
                    F = FB * g + n
                    if n == 0:
                        pool.wait_ge(rw_loaded, 16 * PICKS * (g + 1))
                    for k in range(PICKS):
                        pool.wait_ge(prod_done, 2 * F + k + 1)
                        nc.gpsimd.tensor_tensor(f[:, k, :], f[:, k, :], rw[:, k, :], ALU.mult).then_inc(weighted, 1)
                    pool.wait_ge(weighted, 2 * F + 2)
                    nc.gpsimd.tensor_tensor(f[:, 0, :], f[:, 0, :], f[:, 1, :], ALU.add).then_inc(both_done, 1)
                for half in range(HALVES):
                    pool.wait_ge(t_mul, 4 * g + 2 + half + 1)
                    nc.gpsimd.tensor_tensor(f[:, 2 + half, :], f[:, 2 + half, :], f[:, half, :],
                                            ALU.add).then_inc(t_sum, 1)
                if not last_group:
                    for u in POOL_UNITS:
                        low_input_low(pool, nc.gpsimd, g + 1, u)

            for u in POOL_UNITS:
                low_input_low(pool, nc.gpsimd, 0, u)
            with pool.Fori(0, TOKEN_GROUPS - 1) as g:
                group(g, False)
            group(TOKEN_GROUPS - 1, True)

        @block.vector
        def _(dve):
            def low_input_product(g, u, wait):
                kind, j = UNITS[u]
                dve.wait_ge(a_done, 4 * g + j + 1)
                if u >= 5:
                    low_inputs_split(dve, g, u - 4)
                elif u >= 3 and wait:
                    dve.wait_ge(t_lo, 2 * (g - 1) + u - 2)
                nc.vector.tensor_tensor(unit_slots[u % 5], a_banks[j][:, :], mask(g, kind, j % 2),
                                        ALU.mult).then_inc(am_mul, 1)

            def low_inputs(g, wait):
                low_input_product(g, 0, wait)
                low_input_product(g, 1, wait)
                low_input_low(dve, nc.vector, g, 0)
                if wait:
                    terms_low(g - 1)
                low_input_product(g, 2, wait)
                low_input_product(g, 3, wait)
                low_input_low(dve, nc.vector, g, 3)
                low_input_product(g, 4, wait)
                low_input_product(g, 5, wait)
                low_input_low(dve, nc.vector, g, 4)
                low_input_product(g, 6, wait)
                low_input_product(g, 7, wait)
                low_input_low(dve, nc.vector, g, 7)

            def terms_low(g):
                for half in range(HALVES):
                    dve.wait_ge(t_hi, 2 * g + half + 1)
                    nc.vector.tensor_tensor(hid_lo[:, half, :], f[:, 2 + half, :],
                                            hid_hi[:, half, :].bitcast(FP32), ALU.subtract).then_inc(t_lo, 1)

            def add_to_x(g):
                dve.wait_ge(x_loaded, 16 * (g + 1))
                for o in range(2):
                    dve.wait_ge(b2_done, 2 * g + o + 2)
                    rows = x_g[:, 2 * o:2 * o + 2, :]
                    nc.vector.tensor_tensor(rows, rows, out_banks[o][:, :].rearrange("p (t d) -> p t d", t=2),
                                            ALU.add).then_inc(x_added, 1)

            def masked_terms(g, which):
                dve.wait_ge(terms_done[which], FB * (g + 1) + 1)
                if which == SECOND:
                    low_inputs_split(dve, g, 8)
                else:
                    dve.wait_ge(lo_done, 2 * FB * (g + 1) + 2)
                for half in range(HALVES):
                    nc.vector.tensor_tensor(f[:, (2 if which == SECOND else 0) + half, :],
                                            term_banks[which][half][:, :], mask(g, 1 - which, half),
                                            ALU.mult).then_inc(t_mul, 1)

            def product(F, k):
                dve.wait_ge(silu_done, 2 * F + k + 1)
                nc.vector.tensor_tensor(f[:, k, :], f[:, k, :], x_banks[1][:, :], ALU.mult).then_inc(prod_done, 1)

            def group(g, last_group):
                for n in range(FB):
                    F = FB * g + n
                    if n > 0:
                        product(F, 0)
                    product(F, 1)
                    for which in (SECOND, BOTH):
                        dve.wait_ge(hi_done, 2 * F + which + 1)
                        nc.vector.tensor_tensor(hid_lo[:, which, :], f[:, 1 - which, :],
                                                hid_hi[:, which, :].bitcast(FP32), ALU.subtract).then_inc(lo_done, 1)
                masked_terms(g, SECOND)
                masked_terms(g, BOTH)
                if last_group:
                    terms_low(g)
                else:
                    low_inputs(g + 1, True)
                if not last_group:
                    product(FB * (g + 1), 0)
                add_to_x(g)

            low_inputs(0, False)
            product(0, 0)
            dve.wait_ge(masks_loaded, 16 * 2 * HALVES)
            with dve.Fori(0, TOKEN_GROUPS - 1) as g:
                group(g, False)
            group(TOKEN_GROUPS - 1, True)


def lora_weights(inputs):
    import numpy as np

    def rows_in_halves(w):
        w = np.asarray(w)
        return w.reshape(HALVES, P, -1).transpose(1, 0, 2).reshape(P, -1)

    def get(n):
        return np.asarray(inputs["L1_ffn_" + n])

    b1, b3 = (get(n).transpose(0, 2, 1).reshape(DIM, -1) for n in ("B1", "B3"))
    a2 = get("A2").reshape(DIM, -1).T
    chunks = []
    for n in range(LORA_BLOCKS):
        fs = slice(n * P, (n + 1) * P)
        chunks.append(np.concatenate([rows_in_halves(m) for m in (
            get("W1")[fs].T, get("W3")[fs].T, b1[:, fs], b3[:, fs])] + [get("W2").T[fs], a2[fs]], axis=1))
    chunks.append(np.concatenate([rows_in_halves(m) for m in (
        get("A1").reshape(DIM, DIM).T, get("A3").reshape(DIM, DIM).T,
        get("B2").transpose(0, 2, 1).reshape(DIM, DIM))], axis=1))
    return np.stack(chunks)


def moe_weights(inputs):
    import numpy as np

    def blocks(experts, shared):
        return np.concatenate([np.asarray(experts), np.asarray(shared)])

    gate = blocks(np.asarray(inputs["L0_ffn_gate_w"]).reshape(-1, DIM), inputs["L0_ffn_sh_gate_w"])
    up = blocks(np.asarray(inputs["L0_ffn_up_w"]).reshape(-1, DIM), inputs["L0_ffn_sh_up_w"])
    down = blocks(np.asarray(inputs["L0_ffn_down_w"]).transpose(0, 2, 1).reshape(-1, DIM),
                  np.asarray(inputs["L0_ffn_sh_down_w"]).T)
    in_rows = [w.reshape(FBLOCKS, P, HALVES, P).transpose(0, 3, 2, 1).reshape(FBLOCKS, P, DIM) for w in (gate, up)]
    return np.concatenate([*in_rows, down.reshape(FBLOCKS, P, DIM)], axis=2)


def kernel(**inputs):
    import numpy as np
    import concourse.bacc as bacc
    from concourse.bass_utils import run_bass_kernel_spmd

    nc = bacc.Bacc("TRN2", target_bir_lowering=False, num_devices=1)
    ctx = np.asarray(inputs["ctx_2048"])
    ctx_rev = ctx.reshape(TOKENS, HALVES, P)[:, :, ::-1]
    arrays = {
        "x": np.asarray(inputs["x"]).reshape(TOKENS, DIM),
        "ctx_t": ctx_rev.transpose(1, 2, 0),
        "ssm_kernel": inputs["L0_xattn_ssm_kernel"],
        "moe_gate": np.asarray(inputs["L0_ffn_gate_weight"]).T.reshape(HALVES, P, EXPERTS).transpose(1, 0, 2),
        "moe_bias": inputs["L0_ffn_e_score_correction_bias"],
        "moe_weights": moe_weights(inputs),
        "ctx_keys": ctx_rev.reshape(TOKENS, DIM),
        "lora_gate": np.asarray(inputs["L1_ffn_Wg"]).T.reshape(HALVES, P, LORA_EXPERTS).transpose(1, 0, 2),
        "lora_weights": lora_weights(inputs),
        "D": np.asarray(inputs["L0_xattn_D"]).reshape(HEADS, 1),
    }
    in_map, args = {}, {}
    for name, value in arrays.items():
        value = np.ascontiguousarray(value)
        in_map["in_" + name] = value
        args[name] = nc.dram_tensor("in_" + name, value.shape, mybir.dt.from_np(value.dtype), kind="ExternalInput").ap()
    out = nc.dram_tensor("out_x", (TOKENS, DIM), FP32, kind="ExternalOutput").ap()
    build(nc, args, out)
    r = run_bass_kernel_spmd(nc, [in_map], core_ids=[0])
    return r.results[0]["out_x"].reshape(BATCH, SEQ, DIM)
```

```python
import concourse.bass as bass
from concourse import mybir
from contextlib import ExitStack

FP32 = mybir.dt.float32
F32R = mybir.dt.float32r
BF16 = mybir.dt.bfloat16
ALU = mybir.AluOpType
ACT = mybir.ActivationFunctionType
AX = mybir.AxisListType

P = 128
BATCH = 16
SEQ = 128
DIM = 256
TOKENS = BATCH * SEQ
TILES = TOKENS // P
HALVES = DIM // P
EPS = 1e-5

HEADS = 16
HEAD_DIM = 8
CHUNK_B = 8
CHUNKS = BATCH // CHUNK_B
PAIRS = CHUNK_B * HEAD_DIM * HEAD_DIM
KPAD = 3 * P

GROUP_T = 512
TOKEN_GROUPS = TOKENS // GROUP_T

EXPERTS = 16
GROUPS = 4
TOP_GROUPS = 2
TOP_EXPERTS = 4
ROUTED_SCALE = 2.5
SHARED_BLOCKS = 2
FBLOCKS = EXPERTS + SHARED_BLOCKS
MOE_COLS = 3 * DIM
SHARED_STEPS = TOKEN_GROUPS * SHARED_BLOCKS
LAG = 2
W_SLOTS = 4
W_ORDER = [EXPERTS + n for n in range(SHARED_BLOCKS)] + list(range(EXPERTS))
SPLIT_EARLY = HEADS // 2
STAGES, LATE_STAGES = 4, 2
BIG = 1e30
SENTINELS = 8 - TOP_EXPERTS
STEPS = 5 + TOP_GROUPS * 7 + 3 + 2 + 6

SOFTMAX_SCALE = DIM ** -0.5
EARLY_NORM = TILES - TILES // TOKEN_GROUPS
CTX_SLOTS = 3

LORA_EXPERTS = 8
RANK = 32
PICKS = 2
LORA_BLOCKS = 7
LORA_CHUNKS = LORA_BLOCKS + 1
LORA_COLS = 6 * DIM
LORA_STEPS = 4 + PICKS * 7 + 3


def build(nc, a, out):
    x_rows = a["x"].rearrange("(t p) d -> p t d", p=P)
    out_rows = out.rearrange("(t p) d -> p t d", p=P)
    kpad_dram = nc.dram_tensor("kpad_scratch", [HEADS, KPAD], FP32).ap()
    w_dram = nc.dram_tensor("w_scratch", [EXPERTS, TOKENS], FP32).ap()
    mask_dram = nc.dram_tensor("mask_scratch", [PICKS * LORA_EXPERTS, TOKENS], BF16).ap()
    rw_dram = nc.dram_tensor("rw_scratch", [PICKS, TOKENS], FP32).ap()
    x_dram_rows = nc.dram_tensor("x_scratch", [TOKENS, DIM], FP32).ap().rearrange("(t p) d -> p t d", p=P)

    with ExitStack() as whole:
        banks = [whole.enter_context(nc.psum_tensor(f"bank{i}", [P, 512], FP32)) for i in range(8)]
        first_picks_stored = whole.enter_context(nc.semaphore("first_picks_stored"))
        picks_stored = whole.enter_context(nc.semaphore("picks_stored"))

        def far(name, shape, dt=F32R):
            return whole.enter_context(nc.sbuf_tensor(name, shape, dt, side="right"))

        with ExitStack() as residual:
            def keep(name, shape):
                return residual.enter_context(nc.sbuf_tensor(name, shape, FP32))

            ident = keep("ident", [P, P])
            norm = (keep("stats", [P, TILES, 6]), keep("meanvar", [P, TILES, 2]), keep("rstd", [P, TILES]),
                    keep("minus_half", [P, TILES]))
            x_sb = keep("x_sb", [P, TILES, DIM])

            with ExitStack() as layer:
                def parts(name, shape):
                    return [layer.enter_context(nc.sbuf_tensor(name + part, shape, F32R)) for part in ("_hi", "_lo")]

                w = parts("moe_w", [P, FBLOCKS, MOE_COLS])
                with ExitStack() as queries:
                    q_t = queries.enter_context(nc.sbuf_tensor("q_t", [P, HALVES, TOKENS], FP32, side="right"))
                    with ExitStack() as memory:
                        conv_phase(nc, memory, a, x_rows, kpad_dram, ident, x_sb, norm, q_t, *w, banks)
                    x_parts = parts("moe_x", [P, HALVES, TOKENS])
                    with ExitStack() as memory:
                        conv_end_phase(nc, memory, a, ident, x_sb, norm, q_t, *x_parts, banks)
                ctx_ring = far("ctx_ring", [P, CTX_SLOTS, 2 * DIM], FP32)
                with ExitStack() as memory:
                    moe_phase(nc, memory, a, w_dram, ident, x_sb, norm, *x_parts, *w, ctx_ring, banks)

            w = [far(n, [P, LORA_CHUNKS, LORA_COLS]) for n in ("lora_w_hi", "lora_w_lo")]
            x_parts = [far(n, [P, HALVES, TOKENS]) for n in ("lora_x_hi", "lora_x_lo")]
            masks = far("masks_sb", [P, 2, HALVES, TOKENS], BF16)
            picks_t = far("masks_t", [P, 2, P], BF16), far("rw_t", [TILES * PICKS, P], FP32)
            with ExitStack() as memory:
                softmax_phase(nc, memory, a, x_dram_rows, mask_dram, rw_dram, ident, x_sb, norm, *w, *x_parts, picks_t,
                              first_picks_stored, picks_stored, ctx_ring, banks)
        with ExitStack() as memory:
            lora_experts(nc, memory, out_rows, mask_dram, rw_dram, x_dram_rows, *x_parts, *w, masks, ctx_ring,
                         first_picks_stored, picks_stored, banks)


def conv_phase(nc, memory, a, x_rows, kpad_dram, ident, x_sb, norm, q_t, w_hi, w_lo, banks):
    stats, meanvar, rstd, minus_half = norm

    def sb(name, shape, dt=FP32):
        return memory.enter_context(nc.sbuf_tensor(name, shape, dt))

    ctx_t = sb("ctx_t", [P, HALVES, TOKENS])
    toeplitz = sb("toeplitz", [P, HEADS, 2 * P])
    y = sb("y", [P, 4, DIM])
    kv = sb("kv", [P, 2, HALVES, PAIRS])
    prod = sb("prod", [P, 2, PAIRS])
    kpad = sb("kpad", [HEADS, KPAD])
    d_col = sb("d_col", [HEADS, 1])
    stage = sb("stage", [P, STAGES, MOE_COLS])

    QUARTERS = 4
    TOEPLITZ_PARTS = ((0, 2), (2, HEADS // 2), (HEADS // 2, HEADS))
    with ExitStack() as s:
        def sem(name):
            return s.enter_context(nc.semaphore(name))

        kpad_zero, k_loaded, d_added, kpad_stored = map(sem, ("kpad_zero", "k_loaded", "d_added", "kpad_stored"))
        toeplitz_loaded = [sem(f"toeplitz_loaded{i}") for i in range(len(TOEPLITZ_PARTS))]
        x_loaded = [sem(f"x_loaded{i}") for i in range(QUARTERS)]
        ctx_loaded, consts, ident_zero = map(sem, ("ctx_loaded", "consts", "ident_zero"))
        stats_done, mv_done, rstd_half, rstd_done = map(sem, ("stats_done", "mv_done", "rstd_half", "rstd_done"))
        y_ready, q_transposed, q_copied = map(sem, ("y_ready", "q_transposed", "q_copied"))
        kv_ready, conv_done, prod_ready, reduced = map(sem, ("kv_ready", "conv_done", "prod_ready", "reduced"))
        hi_split, lo_split = sem("hi_split"), sem("lo_split")
        staged = [sem(f"staged{i}") for i in range(STAGES)]
        q_banks, conv_banks = banks[4:8], banks[0:4]
        wide = [P, CHUNK_B, HEAD_DIM, HEAD_DIM]
        block = s.enter_context(nc.Block())

        @block.sync
        def _(sp):
            for i in range(QUARTERS):
                sp.dma_start(x_sb[:, 4 * i:4 * i + 4, :], x_rows[:, 4 * i:4 * i + 4, :]).then_inc(x_loaded[i], 16)
            def load_toeplitz(part):
                first, end = TOEPLITZ_PARTS[part]
                sp.dma_start(toeplitz[:, first:end, :], bass.AP(kpad_dram.tensor, first * KPAD, [
                    [1, P], [KPAD, end - first], [1, 2 * P]])).then_inc(toeplitz_loaded[part], 16)

            sp.wait_ge(kpad_stored, 16)
            load_toeplitz(0)
            for h in range(HALVES):
                sp.dma_start(ctx_t[:, h, :], a["ctx_t"][h]).then_inc(ctx_loaded, 16)
            for part in range(1, len(TOEPLITZ_PARTS)):
                load_toeplitz(part)
            for k, n in enumerate(W_ORDER[:SPLIT_EARLY]):
                if k >= STAGES:
                    sp.wait_ge(lo_split, k - STAGES + 1)
                sp.dma_start(stage[:, k % STAGES, :], a["moe_weights"][n]).then_inc(staged[k % STAGES], 16)

        @block.gpsimd
        def _(pool):
            nc.gpsimd.memset(kpad[:, :], 0.0).then_inc(kpad_zero, 1)
            nc.gpsimd.memset(ident[:, :], 0.0).then_inc(ident_zero, 1)
            nc.gpsimd.memset(minus_half[:, :], -0.5)
            pool.wait_ge(ident_zero, 1)
            nc.gpsimd.affine_select(out=ident[:, :], in_=ident[:, :], compare_op=ALU.not_equal, fill=1.0,
                                    base=0, pattern=[[-1, P]], channel_multiplier=1).then_inc(consts, 1)
            for i in range(QUARTERS):
                tiles = slice(4 * i, 4 * i + 4)
                pool.wait_ge(mv_done, i + 1)
                nc.gpsimd.tensor_scalar_add(rstd[:, tiles], meanvar[:, tiles, 1], EPS).then_inc(rstd_half, 1)
                pool.wait_ge(rstd_half, i + 1)
                nc.gpsimd.tensor_tensor(rstd[:, tiles], rstd[:, tiles], minus_half[:, tiles], ALU.pow)\
                  .then_inc(rstd_done, 1)
            pool.sem_inc(conv_done, CHUNKS)
            pool.wait_ge(ctx_loaded, 16 * HALVES)
            for h in range(HEADS):
                if h % 2:
                    k, n = h // 2, W_ORDER[h // 2]
                    pool.wait_ge(hi_split, k + 1)
                    nc.gpsimd.tensor_tensor(w_lo[:, n, :], stage[:, k % STAGES, :], w_hi[:, n, :].bitcast(FP32),
                                            ALU.subtract).then_inc(lo_split, 1)
                for c in range(CHUNKS):
                    pool.wait_ge(conv_done, CHUNKS * h + c + 1)
                    for m in range(HALVES):
                        feat = ctx_t[:, m, :].rearrange("p (b t) -> p b t", t=SEQ)[
                            :, c * CHUNK_B:(c + 1) * CHUNK_B, bass.ds(h * HEAD_DIM, HEAD_DIM)]
                        last = nc.gpsimd.tensor_tensor(
                            kv[:, c, m, :].rearrange("p (b j i) -> p b j i", j=HEAD_DIM, i=HEAD_DIM),
                            feat.unsqueeze(2).broadcast_to(wide), feat.unsqueeze(3).broadcast_to(wide), ALU.mult)
                    last.then_inc(kv_ready, 1)

        @block.scalar
        def _(act):
            act.wait_ge(kpad_zero, 1)
            act.dma_start(kpad[:, P - 1:P - 1 + DIM], a["ssm_kernel"]).then_inc(k_loaded, 16)
            act.dma_start(d_col[:, :], a["D"]).then_inc(k_loaded, 16)
            act.wait_ge(d_added, 1)
            act.dma_start(kpad_dram, kpad[:, :]).then_inc(kpad_stored, 16)
            for n in range(TILES // 2):
                act.wait_ge(q_transposed, n + 1)
                nc.scalar.copy(q_t[:, :, n * 2 * P:(n + 1) * 2 * P],
                               q_banks[n % 4][:, :].rearrange("p (c t) -> p c t", c=HALVES)).then_inc(q_copied, 1)
            for k, n in enumerate(W_ORDER[:SPLIT_EARLY]):
                act.wait_ge(staged[k % STAGES], 16 * (k // STAGES + 1))
                nc.scalar.copy(w_hi[:, n, :], stage[:, k % STAGES, :]).then_inc(hi_split, 1)

        @block.tensor
        def _(pe):
            pe.wait_ge(consts, 1)
            for n in range(TILES // 2):
                pe.wait_ge(y_ready, n + 1)
                if n >= 4:
                    pe.wait_ge(q_copied, n - 3)
                for c in range(HALVES):
                    for k in range(2):
                        last = nc.tensor.transpose(q_banks[n % 4][:, (2 * c + k) * P:(2 * c + k + 1) * P],
                                                   y[:, (2 * n + k) % 4, c * P:(c + 1) * P], ident[:, :])
                last.then_inc(q_transposed, 1)
            for h in range(HEADS):
                for part, (first, _) in enumerate(TOEPLITZ_PARTS):
                    if h == first:
                        pe.wait_ge(toeplitz_loaded[part], 16)
                for c in range(CHUNKS):
                    n = CHUNKS * h + c
                    pe.wait_ge(kv_ready, n + 1)
                    if h >= 1:
                        pe.wait_ge(prod_ready, HALVES * (n - CHUNKS + 1))
                    same, across = toeplitz[:, h, 0:P], toeplitz[:, h, P:2 * P]
                    nc.tensor.matmul(conv_banks[2 * c][:, :], same, kv[:, c, 0, :], start=True, stop=True)
                    nc.tensor.matmul(conv_banks[2 * c + 1][:, :], across, kv[:, c, 0, :], start=True, stop=False)
                    nc.tensor.matmul(conv_banks[2 * c + 1][:, :], same, kv[:, c, 1, :], start=False,
                                     stop=True).then_inc(conv_done, 1)

        @block.vector
        def _(dve):
            dve.wait_ge(k_loaded, 32)
            nc.vector.tensor_tensor(kpad[:, P - 1:P], kpad[:, P - 1:P], d_col[:, :], ALU.add).then_inc(d_added, 1)
            for i in range(QUARTERS + 1):
                if i < QUARTERS:
                    dve.wait_ge(x_loaded[i], 16)
                    for t in range(4 * i, 4 * i + 4):
                        nc.vector.bn_stats(stats[:, t, :], x_sb[:, t, :]).then_inc(stats_done, 1)
                    for t in range(4 * i, 4 * i + 4):
                        dve.wait_ge(stats_done, t + 1)
                        last = nc.vector.bn_aggr(meanvar[:, t, :], stats[:, t, :])
                    last.then_inc(mv_done, 1)
                if i >= 1:
                    dve.wait_ge(rstd_done, i)
                    for t in range(4 * i - 4, 4 * i):
                        if t >= 4 and t % 2 == 0:
                            dve.wait_ge(q_transposed, t // 2 - 1)
                        last = nc.vector.tensor_scalar(y[:, t % 4, :], x_sb[:, t, :], meanvar[:, t, 0:1],
                                                       rstd[:, t:t + 1], ALU.subtract, ALU.mult)
                        if t % 2:
                            last.then_inc(y_ready, 1)
            dve.wait_ge(q_copied, TILES // 2)
            for n in range(HEADS * CHUNKS):
                h, c = n // CHUNKS, n % CHUNKS
                dve.wait_ge(conv_done, CHUNKS + n + 1)
                query = [q_t[:, m, :].rearrange("p (b t) -> p b t", t=SEQ)[
                    :, c * CHUNK_B:(c + 1) * CHUNK_B, h * HEAD_DIM:(h + 1) * HEAD_DIM] for m in range(HALVES)]
                for m in range(HALVES):
                    if n >= 1:
                        dve.wait_ge(reduced, HALVES * (n - 1) + m + 1)
                    nc.vector.tensor_tensor(
                        prod[:, m, :].rearrange("p (b j i) -> p b j i", j=HEAD_DIM, i=HEAD_DIM),
                        conv_banks[2 * c + m][:, :].rearrange("p (b j i) -> p b j i", j=HEAD_DIM, i=HEAD_DIM),
                        query[m].unsqueeze(2).broadcast_to(wide), ALU.mult).then_inc(prod_ready, 1)
                for m in range(HALVES):
                    dve.wait_ge(prod_ready, HALVES * n + m + 1)
                    nc.vector.reduce_sum(query[m], prod[:, m, :].rearrange(
                        "p (b j i) -> p b j i", j=HEAD_DIM, i=HEAD_DIM), axis=AX.X).then_inc(reduced, 1)


def split_products(hi_lo_a, hi_lo_b):
    (a_hi, a_lo), (b_hi, b_lo) = hi_lo_a, hi_lo_b
    return ((a_hi, b_hi), (a_hi, b_lo), (a_lo, b_hi))


def conv_end_phase(nc, memory, a, ident, x_sb, norm, q_t, x_hi, x_lo, banks):
    stats, meanvar, rstd, minus_half = norm

    def sb(name, shape, dt=FP32):
        return memory.enter_context(nc.sbuf_tensor(name, shape, dt))

    gate_sb = sb("moe_gate", [P, HALVES, EXPERTS])
    y, x_t = sb("moe_y", [P, 4, DIM]), sb("moe_x_t", [P, 2, HALVES, 2 * P])
    back_banks, turn_banks, logit_bank = banks[0:4], banks[4:6], banks[7]
    PAIRS_T = TILES // 2
    with ExitStack() as s:
        def sem(name):
            return s.enter_context(nc.semaphore(name))

        att_turned, x_added, stats_done, mv_done, rstd_half, rstd_done, gate_loaded = map(sem, (
            "att_turned", "x_added", "stats_done", "mv_done", "rstd_half", "rstd_done", "gate_loaded"))
        y_ready, turned, xt_copied, hi_done, lo_done, logits_done = map(
            sem, ("y_ready", "turned", "xt_copied", "hi_done", "lo_done", "logits_done"))
        block = s.enter_context(nc.Block())

        @block.sync
        def _(sp):
            sp.dma_start(gate_sb[:, :, :], a["moe_gate"]).then_inc(gate_loaded, 16)

        @block.vector
        def _(dve):
            for i in range(PAIRS_T + 1):
                if i < PAIRS_T:
                    tiles = slice(2 * i, 2 * i + 2)
                    dve.wait_ge(att_turned, i + 1)
                    nc.vector.tensor_tensor(x_sb[:, tiles, :], x_sb[:, tiles, :],
                                            back_banks[i % 4][:, :].rearrange("p (t d) -> p t d", t=2),
                                            ALU.add).then_inc(x_added, 1)
                    dve.wait_ge(x_added, i + 1)
                    for t in (2 * i, 2 * i + 1):
                        last = nc.vector.bn_stats(stats[:, t, :], x_sb[:, t, :])
                    last.then_inc(stats_done, 1)
                if i >= 1:
                    n = i - 1
                    dve.wait_ge(rstd_done, n + 1)
                    if n >= 2:
                        dve.wait_ge(turned, n - 1)
                    for t in (2 * n, 2 * n + 1):
                        last = nc.vector.tensor_scalar(y[:, t % 4, :], x_sb[:, t, :], meanvar[:, t, 0:1],
                                                       rstd[:, t:t + 1], ALU.subtract, ALU.mult)
                    last.then_inc(y_ready, 1)
                if i < PAIRS_T:
                    dve.wait_ge(stats_done, i + 1)
                    for t in (2 * i, 2 * i + 1):
                        last = nc.vector.bn_aggr(meanvar[:, t, :], stats[:, t, :])
                    last.then_inc(mv_done, 1)

        @block.gpsimd
        def _(pool):
            for i in range(PAIRS_T + 2):
                if i < PAIRS_T:
                    tiles = slice(2 * i, 2 * i + 2)
                    pool.wait_ge(mv_done, i + 1)
                    nc.gpsimd.tensor_scalar_add(rstd[:, tiles], meanvar[:, tiles, 1], EPS).then_inc(rstd_half, 1)
                    pool.wait_ge(rstd_half, i + 1)
                    nc.gpsimd.tensor_tensor(rstd[:, tiles], rstd[:, tiles], minus_half[:, tiles],
                                            ALU.pow).then_inc(rstd_done, 1)
                if i >= 2:
                    n = i - 2
                    pool.wait_ge(hi_done, n + 1)
                    cols = slice(2 * P * n, 2 * P * (n + 1))
                    nc.gpsimd.tensor_tensor(x_lo[:, :, cols], x_t[:, n % 2, :, :], x_hi[:, :, cols].bitcast(FP32),
                                            ALU.subtract).then_inc(lo_done, 1)

        @block.scalar
        def _(act):
            for n in range(PAIRS_T):
                act.wait_ge(turned, n + 1)
                if n >= 2:
                    act.wait_ge(lo_done, n - 1)
                    act.wait_ge(logits_done, n - 1)
                nc.scalar.copy(x_t[:, n % 2, :, :], turn_banks[n % 2][:, :].rearrange(
                    "p (c t) -> p c t", c=HALVES)).then_inc(xt_copied, 1)
                act.wait_ge(xt_copied, n + 1)
                nc.scalar.copy(x_hi[:, :, 2 * P * n:2 * P * (n + 1)], x_t[:, n % 2, :, :]).then_inc(hi_done, 1)

        @block.tensor
        def _(pe):
            def attention_back(n):
                if n >= 4:
                    pe.wait_ge(x_added, n - 3)
                for k in range(2):
                    for c in range(HALVES):
                        last = nc.tensor.transpose(back_banks[n % 4][:, (2 * k + c) * P:(2 * k + c + 1) * P],
                                                   q_t[:, c, (2 * n + k) * P:(2 * n + k + 1) * P], ident[:, :])
                last.then_inc(att_turned, 1)

            attention_back(0)
            attention_back(1)
            for i in range(PAIRS_T + 2):
                if i + 2 < PAIRS_T:
                    attention_back(i + 2)
                if 1 <= i <= PAIRS_T:
                    n = i - 1
                    pe.wait_ge(y_ready, n + 1)
                    if n >= 2:
                        pe.wait_ge(xt_copied, n - 1)
                    for c in range(HALVES):
                        for k in range(2):
                            last = nc.tensor.transpose(turn_banks[n % 2][:, (2 * c + k) * P:(2 * c + k + 1) * P],
                                                       y[:, (2 * n + k) % 4, c * P:(c + 1) * P], ident[:, :])
                    last.then_inc(turned, 1)
                if i >= 2:
                    n = i - 2
                    if n == 0:
                        pe.wait_ge(gate_loaded, 16)
                    pe.wait_ge(xt_copied, n + 1)
                    for k in range(2):
                        t = 2 * n + k
                        for c in range(HALVES):
                            last = nc.tensor.matmul(logit_bank[:, t * EXPERTS:(t + 1) * EXPERTS],
                                                    x_t[:, n % 2, c, k * P:(k + 1) * P], gate_sb[:, c, :],
                                                    start=(c == 0), stop=(c == HALVES - 1))
                    last.then_inc(logits_done, 1)


def pick_first_max(dve_step, nc, values, shape, order, scratch):
    top, hit, top_hit = scratch
    top_wide, top_hit_wide = top.unsqueeze(2).broadcast_to(shape), top_hit.unsqueeze(2).broadcast_to(shape)
    dve_step(nc.vector.reduce_max(top, values, axis=AX.X))
    dve_step(nc.vector.tensor_tensor(hit, values, top_wide, ALU.is_equal))
    dve_step(nc.vector.tensor_tensor(hit, hit, order, ALU.mult))
    dve_step(nc.vector.reduce_max(top_hit, hit, axis=AX.X))
    dve_step(nc.vector.tensor_tensor(hit, hit, top_hit_wide, ALU.is_equal))
    dve_step(nc.vector.scalar_tensor_tensor(values, hit, -BIG, values, ALU.mult, ALU.add))
    return hit


def attention_rstd(nc, norm, tiles, step):
    meanvar, rstd, minus_half = norm[1:]
    nc.gpsimd.tensor_scalar_add(rstd[:, tiles], meanvar[:, tiles, 1], EPS).then_inc(step, 1)
    nc.gpsimd.wait_ge(step, 1)
    nc.gpsimd.tensor_tensor(rstd[:, tiles], rstd[:, tiles], minus_half[:, tiles], ALU.pow).then_inc(step, 1)
    nc.gpsimd.wait_ge(step, 2)
    nc.gpsimd.tensor_scalar_mul(rstd[:, tiles], rstd[:, tiles], SOFTMAX_SCALE).then_inc(step, 1)


def moe_phase(nc, memory, a, w_dram, ident, x_sb, norm, x_hi, x_lo, w_hi, w_lo, ctx_ring, banks):
    stats, meanvar, rstd, minus_half = norm

    def sb(name, shape, dt=FP32):
        return memory.enter_context(nc.sbuf_tensor(name, shape, dt))

    T, E, G, PER = TILES, EXPERTS, GROUPS, EXPERTS // GROUPS
    scores, weights = sb("scores", [P, T, E]), sb("router_weights", [P, T, E])
    choice, rest = sb("choice", [P, T, E + SENTINELS]), sb("rest", [P, T, E + SENTINELS])
    bias_sb, order, best = sb("bias_sb", [P, E]), sb("order", [P, G]), sb("best", [P, T, 8])
    pair_hi, pair_lo = sb("pair_hi", [P, T * G, 2]), sb("pair_lo", [P, T * G, 2])
    g_top, g_second, g_score, g_hit, g_mask, g_pen = (sb(n, [P, T, G]) for n in (
        "g_top", "g_second", "g_score", "g_hit", "g_mask", "g_pen"))
    top, top_hit, w_sum = (sb(n, [P, T]) for n in ("top", "top_hit", "w_sum"))
    w_t = sb("w_t", [P, 2, P])
    stage = sb("late_stage", [P, LATE_STAGES, MOE_COLS])
    late = W_ORDER[SPLIT_EARLY:]
    w_ring = sb("w_ring", [P, W_SLOTS, GROUP_T])
    silu, prod, act = (sb(n, [P, 2, GROUP_T]) for n in ("moe_silu", "moe_prod", "moe_act"))
    act_hi, act_lo = (sb(n, [P, 2, GROUP_T], F32R) for n in ("moe_act_hi", "moe_act_lo"))
    gate_banks, up_banks, out_banks, shared_banks = banks[0:2], banks[2:4], banks[4:6], (banks[4:6], banks[6:8])
    router_bank = banks[6]
    with ExitStack() as s:
        def sem(name):
            return s.enter_context(nc.semaphore(name))

        bias_loaded, order_done, sigmoid_done, step, w_transposed, w_copied, w_stored = map(sem, (
            "bias_loaded", "order_done", "sigmoid_done", "step", "w_transposed", "w_copied", "w_stored"))
        w_loaded = [sem(f"w_loaded{i}") for i in range(W_SLOTS)]
        gu_done, silu_done, prod_done, act_ready, hi_done, lo_done, down_done, x_added = map(sem, (
            "gu_done", "silu_done", "prod_done", "act_ready", "hi_done", "lo_done", "down_done", "x_added"))
        shared_lo, hi_split, lo_split = map(sem, ("shared_lo_done", "hi_split", "lo_split"))
        staged = [sem(f"staged{i}") for i in range(LATE_STAGES)]
        stats_done, mv_done, rstd_step, ctx_loaded = map(sem, ("stats_done", "mv_done", "rstd_step", "ctx_loaded"))
        block = s.enter_context(nc.Block())

        def late_splits(m):
            return range(m * len(late) // SHARED_STEPS, (m + 1) * len(late) // SHARED_STEPS)

        def step_of(g, n):
            return SHARED_STEPS + g * EXPERTS + n

        @block.sync
        def _(sp):
            sp.sem_inc(act_ready, W_SLOTS)
            sp.dma_start(bias_sb[:, :], a["moe_bias"].partition_broadcast(P)).then_inc(bias_loaded, 16)
            for k, n in enumerate(late):
                if k >= LATE_STAGES:
                    sp.wait_ge(lo_split, k - LATE_STAGES + 1)
                sp.dma_start(stage[:, k % LATE_STAGES, :], a["moe_weights"][n]).then_inc(staged[k % LATE_STAGES], 16)
            for half in range(2):
                sp.wait_ge(w_copied, half + 1)
                sp.dma_start(w_dram.rearrange("e (t k) -> t e k", k=P)[half * 8:half * 8 + 8], w_t[:, half, :])\
                  .then_inc(w_stored, 16)
            sp.wait_ge(w_stored, 32)
            with sp.Fori(0, TOKEN_GROUPS) as g:
                for e in range(EXPERTS):
                    sp.wait_ge(act_ready, g * EXPERTS + e + 1)
                    sp.dma_start(w_ring[:, e % W_SLOTS, :],
                                 w_dram[e, bass.ds(g * GROUP_T, GROUP_T)].partition_broadcast(P))\
                      .then_inc(w_loaded[e % W_SLOTS], 16)
            for b in range(CTX_SLOTS):
                load_ctx(sp, a, ctx_ring, b, ctx_loaded)
            sp.wait_ge(ctx_loaded, 32 * CTX_SLOTS)

        @block.tensor
        def _(pe):
            def gate_up(n, token):
                for bank, off in ((gate_banks[n % 2], 0), (up_banks[n % 2], HALVES * P)):
                    last = None
                    for c in range(HALVES):
                        cols = slice(off + c * P, off + (c + 1) * P)
                        w = w_hi[:, n, cols], w_lo[:, n, cols]
                        x = (x_hi[:, c, bass.ds(token, GROUP_T)], x_lo[:, c, bass.ds(token, GROUP_T)])
                        for k, (wp, xp) in enumerate(split_products(w, x)):
                            last = nc.tensor.matmul(bank[:, :], wp, xp, start=(c == 0 and k == 0),
                                                    stop=(c == HALVES - 1 and k == 2))
                last.then_inc(gu_done, 1)

            def expert_gate_up(g, n):
                pe.wait_ge(prod_done, step_of(g, n) - 1)
                if n >= SPLIT_EARLY - SHARED_BLOCKS:
                    pe.wait_ge(lo_split, n + 1 - (SPLIT_EARLY - SHARED_BLOCKS))
                gate_up(n, g * GROUP_T)

            def down(n, into, first, last_one):
                for t in range(GROUP_T // P):
                    rows = slice(t * P, (t + 1) * P)
                    act_parts = act_hi[:, n % 2, rows], act_lo[:, n % 2, rows]
                    w = w_hi[:, n, 2 * DIM:3 * DIM], w_lo[:, n, 2 * DIM:3 * DIM]
                    for k, (ap, wp) in enumerate(split_products(act_parts, w)):
                        last = nc.tensor.matmul(into[t // 2][:, (t % 2) * DIM:(t % 2 + 1) * DIM], ap, wp,
                                                start=(first and k == 0 and t % 2 == 0),
                                                stop=(last_one and k == 2), skip_group_check=True)
                last.then_inc(down_done, 1)

            def expert_down(g, n):
                pe.wait_ge(lo_done, g * EXPERTS + n + 3)
                if n == 0:
                    pe.wait_ge(x_added, 2 * g + 2 * TOKEN_GROUPS)
                down(n, out_banks, n == 0, n == EXPERTS - 1)

            def shared_gate_up(m):
                if m >= 2:
                    pe.wait_ge(prod_done, m - 1)
                gate_up(EXPERTS + m % SHARED_BLOCKS, m // SHARED_BLOCKS * GROUP_T)

            def group(g, last_group):
                for n in range(LAG, EXPERTS):
                    expert_gate_up(g, n)
                    expert_down(g, n - LAG)
                for n in range(LAG):
                    if not last_group:
                        expert_gate_up(g + 1, n)
                    expert_down(g, EXPERTS - LAG + n)

            for m in range(LAG):
                shared_gate_up(m)
            for m in range(SHARED_STEPS):
                if m + LAG < SHARED_STEPS:
                    shared_gate_up(m + LAG)
                else:
                    expert_gate_up(0, m + LAG - SHARED_STEPS)
                g, n = m // SHARED_BLOCKS, m % SHARED_BLOCKS
                pe.wait_ge(shared_lo, m + 1)
                if n == 0 and g == 1:
                    pe.wait_ge(sigmoid_done, 1)
                if n == 0 and g >= 2:
                    pe.wait_ge(x_added, 2 * (g - 1))
                if m == SHARED_STEPS - SHARED_BLOCKS:
                    pe.wait_ge(step, STEPS)
                    for half in range(2):
                        last = nc.tensor.transpose(router_bank[:, half * P:(half + 1) * P],
                                                   weights[:, half * 8:half * 8 + 8, :], ident[:, :])
                    last.then_inc(w_transposed, 1)
                    pe.wait_ge(w_copied, 2)
                down(EXPERTS + n, shared_banks[g % 2], n == 0, n == SHARED_BLOCKS - 1)
            with pe.Fori(0, TOKEN_GROUPS - 1) as g:
                group(g, False)
            group(TOKEN_GROUPS - 1, True)

        @block.scalar
        def _(act_eng):
            def silu_of(F, n):
                act_eng.wait_ge(gu_done, F + 1)
                nc.scalar.activation(silu[:, n % 2, :], gate_banks[n % 2][:, :], ACT.Silu).then_inc(silu_done, 1)

            def high_part(n):
                nc.scalar.copy(act_hi[:, n % 2, :], act[:, n % 2, :]).then_inc(hi_done, 1)

            def expert_high_part(g, n):
                act_eng.wait_ge(act_ready, g * EXPERTS + n + 1 + W_SLOTS)
                act_eng.wait_ge(down_done, step_of(g, n) - 1)
                high_part(n)

            def shared_high_part(m):
                act_eng.wait_ge(prod_done, m + 1)
                if m >= 2:
                    act_eng.wait_ge(down_done, m - 1)
                high_part(m)

            def group(g, last_group):
                for n in range(LAG, EXPERTS):
                    silu_of(step_of(g, n), n)
                    expert_high_part(g, n - 1)
                if not last_group:
                    silu_of(step_of(g + 1, 0), 0)
                expert_high_part(g, EXPERTS - 1)
                if not last_group:
                    silu_of(step_of(g + 1, 1), 1)
                    expert_high_part(g + 1, 0)

            nc.scalar.activation(scores[:, :, :], banks[7][:, 0:T * E].rearrange("p (t e) -> p t e", e=E),
                                 ACT.Sigmoid).then_inc(sigmoid_done, 1)
            silu_of(0, 0)
            for m in range(SHARED_STEPS):
                silu_of(m + 1, m + 1)
                shared_high_part(m)
                for k in late_splits(m):
                    act_eng.wait_ge(staged[k % LATE_STAGES], 16 * (k // LATE_STAGES + 1))
                    nc.scalar.copy(w_hi[:, late[k], :], stage[:, k % LATE_STAGES, :]).then_inc(hi_split, 1)
                if m == SHARED_STEPS - SHARED_BLOCKS:
                    act_eng.wait_ge(w_transposed, 1)
                    for half in range(2):
                        nc.scalar.copy(w_t[:, half, :], router_bank[:, half * P:(half + 1) * P]).then_inc(w_copied, 1)
            silu_of(step_of(0, 1), 1)
            expert_high_part(0, 0)
            with act_eng.Fori(0, TOKEN_GROUPS - 1) as g:
                group(g, False)
            group(TOKEN_GROUPS - 1, True)

        @block.gpsimd
        def _(pool):
            nc.gpsimd.iota(order[:, :], pattern=[[-1, G]], base=G, channel_multiplier=0,
                           allow_small_or_imprecise_dtypes=True)
            nc.gpsimd.memset(choice[:, :, E:], 2 * BIG).then_inc(order_done, 1)
            for m in range(SHARED_STEPS):
                pool.wait_ge(hi_done, m + 1)
                if m >= 2:
                    pool.wait_ge(down_done, m - 1)
                nc.gpsimd.tensor_tensor(act_lo[:, m % 2, :], act[:, m % 2, :], act_hi[:, m % 2, :].bitcast(FP32),
                                        ALU.subtract).then_inc(shared_lo, 1)
                for k in late_splits(m):
                    pool.wait_ge(hi_split, k + 1)
                    n = late[k]
                    nc.gpsimd.tensor_tensor(w_lo[:, n, :], stage[:, k % LATE_STAGES, :], w_hi[:, n, :].bitcast(FP32),
                                            ALU.subtract).then_inc(lo_split, 1)
            pool.wait_ge(shared_lo, SHARED_STEPS)
            pool.sem_inc(lo_done, 2)
            with pool.Fori(0, TOKEN_GROUPS) as g:
                for e in range(EXPERTS):
                    pool.wait_ge(w_loaded[e % W_SLOTS], 16 * (g * (EXPERTS // W_SLOTS) + e // W_SLOTS + 1))
                    pool.wait_ge(prod_done, step_of(g, e) + 1)
                    pool.wait_ge(lo_done, g * EXPERTS + e + 1)
                    nc.gpsimd.tensor_tensor(act[:, e % 2, :], prod[:, e % 2, :], w_ring[:, e % W_SLOTS, :],
                                            ALU.mult).then_inc(act_ready, 1)
            pool.wait_ge(mv_done, EARLY_NORM)
            attention_rstd(nc, norm, slice(0, EARLY_NORM), rstd_step)

        @block.vector
        def _(dve):
            steps = [0]

            def dve_step(ins):
                steps[0] += 1
                ins.then_inc(step, 1)
                dve.wait_ge(step, steps[0])

            flat_top, flat_second, flat_score, flat_pen = (
                v[:, :, :].rearrange("p t g -> p (t g)") for v in (g_top, g_second, g_score, g_pen))
            wide_g, wide_e = [P, T, G], [P, T, E]

            def group_scores():
                dve.wait_ge(sigmoid_done, 1)
                dve.wait_ge(bias_loaded, 16)
                dve.wait_ge(order_done, 1)
                dve_step(nc.vector.tensor_tensor(choice[:, :, 0:E], scores[:, :, :],
                                                 bias_sb[:, :].unsqueeze(1).broadcast_to([P, T, E]), ALU.add))
                for half in range(2):
                    pairs = [choice[:, :, 0:E].rearrange("p t (g q r) -> p t g q r", g=G, r=2)[:, :, :, half, r]
                             for r in range(2)]
                    into = [v[:, :, half].rearrange("p (t g) -> p t g", g=G) for v in (pair_hi, pair_lo)]
                    nc.vector.tensor_tensor(into[0], pairs[0], pairs[1], ALU.max)
                    last = nc.vector.tensor_tensor(into[1], pairs[0], pairs[1], ALU.min)
                dve_step(last)
                nc.vector.tensor_tensor(flat_top, pair_hi[:, :, 0], pair_hi[:, :, 1], ALU.max)
                nc.vector.tensor_tensor(flat_second, pair_hi[:, :, 0], pair_hi[:, :, 1], ALU.min)
                dve_step(nc.vector.tensor_tensor(flat_pen, pair_lo[:, :, 0], pair_lo[:, :, 1], ALU.max))
                dve_step(nc.vector.tensor_tensor(flat_second, flat_second, flat_pen, ALU.max))
                dve_step(nc.vector.tensor_tensor(flat_score, flat_top, flat_second, ALU.add))

            def pick_group(n):
                hit = pick_first_max(dve_step, nc, g_score[:, :, :], wide_g,
                                     order[:, :].unsqueeze(1).broadcast_to(wide_g),
                                     (top[:, :], g_hit[:, :, :], top_hit[:, :]))
                if n == 0:
                    dve_step(nc.vector.tensor_copy(g_mask[:, :, :], hit))
                else:
                    dve_step(nc.vector.tensor_tensor(g_mask[:, :, :], g_mask[:, :, :], hit, ALU.add))

            def drop_groups():
                dve_step(nc.vector.tensor_scalar(g_pen[:, :, :], g_mask[:, :, :], BIG, -BIG, ALU.mult, ALU.add))
                for per_group, op in ((g_mask, ALU.mult), (g_pen, ALU.add)):
                    for g in range(G):
                        of_group = choice[:, :, g * PER:(g + 1) * PER]
                        last = nc.vector.tensor_tensor(
                            of_group, of_group, per_group[:, :, g:g + 1].broadcast_to([P, T, PER]), op)
                    dve_step(last)

            def best_experts():
                for t in range(T):
                    last = nc.vector.max(best[:, t, :], choice[:, t, :])
                dve_step(last)

            def take_out():
                for t in range(T):
                    last = nc.vector.match_replace(rest[:, t, :], best[:, t, :], choice[:, t, :], -3 * BIG)
                dve_step(last)

            def expert_weights():
                dve_step(nc.vector.scalar_tensor_tensor(weights[:, :, :], rest[:, :, 0:E], -2 * BIG, scores[:, :, :],
                                                        ALU.is_lt, ALU.mult))
                dve_step(nc.vector.reduce_sum(w_sum[:, :], weights[:, :, :], axis=AX.X))
                dve_step(nc.vector.tensor_scalar_add(w_sum[:, :], w_sum[:, :], 1e-20))
                dve_step(nc.vector.reciprocal(w_sum[:, :], w_sum[:, :]))
                dve_step(nc.vector.tensor_scalar_mul(w_sum[:, :], w_sum[:, :], ROUTED_SCALE))
                dve_step(nc.vector.tensor_tensor(weights[:, :, :], weights[:, :, :],
                                                 w_sum[:, :].unsqueeze(2).broadcast_to(wide_e), ALU.mult))

            def product(F, n, into):
                dve.wait_ge(silu_done, F + 1)
                nc.vector.tensor_tensor(into[:, n % 2, :], silu[:, n % 2, :], up_banks[n % 2][:, :],
                                        ALU.mult).then_inc(prod_done, 1)

            def shared_product(m):
                if m >= 2:
                    dve.wait_ge(shared_lo, m - 1)
                product(m, m, act)

            def expert_product(g, n):
                dve.wait_ge(act_ready, g * EXPERTS + n - 1 + W_SLOTS)
                product(step_of(g, n), n, prod)

            def low_part(g, n):
                dve.wait_ge(hi_done, step_of(g, n) + 1)
                nc.vector.tensor_tensor(act_lo[:, n % 2, :], act[:, n % 2, :], act_hi[:, n % 2, :].bitcast(FP32),
                                        ALU.subtract).then_inc(lo_done, 1)

            def add_to_x(g, from_banks, down_steps):
                dve.wait_ge(down_done, down_steps)
                for o in range(2):
                    rows = x_sb[:, bass.ds(g * 4 + 2 * o, 2), :]
                    nc.vector.tensor_tensor(rows, rows, from_banks[o][:, :].rearrange("p (t d) -> p t d", t=2),
                                            ALU.add).then_inc(x_added, 1)

            def add_experts_to_x(g):
                add_to_x(g, out_banks, step_of(g, EXPERTS))
                for k in range(4):
                    if k % 2 == 0:
                        dve.wait_ge(x_added, 2 * TOKEN_GROUPS + 2 * g + 1 + k // 2)
                    nc.vector.bn_stats(stats[:, bass.ds(g * 4 + k, 1), :].rearrange("p o s -> p (o s)"),
                                       x_sb[:, bass.ds(g * 4 + k, 1), :].rearrange("p o d -> p (o d)"))\
                      .then_inc(stats_done, 1)

            def group(g, last_group):
                for n in range(LAG, EXPERTS):
                    expert_product(g, n)
                    low_part(g, n - 1)
                if not last_group:
                    expert_product(g + 1, 0)
                low_part(g, EXPERTS - 1)
                if not last_group:
                    expert_product(g + 1, 1)
                    low_part(g + 1, 0)
                else:
                    for t in range(EARLY_NORM):
                        dve.wait_ge(stats_done, t + 1)
                        nc.vector.bn_aggr(meanvar[:, t, :], stats[:, t, :]).then_inc(mv_done, 1)
                add_experts_to_x(g)

            group_scores()
            shared_product(0)
            pick_group(0)
            shared_product(1)
            pick_group(1)
            drop_groups()
            shared_product(2)
            best_experts()
            take_out()
            shared_product(3)
            add_to_x(0, shared_banks[0], SHARED_BLOCKS)
            expert_weights()
            assert steps[0] == STEPS, steps
            for m in range(4, SHARED_STEPS + 1):
                if m < SHARED_STEPS:
                    shared_product(m)
                else:
                    expert_product(0, 0)
                if m % 2 == 1:
                    g = (m - 3) // 2
                    add_to_x(g, shared_banks[g % 2], SHARED_BLOCKS * (g + 1))
            expert_product(0, 1)
            add_to_x(TOKEN_GROUPS - 1, shared_banks[1], SHARED_STEPS)
            low_part(0, 0)
            with dve.Fori(0, TOKEN_GROUPS - 1) as g:
                group(g, False)
            group(TOKEN_GROUPS - 1, True)


def load_ctx(sp, a, ctx_ring, b, loaded):
    slot = b % CTX_SLOTS
    sp.dma_start(ctx_ring[:, slot, 0:DIM], a["ctx_keys"][b * SEQ:(b + 1) * SEQ, :]).then_inc(loaded, 16)
    sp.dma_start(ctx_ring[:, slot, DIM:].rearrange("p (m t) -> p m t", m=HALVES),
                 a["ctx_t"].rearrange("m p t -> p m t")[:, :, b * SEQ:(b + 1) * SEQ]).then_inc(loaded, 16)


X_BANKS, OUT_BANKS, A_BANKS = (0, 1), (2, 3), (6, 7, 4, 5)


def low_rank_in_product(nc, banks, w_hi, w_lo, x_hi, x_lo, g, j):
    w, half = j // 2, j % 2
    last = None
    for c in range(HALVES):
        cols = slice(w * 2 * DIM + c * DIM + half * P, w * 2 * DIM + c * DIM + (half + 1) * P)
        w_parts = w_hi[:, LORA_BLOCKS, cols], w_lo[:, LORA_BLOCKS, cols]
        x_parts = x_hi[:, c, bass.ds(g * GROUP_T, GROUP_T)], x_lo[:, c, bass.ds(g * GROUP_T, GROUP_T)]
        for k, (wp, xp) in enumerate(split_products(w_parts, x_parts)):
            last = nc.tensor.matmul(banks[A_BANKS[j]][:, :], wp, xp, start=(c == 0 and k == 0),
                                    stop=(c == HALVES - 1 and k == 2))
    return last


def base_products(nc, banks, w_hi, w_lo, x_hi, x_lo, g, n):
    for w in range(2):
        for c in range(HALVES):
            cols = slice(w * DIM + c * P, w * DIM + (c + 1) * P)
            w_parts = w_hi[:, n, cols], w_lo[:, n, cols]
            x_parts = x_hi[:, c, bass.ds(g * GROUP_T, GROUP_T)], x_lo[:, c, bass.ds(g * GROUP_T, GROUP_T)]
            for k, (wp, xp) in enumerate(split_products(w_parts, x_parts)):
                last = nc.tensor.matmul(banks[X_BANKS[w]][:, :], wp, xp, start=(c == 0 and k == 0), stop=False,
                                        skip_group_check=True)
    return last


def softmax_phase(nc, memory, a, x_dram, mask_dram, rw_dram, ident, x_sb, norm, w_hi, w_lo, x_hi, x_lo, picks_t,
                  first_picks_stored, picks_stored, ctx_ring, banks):
    stats, meanvar, rstd, minus_half = norm

    def sb(name, shape, dt=FP32):
        return memory.enter_context(nc.sbuf_tensor(name, shape, dt))

    STAGE_SLOTS, W_COLS, WEIGHT_SLOTS = 4, LORA_COLS // 2, 3
    LAST = BATCH + 7
    T, E = TILES, LORA_EXPERTS
    stage = sb("lora_stage", [P, STAGE_SLOTS, W_COLS])
    y, scaled = sb("att_y", [P, 2, DIM]), sb("att_scaled", [P, 2, DIM])
    weights = sb("att_weights", [P, WEIGHT_SLOTS, HALVES, DIM])
    minus_top, total, inverse = (sb(n, [P, BATCH, HALVES]) for n in ("att_minus_top", "att_total", "att_inverse"))
    gate_sb = sb("lora_gate", [P, HALVES, E])
    warm = sb("exp_warm", [P, 1])
    stats2, meanvar2, rstd2 = sb("stats2", [P, T, 6]), sb("meanvar2", [P, T, 2]), sb("rstd2", [P, T])
    z, x_t = sb("lora_y", [P, 2, DIM]), sb("lora_x_t", [P, 2, HALVES, P])
    probs, order, hit = sb("probs", [P, T, E]), sb("lora_order", [P, E]), sb("lora_hit", [P, T, E])
    masks, rw = sb("picked_masks", [P, T, PICKS, E]), sb("rw", [P, T, PICKS])
    top, top_hit, prob_sum = sb("picked_top", [P, PICKS, T]), sb("lora_top_hit", [P, T]), sb("lora_total", [P, T])
    masks_t, rw_t = picks_t
    score_banks, out_banks, turn_banks, router_bank, logit_bank = banks[0:2], banks[6:8], banks[4:6], banks[2], banks[3]
    with ExitStack() as s:
        def sem(name):
            return s.enter_context(nc.semaphore(name))

        ctx_loaded = [sem(f"ctx_loaded{i}") for i in range(CTX_SLOTS)]
        staged = [sem(f"lora_staged{i}") for i in range(STAGE_SLOTS)]
        hi_split, lo_split_pool, lo_split_dve = map(sem, ("lora_hi_split", "lora_lo_split_pool", "lora_lo_split_dve"))
        y_ready, scores_done, top_done, exp_done, inverse_done, scaled_done, out_done, x_added = map(sem, (
            "y_ready", "scores_done", "top_done", "exp_done", "inverse_done", "scaled_done", "out_done", "x_added"))
        stats_done, mv_done, eps_added, rstd_done, z_ready, turned, xt_copied, x_hi_done, x_lo_done, logits_done = map(
            sem, ("stats_done", "mv_done", "eps_added", "rstd_done", "z_ready", "turned", "xt_copied", "x_hi_done",
                  "x_lo_done", "logits_done"))
        gate_loaded, order_done, exp_ready, probs_exp, step, picks_turned, picks_copied = map(sem, (
            "gate_loaded", "order_done", "exp_ready", "probs_exp", "step", "picks_turned", "picks_copied"))
        x_stored, late_mv, late_rstd = map(sem, ("x_stored", "late_mv", "late_rstd"))
        block = s.enter_context(nc.Block())

        def wait_lo_split(engine, k):
            if k % STAGE_SLOTS == STAGE_SLOTS - 1:
                engine.wait_ge(lo_split_dve, k // STAGE_SLOTS + 1)
            else:
                engine.wait_ge(lo_split_pool, k // STAGE_SLOTS * (STAGE_SLOTS - 1) + k % STAGE_SLOTS + 1)

        def low_weights(engine, ops, k, done):
            engine.wait_ge(hi_split, k + 1)
            cols = slice((k % 2) * W_COLS, (k % 2 + 1) * W_COLS)
            ops.tensor_tensor(w_lo[:, k // 2, cols], stage[:, k % STAGE_SLOTS, :], w_hi[:, k // 2, cols].bitcast(FP32),
                              ALU.subtract).then_inc(done, 1)

        @block.sync
        def _(sp):
            def store_x(n):
                tiles = slice(4 * n, 4 * n + 4)
                sp.wait_ge(x_added, 4 * n + 4)
                sp.dma_start(x_dram[:, tiles, :], x_sb[:, tiles, :]).then_inc(x_stored, 16)

            sp.dma_start(gate_sb[:, :, :], a["lora_gate"]).then_inc(gate_loaded, 16)
            for b in range(BATCH):
                if b >= CTX_SLOTS:
                    sp.wait_ge(scaled_done, HALVES * (b - CTX_SLOTS + 1))
                    load_ctx(sp, a, ctx_ring, b, ctx_loaded[b % CTX_SLOTS])
                if b >= STAGE_SLOTS:
                    wait_lo_split(sp, b - STAGE_SLOTS)
                sp.dma_start(stage[:, b % STAGE_SLOTS, :], a["lora_weights"][b // 2, :, (b % 2) * W_COLS:
                                                                           (b % 2 + 1) * W_COLS])\
                  .then_inc(staged[b % STAGE_SLOTS], 16)
                if b in (9, 13):
                    store_x(b // 4 - 2)
            store_x(2)
            store_x(3)
            for half in range(2):
                sp.wait_ge(picks_copied, half + 1)
                sp.dma_start(mask_dram.rearrange("e (t k) -> t e k", k=P)[half * 8:half * 8 + 8], masks_t[:, half, :])\
                  .then_inc(first_picks_stored if half == 0 else picks_stored, 16)
            sp.wait_ge(picks_copied, 3)
            sp.dma_start(rw_dram.rearrange("e (t k) -> t e k", k=P), rw_t[:, :]).then_inc(picks_stored, 16)
            sp.wait_ge(x_stored, 64)

        @block.gpsimd
        def _(pool):
            nc.gpsimd.iota(order[:, :], pattern=[[-1, E]], base=E, channel_multiplier=0,
                           allow_small_or_imprecise_dtypes=True).then_inc(order_done, 1)
            pool.wait_ge(late_mv, TILES - EARLY_NORM)
            attention_rstd(nc, norm, slice(EARLY_NORM, TILES), late_rstd)
            for i in range(LAST):
                if 1 <= i <= BATCH:
                    b = i - 1
                    if b % STAGE_SLOTS < STAGE_SLOTS - 1:
                        low_weights(pool, nc.gpsimd, b, lo_split_pool)
                if i >= 7:
                    t = i - 7
                    pool.wait_ge(x_hi_done, t + 1)
                    cols = slice(P * t, P * (t + 1))
                    nc.gpsimd.tensor_tensor(x_lo[:, :, cols], x_t[:, t % 2, :, :], x_hi[:, :, cols].bitcast(FP32),
                                            ALU.subtract).then_inc(x_lo_done, 1)
                if 3 <= i < BATCH + 3:
                    b = i - 3
                    pool.wait_ge(mv_done, b + 1)
                    nc.gpsimd.tensor_scalar_add(rstd2[:, b:b + 1], meanvar2[:, b, 1:2], EPS).then_inc(eps_added, 1)
                    pool.wait_ge(eps_added, b + 1)
                    nc.gpsimd.tensor_tensor(rstd2[:, b:b + 1], rstd2[:, b:b + 1], minus_half[:, 0:1],
                                            ALU.pow).then_inc(rstd_done, 1)

        @block.scalar
        def _(act):
            nc.scalar.activation(warm[:, :], rstd[:, 0:1], ACT.Exp)
            for i in range(LAST):
                if 6 <= i < BATCH + 6:
                    t = i - 6
                    act.wait_ge(turned, t + 1)
                    if t >= 2:
                        act.wait_ge(x_lo_done, t - 1)
                        act.wait_ge(logits_done, t - 1)
                    nc.scalar.copy(x_t[:, t % 2, :, :], turn_banks[t % 2][:, 0:DIM].rearrange(
                        "p (c t) -> p c t", c=HALVES)).then_inc(xt_copied, 1)
                if i < BATCH:
                    b = i
                    act.wait_ge(top_done, b + 1)
                    if b >= WEIGHT_SLOTS:
                        act.wait_ge(out_done, b - WEIGHT_SLOTS + 1)
                    for m in range(HALVES):
                        nc.scalar.activation(weights[:, b % WEIGHT_SLOTS, m, :],
                                             score_banks[b % 2][:, m * DIM:(m + 1) * DIM], ACT.Exp,
                                             bias=minus_top[:, b, m:m + 1],
                                             accum_out=total[:, b, m:m + 1]).then_inc(exp_done, 1)
                if 6 <= i < BATCH + 6:
                    t = i - 6
                    act.wait_ge(xt_copied, t + 1)
                    nc.scalar.copy(x_hi[:, :, P * t:P * (t + 1)], x_t[:, t % 2, :, :]).then_inc(x_hi_done, 1)
                if i < BATCH:
                    act.wait_ge(staged[i % STAGE_SLOTS], 16 * (i // STAGE_SLOTS + 1))
                    nc.scalar.copy(w_hi[:, i // 2, (i % 2) * W_COLS:(i % 2 + 1) * W_COLS],
                                   stage[:, i % STAGE_SLOTS, :]).then_inc(hi_split, 1)
            act.wait_ge(exp_ready, 1)
            nc.scalar.activation(probs[:, :, :], probs[:, :, :], ACT.Exp).then_inc(probs_exp, 1)
            act.wait_ge(picks_turned, 1)
            for half in range(2):
                nc.scalar.copy(masks_t[:, half, :], router_bank[:, half * P:(half + 1) * P]).then_inc(picks_copied, 1)
            nc.scalar.copy(rw_t[:, :], router_bank[0:T * PICKS, 2 * P:3 * P]).then_inc(picks_copied, 1)

        @block.tensor
        def _(pe):
            for i in range(LAST):
                if i < BATCH:
                    b = i
                    if b >= CTX_SLOTS:
                        pe.wait_ge(ctx_loaded[b % CTX_SLOTS], 32 * (b // CTX_SLOTS))
                    pe.wait_ge(y_ready, b + 1)
                    if b >= 2:
                        pe.wait_ge(exp_done, HALVES * (b - 1))
                    for m in range(HALVES):
                        last = nc.tensor.matmul(score_banks[b % 2][:, m * DIM:(m + 1) * DIM],
                                                ctx_ring[:, b % CTX_SLOTS, m * P:(m + 1) * P], y[:, b % 2, :],
                                                start=True, stop=True)
                    last.then_inc(scores_done, 1)
                if 2 <= i < BATCH + 2:
                    b = i - 2
                    pe.wait_ge(scaled_done, HALVES * (b + 1))
                    pe.wait_ge(exp_done, HALVES * (b + 1))
                    if b >= 2:
                        pe.wait_ge(x_added, b - 1)
                    for m in range(HALVES):
                        last = nc.tensor.matmul(out_banks[b % 2][:, 0:DIM], scaled[:, b % 2, m * P:(m + 1) * P],
                                                weights[:, b % WEIGHT_SLOTS, m, :], start=(m == 0),
                                                stop=(m == HALVES - 1))
                    last.then_inc(out_done, 1)
                if 5 <= i < BATCH + 5:
                    t = i - 5
                    pe.wait_ge(z_ready, t + 1)
                    if t >= 2:
                        pe.wait_ge(xt_copied, t - 1)
                    for c in range(HALVES):
                        last = nc.tensor.transpose(turn_banks[t % 2][:, c * P:(c + 1) * P],
                                                   z[:, t % 2, c * P:(c + 1) * P], ident[:, :])
                    last.then_inc(turned, 1)
                if i >= 7:
                    t = i - 7
                    if t == 0:
                        pe.wait_ge(gate_loaded, 16)
                    pe.wait_ge(xt_copied, t + 1)
                    for c in range(HALVES):
                        last = nc.tensor.matmul(logit_bank[:, t * E:(t + 1) * E],
                                                x_t[:, t % 2, c, :], gate_sb[:, c, :],
                                                start=(c == 0), stop=(c == HALVES - 1))
                    last.then_inc(logits_done, 1)
            pe.wait_ge(x_added, BATCH)
            pe.wait_ge(xt_copied, T)
            pe.wait_ge(x_hi_done, GROUP_T // P)
            pe.wait_ge(x_lo_done, GROUP_T // P)
            for k in (BATCH - 1, BATCH - 2):
                wait_lo_split(pe, k)
            for j in range(4):
                low_rank_in_product(nc, banks, w_hi, w_lo, x_hi, x_lo, 0, j)
            pe.wait_ge(step, LORA_STEPS)
            for half in range(2):
                nc.tensor.transpose(router_bank[:, half * P:(half + 1) * P], masks[:, half * 8:half * 8 + 8, :, :],
                                    ident[:, :])
            nc.tensor.transpose(router_bank[0:T * PICKS, 2 * P:3 * P], rw[:, :, :], ident[:, :])\
              .then_inc(picks_turned, 1)

        @block.vector
        def _(dve):
            steps = [0]

            def dve_step(ins):
                steps[0] += 1
                ins.then_inc(step, 1)
                dve.wait_ge(step, steps[0])

            wide = [P, T, E]

            def router_shift():
                logits = logit_bank[:, 0:T * E].rearrange("p (t e) -> p t e", e=E)
                dve.wait_ge(logits_done, T)
                dve_step(nc.vector.reduce_max(prob_sum[:, :], logits, axis=AX.X))
                nc.vector.tensor_tensor(probs[:, :, :], logits, prob_sum[:, :].unsqueeze(2).broadcast_to(wide),
                                        ALU.subtract).then_inc(exp_ready, 1)

            def router_probs():
                dve.wait_ge(probs_exp, 1)
                dve_step(nc.vector.reduce_sum(prob_sum[:, :], probs[:, :, :], axis=AX.X))
                dve_step(nc.vector.reciprocal(prob_sum[:, :], prob_sum[:, :]))
                dve_step(nc.vector.tensor_tensor(probs[:, :, :], probs[:, :, :],
                                                 prob_sum[:, :].unsqueeze(2).broadcast_to(wide), ALU.mult))

            def router_pick(k):
                if k == 0:
                    dve.wait_ge(order_done, 1)
                pick_first_max(dve_step, nc, probs[:, :, :], wide, order[:, :].unsqueeze(1).broadcast_to(wide),
                               (top[:, k, :], hit[:, :, :], top_hit[:, :]))
                if k == 0:
                    dve_step(nc.vector.tensor_copy(masks[:, :, 0, :], hit[:, :, :]))
                else:
                    dve_step(nc.vector.tensor_tensor(masks[:, :, 1, :], hit[:, :, :], masks[:, :, 0, :],
                                                     ALU.subtract))

            def router_weights():
                dve_step(nc.vector.tensor_tensor(prob_sum[:, :], top[:, 0, :], top[:, 1, :], ALU.add))
                dve_step(nc.vector.reciprocal(prob_sum[:, :], prob_sum[:, :]))
                dve_step(nc.vector.tensor_tensor(rw[:, :, :].rearrange("p t k -> p k t"), top[:, :, :],
                                                 prob_sum[:, :].unsqueeze(1).broadcast_to([P, PICKS, T]), ALU.mult))

            def normalize(b):
                if b == EARLY_NORM:
                    dve.wait_ge(late_rstd, 3)
                if b >= 2:
                    dve.wait_ge(scores_done, b - 1)
                nc.vector.tensor_scalar(y[:, b % 2, :], x_sb[:, b, :], meanvar[:, b, 0:1], rstd[:, b:b + 1],
                                        ALU.subtract, ALU.mult).then_inc(y_ready, 1)

            normalize(0)
            for t in range(EARLY_NORM, TILES):
                nc.vector.bn_aggr(meanvar[:, t, :], stats[:, t, :]).then_inc(late_mv, 1)
            for i in range(LAST):
                if i < BATCH:
                    dve.wait_ge(scores_done, i + 1)
                    nc.vector.tensor_reduce(minus_top[:, i, :], score_banks[i % 2][:, :].rearrange(
                        "p (m d) -> p m d", m=HALVES), AX.X, ALU.max, negate=True).then_inc(top_done, 1)
                if 1 <= i <= BATCH:
                    dve.wait_ge(exp_done, HALVES * i)
                    nc.vector.reciprocal(inverse[:, i - 1, :], total[:, i - 1, :]).then_inc(inverse_done, 1)
                if i + 1 < BATCH:
                    normalize(i + 1)
                if 1 <= i <= BATCH:
                    b = i - 1
                    dve.wait_ge(inverse_done, b + 1)
                    if b >= 2:
                        dve.wait_ge(out_done, b - 1)
                    for m in range(HALVES):
                        nc.vector.tensor_scalar_mul(scaled[:, b % 2, m * P:(m + 1) * P],
                                                    ctx_ring[:, b % CTX_SLOTS, DIM + m * P:DIM + (m + 1) * P],
                                                    inverse[:, b, m:m + 1]).then_inc(scaled_done, 1)
                if 3 <= i < BATCH + 3:
                    b = i - 3
                    dve.wait_ge(out_done, b + 1)
                    nc.vector.tensor_tensor(x_sb[:, b, :], x_sb[:, b, :], out_banks[b % 2][:, 0:DIM],
                                            ALU.add).then_inc(x_added, 1)
                if 4 <= i < BATCH + 4:
                    t = i - 4
                    dve.wait_ge(rstd_done, t + 1)
                    if t >= 2:
                        dve.wait_ge(turned, t - 1)
                    nc.vector.tensor_scalar(z[:, t % 2, :], x_sb[:, t, :], meanvar2[:, t, 0:1], rstd2[:, t:t + 1],
                                            ALU.subtract, ALU.mult).then_inc(z_ready, 1)
                if 3 <= i < BATCH + 3:
                    b = i - 3
                    dve.wait_ge(x_added, b + 1)
                    nc.vector.bn_stats(stats2[:, b, :], x_sb[:, b, :]).then_inc(stats_done, 1)
                    dve.wait_ge(stats_done, b + 1)
                    nc.vector.bn_aggr(meanvar2[:, b, :], stats2[:, b, :]).then_inc(mv_done, 1)
                if 1 <= i <= BATCH and i % STAGE_SLOTS == 0:
                    low_weights(dve, nc.vector, i - 1, lo_split_dve)
            router_shift()
            router_probs()
            for k in range(PICKS):
                router_pick(k)
            router_weights()
            assert steps[0] == LORA_STEPS, steps


def lora_experts(nc, memory, out_rows, mask_dram, rw_dram, x_rows, x_hi, x_lo, w_hi, w_lo, masks, scratch,
                 first_picks_stored, picks_stored, banks):
    def sb(name, shape, dt=FP32):
        return memory.enter_context(nc.sbuf_tensor(name, shape, dt))

    am_hi, am_lo = (sb(n, [P, 2, 2, HALVES, GROUP_T], F32R) for n in ("am_hi", "am_lo"))
    rw = sb("rw_sb", [P, PICKS, GROUP_T])
    hid_hi, hid_lo = (sb(n, [P, 2, GROUP_T], F32R) for n in ("hid_hi", "hid_lo"))
    f = sb("hid", [P, 4, GROUP_T])
    x_g = sb("x_g", [P, GROUP_T // P, DIM])
    warm = sb("silu_warm", [P, 1])
    FB, TG = LORA_BLOCKS, GROUP_T // P
    SECOND, BOTH = range(2)
    UNITS = [(kind, j) for kind in range(2) for j in range(4)]
    POOL_UNITS = (1, 2, 5, 6)
    unit_slots = [scratch[:, k, :] for k in range(3)] + [f[:, 2, :], f[:, 3, :]]
    x_banks, out_banks, a_banks = ([banks[b] for b in group] for group in (X_BANKS, OUT_BANKS, A_BANKS))
    term_banks = {BOTH: a_banks[2:4], SECOND: a_banks[0:2]}
    with ExitStack() as s:
        def sem(name):
            return s.enter_context(nc.semaphore(name))

        masks_loaded, rw_loaded, x_loaded, stored = map(sem, ("masks_loaded", "rw_loaded", "x_loaded", "stored"))
        first_masks_loaded = [sem(f"first_masks_loaded{kind}") for kind in range(2)]
        a_done, am_mul, am_hi_done, am_lo_dve, am_lo_pool = map(sem, (
            "a_done", "am_mul", "am_hi_done", "am_lo_dve", "am_lo_pool"))
        first_done, second_done, silu_done, prod_done, weighted, both_done = map(sem, (
            "first_done", "second_done", "silu_done", "prod_done", "weighted", "both_done"))
        hi_done, lo_done, down_done = sem("hi_done"), sem("lo_done"), sem("down_done")
        terms_done = [sem("second_terms_done"), sem("both_terms_done")]
        t_mul, t_sum, t_hi, t_lo, b2_done, x_added = map(sem, ("t_mul", "t_sum", "t_hi", "t_lo", "b2_done", "x_added"))
        block = s.enter_context(nc.Block())

        def mask(g, kind, half):
            return masks[:, kind, half, bass.ds(g * GROUP_T, GROUP_T)]

        def low_inputs_split(engine, g, units):
            on_pool = sum(u in POOL_UNITS for u in range(units))
            engine.wait_ge(am_lo_dve, 4 * g + units - on_pool)
            if on_pool:
                engine.wait_ge(am_lo_pool, 4 * g + on_pool)

        @block.sync
        def _(sp):
            def load_rw(g):
                for k in range(PICKS):
                    sp.dma_start(rw[:, k, :], rw_dram[k, bass.ds(g * GROUP_T, GROUP_T)].partition_broadcast(P))\
                      .then_inc(rw_loaded, 16)

            def load_x(g):
                sp.dma_start(x_g[:, :, :], x_rows[:, bass.ds(g * TG, TG), :]).then_inc(x_loaded, 16)

            def store(g):
                for o in range(2):
                    sp.wait_ge(x_added, 2 * g + 3 + o)
                    sp.dma_start(out_rows[:, bass.ds(g * TG + 2 * o, 2), :], x_g[:, 2 * o:2 * o + 2, :])\
                      .then_inc(stored, 16)

            sp.wait_ge(first_picks_stored, 16)
            for first, end, loaded in ((0, GROUP_T, first_masks_loaded), (GROUP_T, TOKENS, [masks_loaded] * 2)):
                for kind in range(2):
                    for half in range(HALVES):
                        source = bass.AP(mask_dram.tensor, (kind * LORA_EXPERTS + half * 4) * TOKENS + first,
                                         [[TOKENS, 4], [0, RANK], [1, end - first]])
                        sp.dma_start(masks[:, kind, half, first:end], source).then_inc(loaded[kind], 16)
                if first == 0:
                    sp.wait_ge(picks_stored, 32)
                    load_rw(0)
                    load_x(0)
            with sp.Fori(0, TOKEN_GROUPS - 1) as g:
                sp.wait_ge(weighted, 2 * FB * (g + 1))
                load_rw(g + 1)
                store(g)
                sp.wait_ge(stored, 32 * (g + 1))
                load_x(g + 1)
            store(TOKEN_GROUPS - 1)
            sp.wait_ge(stored, 32 * TOKEN_GROUPS)

        def weight_cols(chunk, which, c):
            cols = slice(which * DIM + c * P, which * DIM + (c + 1) * P)
            return w_hi[:, chunk, cols], w_lo[:, chunk, cols]

        @block.tensor
        def _(pe):
            def low_rank_in(g, parts):
                for j in parts:
                    pe.wait_ge(t_mul, 4 * (g - 1) + j + 1)
                    low_rank_in_product(nc, banks, w_hi, w_lo, x_hi, x_lo, g, j).then_inc(a_done, 1)

            def base(g, n):
                pe.wait_ge(prod_done, 2 * (FB * g + n))
                base_products(nc, banks, w_hi, w_lo, x_hi, x_lo, g, n)

            def low_rank(g, n, kind):
                if n == 0:
                    low_inputs_split(pe, g, 4 * (kind + 1))
                if kind == 1:
                    pe.wait_ge(prod_done, 2 * (FB * g + n) + 1)
                for w in range(2):
                    for half in range(HALVES):
                        am = am_hi[:, kind, w, half, :], am_lo[:, kind, w, half, :]
                        for k, (wp, ap) in enumerate(split_products(weight_cols(n, 2 + w, half), am)):
                            last = nc.tensor.matmul(x_banks[w][:, :], wp, ap, start=False,
                                                    stop=(half == 1 and k == 2), skip_group_check=True)
                last.then_inc(second_done if kind else first_done, 1)

            def terms(g, n, which):
                pe.wait_ge(lo_done, 2 * (FB * g + n) + which + 3)
                for half in range(HALVES):
                    hid = hid_hi[:, which, :], hid_lo[:, which, :]
                    for j, (wp, hp) in enumerate(split_products(weight_cols(n, 5, half), hid)):
                        last = nc.tensor.matmul(term_banks[which][half][:, :], wp, hp, start=(n == 0 and j == 0),
                                                stop=(n == FB - 1 and j == 2))
                last.then_inc(terms_done[which], 1)

            def down(g, n, tiles):
                pe.wait_ge(lo_done, 2 * (FB * g + n) + BOTH + 3)
                if n == 0 and tiles[0] == 0:
                    pe.wait_ge(x_added, 2 * g + 2)
                for t in tiles:
                    rows = slice(t * P, (t + 1) * P)
                    w = w_hi[:, n, 4 * DIM:5 * DIM], w_lo[:, n, 4 * DIM:5 * DIM]
                    for k, (hp, wp) in enumerate(split_products((hid_hi[:, BOTH, rows], hid_lo[:, BOTH, rows]), w)):
                        last = nc.tensor.matmul(out_banks[t // 2][:, (t % 2) * DIM:(t % 2 + 1) * DIM], hp, wp,
                                                start=(n == 0 and k == 0 and t % 2 == 0), stop=False,
                                                skip_group_check=True)
                if tiles[-1] == TG - 1:
                    last.then_inc(down_done, 1)

            def low_rank_out(g, tiles):
                if tiles[0] == 0:
                    pe.wait_ge(t_lo, 2 * (g + 1))
                for t in tiles:
                    for half in range(HALVES):
                        rows = slice(t * P, (t + 1) * P)
                        cols = slice(4 * DIM + half * DIM, 4 * DIM + (half + 1) * DIM)
                        w = w_hi[:, FB, cols], w_lo[:, FB, cols]
                        parts = hid_hi[:, half, rows], hid_lo[:, half, rows]
                        for k, (hp, wp) in enumerate(split_products(parts, w)):
                            last = nc.tensor.matmul(out_banks[t // 2][:, (t % 2) * DIM:(t % 2 + 1) * DIM], hp, wp,
                                                    start=False, stop=(half == 1 and k == 2), skip_group_check=True)
                last.then_inc(b2_done, 1)

            def group(g, last_group):
                low_rank(g, 0, 1)
                for n in range(1, FB):
                    base(g, n)
                    low_rank(g, n, 0)
                    terms(g, n - 1, BOTH)
                    ahead = () if last_group and n == FB - 1 else (0, 1)
                    if ahead:
                        down(g, n - 1, ahead)
                    low_rank(g, n, 1)
                    terms(g, n - 1, SECOND)
                    down(g, n - 1, range(len(ahead), TG))
                if not last_group:
                    base(g + 1, 0)
                terms(g, FB - 1, SECOND)
                terms(g, FB - 1, BOTH)
                if not last_group:
                    low_rank_in(g + 1, (0, 1))
                down(g, FB - 1, (0, 1, 2, 3))
                if not last_group:
                    low_rank_in(g + 1, (2, 3))
                low_rank_out(g, (0, 1))
                if not last_group:
                    low_rank(g + 1, 0, 0)
                low_rank_out(g, (2, 3))

            pe.sem_inc(x_added, 2)
            base_products(nc, banks, w_hi, w_lo, x_hi, x_lo, 0, 0)
            low_rank(0, 0, 0)
            with pe.Fori(0, TOKEN_GROUPS - 1) as g:
                group(g, False)
            group(TOKEN_GROUPS - 1, True)

        @block.scalar
        def _(act):
            def low_inputs_high(g, units):
                for u in units:
                    kind, j = UNITS[u]
                    act.wait_ge(am_mul, 8 * g + u + 1)
                    nc.scalar.copy(am_hi[:, kind, j // 2, j % 2, :], unit_slots[u % 5]).then_inc(am_hi_done, 1)

            def silu_of_first(F):
                act.wait_ge(first_done, F + 1)
                act.wait_ge(lo_done, 2 * F + 2)
                nc.scalar.activation(f[:, 0, :], x_banks[0][:, :], ACT.Silu).then_inc(silu_done, 1)

            def group(g, last_group):
                for n in range(FB):
                    F = FB * g + n
                    if n > 0:
                        silu_of_first(F)
                    act.wait_ge(second_done, F + 1)
                    nc.scalar.activation(f[:, 1, :], x_banks[0][:, :], ACT.Silu).then_inc(silu_done, 1)
                    act.wait_ge(weighted, 2 * F + 2)
                    act.wait_ge(terms_done[SECOND], F + 1)
                    if n == 0:
                        act.wait_ge(b2_done, 2 * g + 1)
                    nc.scalar.copy(hid_hi[:, SECOND, :], f[:, 1, :]).then_inc(hi_done, 1)
                    act.wait_ge(both_done, F + 1)
                    act.wait_ge(down_done, F + 1)
                    nc.scalar.copy(hid_hi[:, BOTH, :], f[:, 0, :]).then_inc(hi_done, 1)
                if not last_group:
                    low_inputs_high(g + 1, (0, 1))
                for half in range(HALVES):
                    act.wait_ge(t_sum, 2 * g + half + 1)
                    if half == 0:
                        act.wait_ge(down_done, FB * (g + 1) + 1)
                    nc.scalar.copy(hid_hi[:, half, :], f[:, 2 + half, :]).then_inc(t_hi, 1)
                if not last_group:
                    low_inputs_high(g + 1, range(2, 8))
                    silu_of_first(FB * (g + 1))

            for which in range(2):
                act.sem_inc(terms_done[which], 1)
            act.sem_inc(down_done, 1)
            act.sem_inc(b2_done, 1)
            act.sem_inc(lo_done, 2)
            nc.scalar.activation(warm[:, :], x_hi[:, 0, 0:1].bitcast(FP32), ACT.Silu)
            low_inputs_high(0, range(8))
            silu_of_first(0)
            with act.Fori(0, TOKEN_GROUPS - 1) as g:
                group(g, False)
            group(TOKEN_GROUPS - 1, True)

        def low_input_low(engine, ops, g, u):
            kind, j = UNITS[u]
            engine.wait_ge(am_hi_done, 8 * g + u + 1)
            ops.tensor_tensor(am_lo[:, kind, j // 2, j % 2, :], unit_slots[u % 5],
                              am_hi[:, kind, j // 2, j % 2, :].bitcast(FP32), ALU.subtract)\
               .then_inc(am_lo_pool if u in POOL_UNITS else am_lo_dve, 1)

        def low_rank_sum(engine, ops, g, half):
            engine.wait_ge(t_mul, 4 * g + 2 + half + 1)
            ops.tensor_tensor(f[:, 2 + half, :], f[:, 2 + half, :], f[:, half, :], ALU.add).then_inc(t_sum, 1)

        @block.gpsimd
        def _(pool):
            def group(g, last_group):
                for n in range(FB):
                    F = FB * g + n
                    if n == 0:
                        pool.wait_ge(rw_loaded, 16 * PICKS * (g + 1))
                    for k in range(PICKS):
                        pool.wait_ge(prod_done, 2 * F + k + 1)
                        nc.gpsimd.tensor_tensor(f[:, k, :], f[:, k, :], rw[:, k, :], ALU.mult).then_inc(weighted, 1)
                    pool.wait_ge(weighted, 2 * F + 2)
                    nc.gpsimd.tensor_tensor(f[:, 0, :], f[:, 0, :], f[:, 1, :], ALU.add).then_inc(both_done, 1)
                if not last_group:
                    for half in range(HALVES):
                        low_rank_sum(pool, nc.gpsimd, g, half)
                    for u in POOL_UNITS:
                        low_input_low(pool, nc.gpsimd, g + 1, u)

            for u in POOL_UNITS:
                low_input_low(pool, nc.gpsimd, 0, u)
            with pool.Fori(0, TOKEN_GROUPS - 1) as g:
                group(g, False)
            group(TOKEN_GROUPS - 1, True)

        @block.vector
        def _(dve):
            def low_input_product(g, u, wait):
                kind, j = UNITS[u]
                if wait:
                    dve.wait_ge(a_done, 4 * (g - 1) + j + 1)
                if j == 0 and not wait:
                    dve.wait_ge(first_masks_loaded[kind], 16 * HALVES)
                if u >= 5:
                    low_inputs_split(dve, g, u - 4)
                elif u >= 3 and wait:
                    dve.wait_ge(t_lo, 2 * (g - 1) + u - 2)
                nc.vector.tensor_tensor(unit_slots[u % 5], a_banks[j][:, :], mask(g, kind, j % 2),
                                        ALU.mult).then_inc(am_mul, 1)

            def low_inputs(g, wait):
                low_input_product(g, 0, wait)
                if wait:
                    low_input_low(dve, nc.vector, g, 0)
                low_input_product(g, 1, wait)
                if wait:
                    terms_low(g - 1)
                low_input_product(g, 2, wait)
                low_input_product(g, 3, wait)
                if not wait:
                    low_input_low(dve, nc.vector, g, 0)
                low_input_low(dve, nc.vector, g, 3)
                low_input_product(g, 4, wait)
                low_input_product(g, 5, wait)
                low_input_low(dve, nc.vector, g, 4)
                low_input_product(g, 6, wait)
                low_input_product(g, 7, wait)
                low_input_low(dve, nc.vector, g, 7)

            def terms_low(g):
                for half in range(HALVES):
                    dve.wait_ge(t_hi, 2 * g + half + 1)
                    nc.vector.tensor_tensor(hid_lo[:, half, :], f[:, 2 + half, :],
                                            hid_hi[:, half, :].bitcast(FP32), ALU.subtract).then_inc(t_lo, 1)

            def add_to_x(g):
                dve.wait_ge(x_loaded, 16 * (g + 1))
                for o in range(2):
                    dve.wait_ge(b2_done, 2 * g + o + 2)
                    rows = x_g[:, 2 * o:2 * o + 2, :]
                    nc.vector.tensor_tensor(rows, rows, out_banks[o][:, :].rearrange("p (t d) -> p t d", t=2),
                                            ALU.add).then_inc(x_added, 1)

            def masked_terms(g, which, last_group):
                dve.wait_ge(terms_done[which], FB * (g + 1) + 1)
                if which == SECOND:
                    low_inputs_split(dve, g, 8)
                else:
                    dve.wait_ge(lo_done, 2 * FB * (g + 1) + 2)
                for half in range(HALVES):
                    nc.vector.tensor_tensor(f[:, (2 if which == SECOND else 0) + half, :],
                                            term_banks[which][half][:, :], mask(g, 1 - which, half),
                                            ALU.mult).then_inc(t_mul, 1)
                    if last_group and which == BOTH:
                        low_rank_sum(dve, nc.vector, g, half)

            def product(F, k):
                dve.wait_ge(silu_done, 2 * F + k + 1)
                nc.vector.tensor_tensor(f[:, k, :], f[:, k, :], x_banks[1][:, :], ALU.mult).then_inc(prod_done, 1)

            def group(g, last_group):
                for n in range(FB):
                    F = FB * g + n
                    if n > 0:
                        product(F, 0)
                    product(F, 1)
                    for which in (SECOND, BOTH):
                        dve.wait_ge(hi_done, 2 * F + which + 1)
                        nc.vector.tensor_tensor(hid_lo[:, which, :], f[:, 1 - which, :],
                                                hid_hi[:, which, :].bitcast(FP32), ALU.subtract).then_inc(lo_done, 1)
                masked_terms(g, SECOND, last_group)
                masked_terms(g, BOTH, last_group)
                if last_group:
                    terms_low(g)
                else:
                    low_inputs(g + 1, True)
                if not last_group:
                    product(FB * (g + 1), 0)
                add_to_x(g)

            low_inputs(0, False)
            product(0, 0)
            dve.wait_ge(masks_loaded, 16 * 2 * HALVES)
            with dve.Fori(0, TOKEN_GROUPS - 1) as g:
                group(g, False)
            group(TOKEN_GROUPS - 1, True)


def lora_weights(inputs):
    import numpy as np

    def rows_in_halves(w):
        w = np.asarray(w)
        return w.reshape(HALVES, P, -1).transpose(1, 0, 2).reshape(P, -1)

    def get(n):
        return np.asarray(inputs["L1_ffn_" + n])

    b1, b3 = (get(n).transpose(0, 2, 1).reshape(DIM, -1) for n in ("B1", "B3"))
    a2 = get("A2").reshape(DIM, -1).T
    chunks = []
    for n in range(LORA_BLOCKS):
        fs = slice(n * P, (n + 1) * P)
        chunks.append(np.concatenate([rows_in_halves(m) for m in (
            get("W1")[fs].T, get("W3")[fs].T, b1[:, fs], b3[:, fs])] + [get("W2").T[fs], a2[fs]], axis=1))
    chunks.append(np.concatenate([rows_in_halves(m) for m in (
        get("A1").reshape(DIM, DIM).T, get("A3").reshape(DIM, DIM).T,
        get("B2").transpose(0, 2, 1).reshape(DIM, DIM))], axis=1))
    return np.stack(chunks)


def moe_weights(inputs):
    import numpy as np

    def blocks(experts, shared):
        return np.concatenate([np.asarray(experts), np.asarray(shared)])

    gate = blocks(np.asarray(inputs["L0_ffn_gate_w"]).reshape(-1, DIM), inputs["L0_ffn_sh_gate_w"])
    up = blocks(np.asarray(inputs["L0_ffn_up_w"]).reshape(-1, DIM), inputs["L0_ffn_sh_up_w"])
    down = blocks(np.asarray(inputs["L0_ffn_down_w"]).transpose(0, 2, 1).reshape(-1, DIM),
                  np.asarray(inputs["L0_ffn_sh_down_w"]).T)
    in_rows = [w.reshape(FBLOCKS, P, HALVES, P).transpose(0, 3, 2, 1).reshape(FBLOCKS, P, DIM) for w in (gate, up)]
    return np.concatenate([*in_rows, down.reshape(FBLOCKS, P, DIM)], axis=2)


def kernel(**inputs):
    import numpy as np
    import concourse.bacc as bacc
    from concourse.bass_utils import run_bass_kernel_spmd

    nc = bacc.Bacc("TRN2", target_bir_lowering=False, num_devices=1)
    ctx = np.asarray(inputs["ctx_2048"])
    ctx_rev = ctx.reshape(TOKENS, HALVES, P)[:, :, ::-1]
    arrays = {
        "x": np.asarray(inputs["x"]).reshape(TOKENS, DIM),
        "ctx_t": ctx_rev.transpose(1, 2, 0),
        "ssm_kernel": inputs["L0_xattn_ssm_kernel"],
        "moe_gate": np.asarray(inputs["L0_ffn_gate_weight"]).T.reshape(HALVES, P, EXPERTS).transpose(1, 0, 2),
        "moe_bias": inputs["L0_ffn_e_score_correction_bias"],
        "moe_weights": moe_weights(inputs),
        "ctx_keys": ctx_rev.reshape(TOKENS, DIM),
        "lora_gate": np.asarray(inputs["L1_ffn_Wg"]).T.reshape(HALVES, P, LORA_EXPERTS).transpose(1, 0, 2),
        "lora_weights": lora_weights(inputs),
        "D": np.asarray(inputs["L0_xattn_D"]).reshape(HEADS, 1),
    }
    in_map, args = {}, {}
    for name, value in arrays.items():
        value = np.ascontiguousarray(value)
        in_map["in_" + name] = value
        args[name] = nc.dram_tensor("in_" + name, value.shape, mybir.dt.from_np(value.dtype), kind="ExternalInput").ap()
    out = nc.dram_tensor("out_x", (TOKENS, DIM), FP32, kind="ExternalOutput").ap()
    build(nc, args, out)
    r = run_bass_kernel_spmd(nc, [in_map], core_ids=[0])
    return r.results[0]["out_x"].reshape(BATCH, SEQ, DIM)
```
